# Optimizing a Trainium2 kernel written in Bass

```python
import numpy as np
import jax
import jax.numpy as jnp

def _softmax(x, axis=-1):
    return jax.nn.softmax(x, axis=axis)

def _gelu(x):
    return jax.nn.gelu(x, approximate=True)

def _silu(x):
    return jax.nn.silu(x)

def _sigmoid(x):
    return jax.nn.sigmoid(x)

def _layernorm(x, axis=-1, eps=1e-05):
    m = jnp.mean(x, axis=axis, keepdims=True)
    v = jnp.var(x, axis=axis, keepdims=True)
    return (x - m) / jnp.sqrt(v + eps)

def _scatter_add(tgt, idx, src, axis=0):
    return tgt.at[idx].add(src)

def _segment_sum(src, seg, n):
    return jax.ops.segment_sum(src, seg, n)
kernel_name = 'mk_seq_preln_d2_jaxref_r8_c04eb5'

def setup_inputs(seed: int=0):
    np.random.seed(seed)
    _w = jnp.asarray

    def _L0_attn_setup():
        import jax, jax.numpy as jnp
        import numpy as np
        B, S, H = (2, 512, 128)
        NKH, NVH, DK, DV = (8, 16, 64, 64)
        KEY_DIM = NKH * DK
        VAL_DIM = NVH * DV
        CONV_DIM = 2 * KEY_DIM + VAL_DIM
        KSZ = 4
        EPS = 1e-06

        def _forward(hidden_states, W_qkv, conv_w, W_z, W_b, W_a, dt_bias, A_log, norm_weight, W_out):
            b, s, _ = hidden_states.shape
            mixed = hidden_states @ W_qkv.T
            x = mixed.transpose(0, 2, 1)
            y = jax.lax.conv_general_dilated(x, conv_w, (1,), [(KSZ - 1, 0)], dimension_numbers=('NCH', 'OIH', 'NCH'), feature_group_count=CONV_DIM)
            mixed = jax.nn.silu(y).transpose(0, 2, 1)
            z = (hidden_states @ W_z.T).reshape(b, s, NVH, DV)
            beta = jax.nn.sigmoid(hidden_states @ W_b.T)
            a = hidden_states @ W_a.T
            g = -jnp.exp(A_log) * jax.nn.softplus(a + dt_bias)
            q, k, v = jnp.split(mixed, [KEY_DIM, 2 * KEY_DIM], axis=-1)
            q = q.reshape(b, s, NKH, DK)
            k = k.reshape(b, s, NKH, DK)
            v = v.reshape(b, s, NVH, DV)
            rep = NVH // NKH
            if rep > 1:
                q = jnp.repeat(q, rep, axis=2)
                k = jnp.repeat(k, rep, axis=2)
            q = q * DK ** (-0.5)

            def step(Sst, inp):
                q_t, k_t, v_t, g_t, b_t = inp
                Sst = Sst * jnp.exp(g_t)[..., None, None]
                kv = jnp.einsum('bhkv,bhk->bhv', Sst, k_t)
                delta = (v_t - kv) * b_t[..., None]
                Sst = Sst + k_t[..., None] * delta[..., None, :]
                o = jnp.einsum('bhkv,bhk->bhv', Sst, q_t)
                return (Sst, o)
            S0 = jnp.zeros((b, NVH, DK, DV), jnp.float32)
            xs = (q.transpose(1, 0, 2, 3), k.transpose(1, 0, 2, 3), v.transpose(1, 0, 2, 3), g.transpose(1, 0, 2), beta.transpose(1, 0, 2))
            _, o = jax.lax.scan(step, S0, xs)
            o = o.transpose(1, 0, 2, 3)
            h_ = o * jax.nn.silu(z)
            var = jnp.mean(h_ * h_, axis=-1, keepdims=True)
            h_ = h_ * jax.lax.rsqrt(var + EPS) * norm_weight
            return h_.reshape(b, s, VAL_DIM) @ W_out.T
        key = jax.random.key(seed)
        ks = jax.random.split(key, 8)
        s = 0.02
        return {'hidden_states': jax.random.normal(ks[0], (B, S, H), jnp.float32), 'W_qkv': jax.random.normal(ks[1], (CONV_DIM, H), jnp.float32) * s, 'conv_w': jax.random.normal(ks[2], (CONV_DIM, 1, KSZ), jnp.float32) * 0.1, 'W_z': jax.random.normal(ks[3], (VAL_DIM, H), jnp.float32) * s, 'W_b': jax.random.normal(ks[4], (NVH, H), jnp.float32) * s, 'W_a': jax.random.normal(ks[5], (NVH, H), jnp.float32) * s, 'dt_bias': jnp.ones((NVH,), jnp.float32), 'A_log': jnp.log(jax.random.uniform(ks[6], (NVH,), jnp.float32, 0.1, 16.0)), 'norm_weight': jnp.ones((DV,), jnp.float32), 'W_out': jax.random.normal(ks[7], (H, VAL_DIM), jnp.float32) * s}
    _L0_attn_in = _L0_attn_setup()

    def _L0_ffn_setup():
        import jax, jax.numpy as jnp
        import numpy as np
        S, B, D = (128, 2, 128)
        E, TOPK = (15, 3)
        F = 128
        FS = 256

        def _uinit(k, shape, out_dim):
            std = out_dim ** (-0.5)
            return jax.random.uniform(k, shape, jnp.float32, -std, std)
        key = jax.random.key(seed)
        ks = jax.random.split(key, 10)
        return {'x': jax.random.normal(ks[0], (S, B, D), jnp.float32), 'gate_w': jax.random.normal(ks[1], (E, D), jnp.float32) * D ** (-0.5), 'fc1_w': _uinit(ks[2], (E, 2 * F, D), 2 * F), 'fc1_b': _uinit(ks[3], (E, 2 * F), 2 * F), 'geglu_mult': jnp.ones((E, F), jnp.float32), 'fc2_w': _uinit(ks[4], (E, D, F), D), 'fc2_b': _uinit(ks[5], (E, D), D), 's_fc1_w': _uinit(ks[6], (2 * FS, D), 2 * FS), 's_fc1_b': _uinit(ks[7], (2 * FS,), 2 * FS), 's_geglu_mult': jnp.ones((FS,), jnp.float32), 's_fc2_w': _uinit(ks[8], (D, FS), D), 's_fc2_b': _uinit(ks[9], (D,), D)}
    _L0_ffn_in = _L0_ffn_setup()

    def _L1_attn_setup():
        import jax, jax.numpy as jnp
        import numpy as np
        HEADS = 16
        HIDDEN = 128
        key = jax.random.key(seed)
        ks = jax.random.split(key, 9)
        E, H = (128, HIDDEN)
        N, L = (4, 256)
        s = 0.02
        return {'X_embed': jax.random.normal(ks[0], (N, L, E), dtype=jnp.float32), 'Wq': jax.random.normal(ks[1], (E, H), dtype=jnp.float32) * s, 'bq': jax.random.normal(ks[2], (H,), dtype=jnp.float32) * s, 'Wk': jax.random.normal(ks[3], (E, H), dtype=jnp.float32) * s, 'bk': jax.random.normal(ks[4], (H,), dtype=jnp.float32) * s, 'Wv': jax.random.normal(ks[5], (E, H), dtype=jnp.float32) * s, 'bv': jax.random.normal(ks[6], (H,), dtype=jnp.float32) * s, 'Wo': jax.random.normal(ks[7], (H, H), dtype=jnp.float32) * s, 'bo': jax.random.normal(ks[8], (H,), dtype=jnp.float32) * s}
    _L1_attn_in = _L1_attn_setup()

    def _L1_ffn_setup():
        import jax, jax.numpy as jnp
        import numpy as np
        B, T, D, E, H = (4, 256, 128, 4, 8)
        EPS = 1e-05

        def _uniform(k, shape, bound):
            return jax.random.uniform(k, shape, jnp.float32, -bound, bound)

        def _layernorm(x, w, b):
            mu = jnp.mean(x, axis=-1, keepdims=True)
            var = jnp.mean(jnp.square(x - mu), axis=-1, keepdims=True)
            return (x - mu) * jax.lax.rsqrt(var + EPS) * w + b
        key = jax.random.key(seed)
        ks = jax.random.split(key, 12)
        wb = np.sqrt(6.0 / D) / np.sqrt(6.0)
        wb = 1.0 / np.sqrt(D)
        return {'x': jax.random.normal(ks[0], (B, T, D), jnp.float32), 'router_prob': jax.random.uniform(ks[1], (B, T, E), jnp.float32), 'norm_w': jnp.ones((D,), jnp.float32), 'norm_b': jnp.zeros((D,), jnp.float32), 'q_w': _uniform(ks[2], (D, D), wb), 'q_b': _uniform(ks[3], (D,), wb), 'k_w': _uniform(ks[4], (D, D), wb), 'k_b': _uniform(ks[5], (D,), wb), 'v_w': _uniform(ks[6], (D, D), wb), 'v_b': _uniform(ks[7], (D,), wb), 'o_w': _uniform(ks[8], (D, D), wb), 'o_b': _uniform(ks[9], (D,), wb)}
    _L1_ffn_in = _L1_ffn_setup()
    _d = {'L0_attn_hidden_states': _L0_attn_in['hidden_states'], 'L0_attn_W_qkv': _L0_attn_in['W_qkv'], 'L0_attn_conv_w': _L0_attn_in['conv_w'], 'L0_attn_W_z': _L0_attn_in['W_z'], 'L0_attn_W_b': _L0_attn_in['W_b'], 'L0_attn_W_a': _L0_attn_in['W_a'], 'L0_attn_dt_bias': _L0_attn_in['dt_bias'], 'L0_attn_A_log': _L0_attn_in['A_log'], 'L0_attn_norm_weight': _L0_attn_in['norm_weight'], 'L0_attn_W_out': _L0_attn_in['W_out'], 'L0_ffn_gate_w': _L0_ffn_in['gate_w'], 'L0_ffn_fc1_w': _L0_ffn_in['fc1_w'], 'L0_ffn_fc1_b': _L0_ffn_in['fc1_b'], 'L0_ffn_geglu_mult': _L0_ffn_in['geglu_mult'], 'L0_ffn_fc2_w': _L0_ffn_in['fc2_w'], 'L0_ffn_fc2_b': _L0_ffn_in['fc2_b'], 'L0_ffn_s_fc1_w': _L0_ffn_in['s_fc1_w'], 'L0_ffn_s_fc1_b': _L0_ffn_in['s_fc1_b'], 'L0_ffn_s_geglu_mult': _L0_ffn_in['s_geglu_mult'], 'L0_ffn_s_fc2_w': _L0_ffn_in['s_fc2_w'], 'L0_ffn_s_fc2_b': _L0_ffn_in['s_fc2_b'], 'L1_attn_Wq': _L1_attn_in['Wq'], 'L1_attn_bq': _L1_attn_in['bq'], 'L1_attn_Wk': _L1_attn_in['Wk'], 'L1_attn_bk': _L1_attn_in['bk'], 'L1_attn_Wv': _L1_attn_in['Wv'], 'L1_attn_bv': _L1_attn_in['bv'], 'L1_attn_Wo': _L1_attn_in['Wo'], 'L1_attn_bo': _L1_attn_in['bo'], 'L1_ffn_router_prob': _L1_ffn_in['router_prob'], 'L1_ffn_norm_w': _L1_ffn_in['norm_w'], 'L1_ffn_norm_b': _L1_ffn_in['norm_b'], 'L1_ffn_q_w': _L1_ffn_in['q_w'], 'L1_ffn_q_b': _L1_ffn_in['q_b'], 'L1_ffn_k_w': _L1_ffn_in['k_w'], 'L1_ffn_k_b': _L1_ffn_in['k_b'], 'L1_ffn_v_w': _L1_ffn_in['v_w'], 'L1_ffn_v_b': _L1_ffn_in['v_b'], 'L1_ffn_o_w': _L1_ffn_in['o_w'], 'L1_ffn_o_b': _L1_ffn_in['o_b']}
    _x0 = _d['L0_attn_hidden_states']
    _d['L0_attn_hidden_states'] = jax.random.normal(jax.random.fold_in(jax.random.key(seed), 1), (8, 512, 128), dtype=_x0.dtype)
    del _x0
    return _d

def reference(L0_attn_hidden_states, L0_attn_W_qkv, L0_attn_conv_w, L0_attn_W_z, L0_attn_W_b, L0_attn_W_a, L0_attn_dt_bias, L0_attn_A_log, L0_attn_norm_weight, L0_attn_W_out, L0_ffn_gate_w, L0_ffn_fc1_w, L0_ffn_fc1_b, L0_ffn_geglu_mult, L0_ffn_fc2_w, L0_ffn_fc2_b, L0_ffn_s_fc1_w, L0_ffn_s_fc1_b, L0_ffn_s_geglu_mult, L0_ffn_s_fc2_w, L0_ffn_s_fc2_b, L1_attn_Wq, L1_attn_bq, L1_attn_Wk, L1_attn_bk, L1_attn_Wv, L1_attn_bv, L1_attn_Wo, L1_attn_bo, L1_ffn_router_prob, L1_ffn_norm_w, L1_ffn_norm_b, L1_ffn_q_w, L1_ffn_q_b, L1_ffn_k_w, L1_ffn_k_b, L1_ffn_v_w, L1_ffn_v_b, L1_ffn_o_w, L1_ffn_o_b):

    def _L0_attn_ref(hidden_states, W_qkv, conv_w, W_z, W_b, W_a, dt_bias, A_log, norm_weight, W_out):
        import jax, jax.numpy as jnp
        import numpy as np
        B, S, H = (2, 512, 128)
        NKH, NVH, DK, DV = (8, 16, 64, 64)
        KEY_DIM = NKH * DK
        VAL_DIM = NVH * DV
        CONV_DIM = 2 * KEY_DIM + VAL_DIM
        KSZ = 4
        EPS = 1e-06

        def _forward(hidden_states, W_qkv, conv_w, W_z, W_b, W_a, dt_bias, A_log, norm_weight, W_out):
            b, s, _ = hidden_states.shape
            mixed = hidden_states @ W_qkv.T
            x = mixed.transpose(0, 2, 1)
            y = jax.lax.conv_general_dilated(x, conv_w, (1,), [(KSZ - 1, 0)], dimension_numbers=('NCH', 'OIH', 'NCH'), feature_group_count=CONV_DIM)
            mixed = jax.nn.silu(y).transpose(0, 2, 1)
            z = (hidden_states @ W_z.T).reshape(b, s, NVH, DV)
            beta = jax.nn.sigmoid(hidden_states @ W_b.T)
            a = hidden_states @ W_a.T
            g = -jnp.exp(A_log) * jax.nn.softplus(a + dt_bias)
            q, k, v = jnp.split(mixed, [KEY_DIM, 2 * KEY_DIM], axis=-1)
            q = q.reshape(b, s, NKH, DK)
            k = k.reshape(b, s, NKH, DK)
            v = v.reshape(b, s, NVH, DV)
            rep = NVH // NKH
            if rep > 1:
                q = jnp.repeat(q, rep, axis=2)
                k = jnp.repeat(k, rep, axis=2)
            q = q * DK ** (-0.5)

            def step(Sst, inp):
                q_t, k_t, v_t, g_t, b_t = inp
                Sst = Sst * jnp.exp(g_t)[..., None, None]
                kv = jnp.einsum('bhkv,bhk->bhv', Sst, k_t)
                delta = (v_t - kv) * b_t[..., None]
                Sst = Sst + k_t[..., None] * delta[..., None, :]
                o = jnp.einsum('bhkv,bhk->bhv', Sst, q_t)
                return (Sst, o)
            S0 = jnp.zeros((b, NVH, DK, DV), jnp.float32)
            xs = (q.transpose(1, 0, 2, 3), k.transpose(1, 0, 2, 3), v.transpose(1, 0, 2, 3), g.transpose(1, 0, 2), beta.transpose(1, 0, 2))
            _, o = jax.lax.scan(step, S0, xs)
            o = o.transpose(1, 0, 2, 3)
            h_ = o * jax.nn.silu(z)
            var = jnp.mean(h_ * h_, axis=-1, keepdims=True)
            h_ = h_ * jax.lax.rsqrt(var + EPS) * norm_weight
            return h_.reshape(b, s, VAL_DIM) @ W_out.T
        return _forward(hidden_states, W_qkv, conv_w, W_z, W_b, W_a, dt_bias, A_log, norm_weight, W_out)

    def _L0_ffn_ref(x, gate_w, fc1_w, fc1_b, geglu_mult, fc2_w, fc2_b, s_fc1_w, s_fc1_b, s_geglu_mult, s_fc2_w, s_fc2_b):
        import jax, jax.numpy as jnp
        import numpy as np
        S, B, D = (128, 2, 128)
        E, TOPK = (15, 3)
        F = 128
        FS = 256

        def _uinit(k, shape, out_dim):
            std = out_dim ** (-0.5)
            return jax.random.uniform(k, shape, jnp.float32, -std, std)
        s, b, d = x.shape
        xt = x.reshape(-1, d)
        T = xt.shape[0]
        logits = xt @ gate_w.T
        scores = jax.nn.softmax(logits, axis=-1)
        topk_w, topk_idx = jax.lax.top_k(scores, TOPK)
        topk_w = topk_w / (jnp.sum(topk_w, axis=-1, keepdims=True) + 1e-20)
        comb = jnp.zeros((T, E), xt.dtype).at[jnp.arange(T)[:, None], topk_idx].add(topk_w)
        h = jnp.einsum('td,efd->etf', xt, fc1_w) + fc1_b[:, None, :]
        xh, g = (h[..., :F], h[..., F:])
        a = jax.nn.gelu(g, approximate=False) * xh * geglu_mult[:, None, :]
        yexp = jnp.einsum('etf,edf->etd', a, fc2_w) + fc2_b[:, None, :]
        y = jnp.einsum('etd,te->td', yexp, comb)
        hs = xt @ s_fc1_w.T + s_fc1_b
        xs, gs = (hs[..., :FS], hs[..., FS:])
        as_ = jax.nn.gelu(gs, approximate=False) * xs * s_geglu_mult
        ys = as_ @ s_fc2_w.T + s_fc2_b
        return (y + ys).reshape(s, b, d)

    def _L1_attn_ref(X_embed, Wq, bq, Wk, bk, Wv, bv, Wo, bo):
        import jax, jax.numpy as jnp
        import numpy as np
        HEADS = 16
        HIDDEN = 128
        N, L, _ = X_embed.shape
        H, heads = (HIDDEN, HEADS)
        dh = H // heads
        Q = X_embed @ Wq + bq
        K = X_embed @ Wk + bk
        V = X_embed @ Wv + bv
        Q = Q.reshape(N, heads, L, dh)
        K = K.reshape(N, heads, L, dh)
        V = V.reshape(N, heads, L, dh)
        scale = np.float32(1.0 / np.sqrt(H))
        Q = Q * scale
        K = K * scale
        scores = jnp.einsum('neax,nebx->neab', Q, K)
        A = jax.nn.softmax(scores, axis=2)
        Out = jnp.einsum('neab,neax->neax', A, V)
        Out = Out.reshape(N, L, H)
        return Out @ Wo + bo

    def _L1_ffn_ref(x, router_prob, norm_w, norm_b, q_w, q_b, k_w, k_b, v_w, v_b, o_w, o_b):
        import jax, jax.numpy as jnp
        import numpy as np
        B, T, D, E, H = (4, 256, 128, 4, 8)
        EPS = 1e-05

        def _uniform(k, shape, bound):
            return jax.random.uniform(k, shape, jnp.float32, -bound, bound)

        def _layernorm(x, w, b):
            mu = jnp.mean(x, axis=-1, keepdims=True)
            var = jnp.mean(jnp.square(x - mu), axis=-1, keepdims=True)
            return (x - mu) * jax.lax.rsqrt(var + EPS) * w + b
        e_cnt = router_prob.shape[2]
        b, t, d = x.shape
        n = t // e_cnt
        h = H
        scale = d ** (-0.5)
        qs, ks_, vs = ([], [], [])
        for e in range(e_cnt):
            xe = x[:, e * n:(e + 1) * n, :]
            xn = _layernorm(xe, norm_w, norm_b)
            m = d // 2 ** e
            xm = xn[..., :m]
            qs.append(jnp.einsum('bnm,dm->bnd', xm, q_w[:, :m]) + q_b)
            ks_.append(jnp.einsum('bnm,dm->bnd', xm, k_w[:, :m]) + k_b)
            vs.append(jnp.einsum('bnm,dm->bnd', xm, v_w[:, :m]) + v_b)
        q = jnp.concatenate(qs, axis=1)
        k = jnp.concatenate(ks_, axis=1)
        v = jnp.concatenate(vs, axis=1)
        dh = d // h
        q = q.reshape(b, t, h, dh).transpose(0, 2, 1, 3)
        k = k.reshape(b, t, h, dh).transpose(0, 2, 1, 3)
        v = v.reshape(b, t, h, dh).transpose(0, 2, 1, 3)
        attn = jnp.einsum('bhqd,bhkd->bhqk', q, k) * scale
        attn = jax.nn.softmax(attn, axis=-1)
        attn_out = jnp.einsum('bhqk,bhkd->bhqd', attn, v)
        attn_out = attn_out.transpose(0, 2, 1, 3).reshape(b, t, d)
        outs = []
        for e in range(e_cnt):
            sl = slice(e * n, (e + 1) * n)
            m = d // 2 ** e
            xm = attn_out[:, sl, :m]
            out = jnp.einsum('bnm,om->bno', xm, o_w[:m, :m]) + o_b[:m]
            pad = d - m
            if pad:
                out = jnp.pad(out, ((0, 0), (0, 0), (0, pad)))
            outs.append(out + x[:, sl, :])
        return jnp.concatenate(outs, axis=1)
    x = L0_attn_hidden_states
    x = x + _L0_attn_ref(_layernorm(x, axis=-1), L0_attn_W_qkv, L0_attn_conv_w, L0_attn_W_z, L0_attn_W_b, L0_attn_W_a, L0_attn_dt_bias, L0_attn_A_log, L0_attn_norm_weight, L0_attn_W_out)
    x = x + _L0_ffn_ref(_layernorm(x, axis=-1), L0_ffn_gate_w, L0_ffn_fc1_w, L0_ffn_fc1_b, L0_ffn_geglu_mult, L0_ffn_fc2_w, L0_ffn_fc2_b, L0_ffn_s_fc1_w, L0_ffn_s_fc1_b, L0_ffn_s_geglu_mult, L0_ffn_s_fc2_w, L0_ffn_s_fc2_b)
    x = x + _L1_attn_ref(_layernorm(x, axis=-1), L1_attn_Wq, L1_attn_bq, L1_attn_Wk, L1_attn_bk, L1_attn_Wv, L1_attn_bv, L1_attn_Wo, L1_attn_bo)
    x = x + _L1_ffn_ref(_layernorm(x, axis=-1), L1_ffn_router_prob, L1_ffn_norm_w, L1_ffn_norm_b, L1_ffn_q_w, L1_ffn_q_b, L1_ffn_k_w, L1_ffn_k_b, L1_ffn_v_w, L1_ffn_v_b, L1_ffn_o_w, L1_ffn_o_b)
    return x

_drawn_inputs = setup_inputs


def setup_inputs(seed=0):
    import zlib

    import numpy as np

    out = dict(_drawn_inputs(seed))
    spreads = {'L0_attn_dt_bias': (1.0, 0.6),
     'L0_attn_norm_weight': (1.0, 0.6),
     'L0_ffn_geglu_mult': (1.0, 0.6),
     'L0_ffn_s_geglu_mult': (1.0, 0.6),
     'L1_ffn_norm_w': (1.0, 0.6),
     'L1_ffn_norm_b': (0.0, 0.8)}
    factors = {'L0_attn_W_qkv': 8.0,
     'L0_attn_conv_w': 8.0,
     'L0_attn_W_z': 8.0,
     'L0_attn_W_b': 45.584,
     'L0_attn_W_a': 8.0,
     'L0_attn_A_log': 53.452,
     'L0_attn_W_out': 8.0,
     'L0_ffn_fc1_b': 8.0,
     'L0_ffn_s_fc1_b': 8.0,
     'L1_attn_Wq': 64.0,
     'L1_attn_bq': 64.0,
     'L1_attn_Wk': 64.0,
     'L1_attn_bk': 200.0,
     'L1_attn_bv': 31.994,
     'L1_attn_bo': 2.705,
     'L1_ffn_q_w': 8.0,
     'L1_ffn_q_b': 8.0,
     'L1_ffn_k_w': 8.0,
     'L1_ffn_k_b': 200.0,
     'L1_ffn_v_w': 8.0,
     'L1_ffn_v_b': 6.852,
     'L1_ffn_o_w': 5.818,
     'L1_ffn_o_b': 23.53,
     'L0_ffn_fc2_b': 3.819,
     'L0_ffn_s_fc2_b': 2.911}
    for name, (base, spread) in spreads.items():
        noise = np.random.default_rng([zlib.crc32(name.encode()), seed]).standard_normal(out[name].shape)
        drawn = base * np.exp(spread * noise) if base else spread * noise
        out[name] = jnp.asarray(drawn.astype(out[name].dtype))
    for name, factor in factors.items():
        out[name] = (out[name] * factor).astype(out[name].dtype)
    return out
```

```python
from contextlib import ExitStack

import numpy as np

import concourse.bass as bass
from concourse import mybir

F32 = mybir.dt.float32
BF16 = mybir.dt.bfloat16
ALU = mybir.AluOpType
ACT = mybir.ActivationFunctionType
AX = mybir.AxisListType.X

B, S, D = 8, 512, 128
C = 64
NC = S // C
NT = 16
KSZ = 4
E, TOPK = 15, 3
NE = E + 2
H1 = 16
H2 = 8
NX = 4
LN_EPS, RMS_EPS = 1e-5, 1e-6
SETUP = 15
Q_PARTS, K_PARTS = (0, 0, 1, 0, 1, 2), (0, 1, 0, 2, 1, 0)
LEVELS = [2, 4, 8, 16, 32]


def columns():
    widths = dict(
        wqkv=NT * 128, convw=NT * KSZ, wz=1024, wab=48, dtb=1, alog=1, normw=1, wout=8 * 128,
        gate=E, fc1=E * 256, fc1b=E * 2, gm=E, fc2=E * 128, fc2b=128, sfc1=512, sfc1b=4, sgm=2,
        sfc2=256, sfc2b=1, wq=128, wk=128, wv=128, wo=128, bq=1, bk=1, bv=1, bo=1,
        nw=1, nb=1, qw=128, kw=128, vw=128, ow=128, qb=1, kb=1, vb=128, ob=1,
        ident=128, mean=128, masks=128 * len(LEVELS), mask1=128, identc=64, half=2, sel=32, onehot=256,
        lneps=1, rmseps=1, pads=5)
    at, n = {}, 0
    for name, w in widths.items():
        at[name] = (n, w)
        n += w
    return at, n


def build(nc, x_in, pack, out):
    at, npack = columns()
    with ExitStack() as ctx:
        def sb(name, shape, dt=F32):
            return ctx.enter_context(nc.sbuf_tensor(name, shape, dt))

        class Signal:

            def __init__(self, name, per, credit=0):
                self.sem, self.per, self.credit = ctx.enter_context(nc.semaphore(name)), per, credit

            def at(self, i, k):
                return i * self.per + (k + self.credit)

        W = sb("W", [128, npack])

        def w(name, lo=0, hi=None, p0=0, p1=128):
            o, n = at[name]
            return W[p0:p1, o + lo:o + (n if hi is None else hi)]

        x = sb("x", [128, S])
        xn = sb("xn", [128, S])
        xc = sb("xc", [128, S])
        sq = sb("sq", [128, S])
        sd = sb("sd", [128, S])
        u = sb("u", [128, S])
        expA = sb("expA", [128, 1])
        owm = sb("owm", [128, NX, 128])
        obm = sb("obm", [128, NX])
        gl = sb("gl", [16, NC])
        glB = sb("glB", [128, 8, NC])
        tc = sb("tc", [128, NC, 2, 8])
        var = sb("var", [128, NC, 8])
        rstd = sb("rstd", [128, NC, 8])
        mq = sb("mq", [128, 32])
        mrow = sb("mrow", [32, 128], BF16)

        A = sb("arenaA", [128, 16384])
        KT = A[:, 0:2048].rearrange("a (p t) -> a p t", p=4)
        QT = A[:, 2048:4096].rearrange("a (p t) -> a p t", p=4)
        VT = A[:, 4096:8192].rearrange("a (k t) -> a k t", k=8)
        egB = A[:, 8192:12288].rearrange("a (q t) -> a q t", q=8)
        Hall = A[:, 12288:16384].rearrange("a (c n) -> a c n", c=NC)
        oT = A[:, 0:4096].rearrange("a (k t) -> a k t", k=8)
        combB = A[:, 0:E * S].rearrange("a (j t) -> a j t", j=E)
        QX = A[:, 0:4096].bitcast(BF16).rearrange("a (g t) -> a g t", g=16)
        KX = A[:, 4096:8192].bitcast(BF16).rearrange("a (g t) -> a g t", g=16)
        Rb = A[:, 8192:8704]
        QH = A[:, 0:2048].bitcast(BF16).rearrange("a (h t) -> a h t", h=8)
        KH = A[:, 2048:4096].bitcast(BF16).rearrange("a (h t) -> a h t", h=8)
        Vflat = A[:, 4096:8192]

        def vslots(base):
            return A[:, 4096 + base:4096 + base + 576].rearrange("a (h z) -> a h z", z=144)[:, :, 0:16]

        Vp = A[:, 4096:8192].rearrange("a (k h c) -> a k h c", k=4, h=8)

        Bn = sb("arenaB", [128, 27 * 512])
        slot = [0]

        def take(n):
            slot[0] += n
            return Bn[:, 512 * (slot[0] - n):512 * slot[0]]

        Kbd = take(1).rearrange("a (p t) -> a p t", p=4)
        Qbd = take(1).rearrange("a (p t) -> a p t", p=4)
        KQc = take(1).rearrange("a (p q t) -> a p q t", p=4, q=2)
        Ktok = take(1).rearrange("a (p t) -> a p t", p=4)
        Vc = take(1).rearrange("a (k t) -> a k t", k=8)
        Vtok = take(1)
        P = take(2).rearrange("a (q t) -> a q t", q=8)
        LT = take(2).rearrange("a (q t) -> a q t", q=8)
        Ec, d1, EGc, R, Y, Yd, Ot, sz, hq, St = (take(1) for _ in range(10))
        xch = sb("xch", [128, C])
        tail = slot[0]
        T = take(2).rearrange("a (q t) -> a q t", q=8)
        Z = take(2).rearrange("a (q t) -> a q t", q=8)
        Wm = take(2).rearrange("a (q t) -> a q t", q=8)
        Ot2 = take(1)
        assert slot[0] <= 27
        slot[0] = tail
        ta, tna, tw, tu, tl, td = (take(1) for _ in range(6))
        ybuf = [P[:, 0:4].rearrange("a q t -> a (q t)"), P[:, 4:8].rearrange("a q t -> a (q t)")]
        RT = LT[:, 0:4].rearrange("a q t -> a (q t)")
        EG = LT[:, 4:8].rearrange("a q t -> a (q t)")
        EGm, D1 = R, Y
        slot[0] = 0
        glu = [take(1) for _ in range(3)]
        hid = [take(1) for _ in range(3)]
        act = [take(1) for _ in range(3)]
        combT = take(1)
        lg, scp, rep, pk = (take(1) for _ in range(4))
        lg, scp, rep, pk = (t[:, 0:80].rearrange("a (t e) -> a t e", t=4) for t in (lg, scp, rep, pk))
        small = take(1)
        m8 = small[:, 0:32].rearrange("a (t e) -> a t e", t=4)
        tr8 = small[:, 32:64].rearrange("a (t e) -> a t e", t=4)
        mx4, sm4, rc4 = small[:, 64:68], small[:, 68:72], small[:, 72:76]
        slot[0] = 0
        qs, ks, vT, r1, att = (take(1) for _ in range(5))
        qsp = [take(1)[:, 0:256].bitcast(BF16) for _ in range(3)]
        ksp = [take(1)[:, 0:256].bitcast(BF16) for _ in range(3)]
        Ering = [take(1) for _ in range(4)]
        rs = take(1)
        mcol = take(1)
        zcol, zrec = mcol[:, 16:20], mcol[:, 32:36]
        ZP = take(1)[:, 0:64].rearrange("a (k e) -> a k e", k=4)
        zero = take(1)
        rcp = take(1)
        QXe = [take(1)[:, 0:256].bitcast(BF16) for _ in range(2)]
        KXe = [take(1)[:, 0:256].bitcast(BF16) for _ in range(2)]

        ps = [ctx.enter_context(nc.psum_tensor(f"bank{i}", [128, 512], F32)) for i in range(8)]

        def pair(i, q):
            return ps[i + q // 4][:, 128 * (q % 4):128 * (q % 4) + 128]

        eg_d = nc.dram_tensor("eg_scratch", [16, S], F32, kind="Internal").ap()
        gl_d = nc.dram_tensor("gl_scratch", [16, NC], F32, kind="Internal").ap()
        cb_d = nc.dram_tensor("comb_scratch", [E, S], F32, kind="Internal").ap()
        part_d = nc.dram_tensor("parts_scratch", [6, 128, S], BF16, kind="Internal").ap()
        max_d = nc.dram_tensor("max_scratch", [32, 128], BF16, kind="Internal").ap()
        r_d = nc.dram_tensor("rowsum_scratch", [16, S], F32, kind="Internal").ap()

        pack_in = Signal("pack_in", 0)
        setup = Signal("setup", 0)
        x_in_s = Signal("x_loaded", 16)
        y_out = Signal("y_stored", 16)
        NLN = 5
        ln_pe, ln_dve, ln_act = Signal("ln_pe", 2 * NLN), Signal("ln_dve", 3 * NLN), Signal("ln_act", 2 * NLN)
        qkv_mm = Signal("qkv_mm", NT)
        tap0 = Signal("conv_tap0", NT)
        taps = Signal("conv_taps", 3 * NT)
        conv = Signal("conv_done", NT)
        ab_mm = Signal("ab_mm", 1)
        g_act, g_dve = Signal("gates_act", 4), Signal("gates_dve", 17)
        gamma_ok = Signal("gamma_ready", 1)
        gl_dma, eg_dma = Signal("gl_dma", 48), Signal("eg_dma", 48)
        tc_mm, tc_ok = Signal("tokcols_mm", 1), Signal("tokcols_ready", 1)
        s0, bd0 = Signal("state_zero", 1), Signal("blocks_zeroed", 2)
        c_cp = Signal("chunk_copied", 7)
        eg_cp = Signal("chunk_decays_copied", 1)
        c_d1 = Signal("chunk_beta_diag", 1)
        kq_mm, kt_mm, vt_mm, z_mm = (Signal(n, 1) for n in ("kq_mm", "ktok_mm", "vtok_mm", "z_mm"))
        e_ok = Signal("decay_ready", 1, 1)
        lt_dve, p_dve = Signal("lt_raw", 2), Signal("p_ready", 2)
        lt_ok, z2_ok = Signal("lt_ready", 1), Signal("z2_ready", 1)
        kv_ev = Signal("ktok_vtok_ready", 2)
        sz_ok = Signal("silu_z_ready", 1)
        t2_mm = Signal("t2_mm", 2)
        x_mm, w_ev = Signal("level_x_mm", 10), Signal("level_w_ready", 10)
        tz_mm, t_ev, z_ev = Signal("level_tz_mm", 10), Signal("level_t_ready", 10), Signal("level_z_ready", 10)
        ks_mm, qs_mm = Signal("ks_mm", 1), Signal("qs_mm", 1, 1)
        r_dve = Signal("r_dve", 2)
        y_mm, y_ev, yd_ok = Signal("y_mm", 2), Signal("y_ready", 2), Signal("yd_ready", 1)
        o_mm, o_dve = Signal("o_mm", 2), Signal("o_dve", 4, 4)
        s_mm, s_dve = Signal("state_mm", 1), Signal("state_dve", 2, 2)
        hq_ok, var_ok = Signal("h_squared", NC), Signal("var_ready", NC)
        n_sd, n_rs = Signal("rms_sqrt", 1), Signal("rms_recip", 1)
        hn_ok, ot_mm, ot_ev = Signal("h_normed", NC), Signal("o_turned", NC), Signal("o_turned_ready", NC)
        op_mm = Signal("out_proj", 1)
        xr = Signal("x_updated", 3)
        gt_mm, gt_act, gt_dve = Signal("gate_mm", 1), Signal("gate_exp", 1), Signal("gate_dve", 18)
        ct_mm = Signal("comb_turned", 1)
        cb_dma = Signal("comb_dma", 64)
        f1_mm, f_act, f_dve = (Signal(n, NE) for n in ("fc1_mm", "gelu_ready", "hidden_ready"))
        f_pool = Signal("weighted", E)
        f2_mm = Signal("fc2_mm", NE)
        a_mm, a_dve, a_act = Signal("attn_proj_mm", 3), Signal("attn_split", 12), Signal("attn_v", 1)
        a_wr, b_wr = Signal("a_parts_stored", 96), Signal("b_parts_stored", 96)
        a_dma = Signal("attn_spread", 12 * 16)
        a_kx = Signal("a_qk_copied", 4)
        a_s, a_m, a_e = Signal("a_scores", 8, 8), Signal("a_min", 8), Signal("a_exp", 8, 4)
        a_z, a_zp, a_r = Signal("a_recip", 8), Signal("a_cols", 8), Signal("a_rowsum", 8, 4)
        a_sum = Signal("a_sum_mm", 1)
        a_rs, a_rd, a_at, a_wo = Signal("a_sum_ready", 1), Signal("a_sum_dma", 32), Signal("a_out", 1), Signal("a_wo", 1)
        b_xn = Signal("nested_affine", 1)
        b_mm, b_dve, b_pool, b_v = Signal("b_proj_mm", 3), Signal("b_split", 12), Signal("b_vpad", 3), Signal("b_v_ready", 4)
        b_dma = Signal("b_spread", 12 * 16)
        b_s, b_m = Signal("b_scores", 32), Signal("b_min", 32)
        b_tr, b_row, b_rdma = Signal("b_max_turned", 1), Signal("b_max_row", 1), Signal("b_max_dma", 32)
        b_st, b_e, b_pv = Signal("b_scores_t", 32), Signal("b_exp", 32), Signal("b_pv", 32)
        b_rc, b_at = Signal("b_recip", 2), Signal("b_out", 2)
        b_wo = Signal("b_wo", 1)
        fin = Signal("final", 3)
        zero_ok = Signal("zero_ready", 1)
        passed = Signal("passed", 0)

        block = ctx.enter_context(nc.Block())

        def hold(eng):
            eng.sem_inc(passed.sem, 1)

        @block.sync
        def _(sp):
            def spread(b, split, wrote, sent, q, k, width):
                for t, (dst, parts, order) in enumerate(((q, qsp, Q_PARTS), (k, ksp, K_PARTS))):
                    for part in range(3):
                        sp.wait_ge(split.sem, split.at(b, 6 * t + 2 * part + 2))
                        sp.dma_start(part_d[3 * t + part, :, :], parts[part]).then_inc(wrote.sem, 16)
                        sp.wait_ge(wrote.sem, wrote.at(b, 16 * (3 * t + part + 1)))
                        src = part_d[3 * t + part, :, :].rearrange("(g x) t -> x g t", x=width)
                        for i in range(6):
                            if order[i] == part:
                                sp.dma_start(dst[width * i:width * i + width, :, :], src).then_inc(sent.sem, 16)

            half = npack // 2
            sp.dma_start(W[:, 0:half], pack[:, 0:half]).then_inc(pack_in.sem, 16)
            sp.dma_start(W[:, half:npack], pack[:, half:npack]).then_inc(pack_in.sem, 16)
            with sp.Fori(0, B) as b:
                sp.dma_start(x[:, :], x_in[b, :, :]).then_inc(x_in_s.sem, 16)
                sp.wait_ge(g_dve.sem, g_dve.at(b, 16))
                sp.dma_start(eg_d, EGm[0:16, :]).then_inc(eg_dma.sem, 16)
                sp.wait_ge(g_dve.sem, g_dve.at(b, 17))
                sp.dma_start(gl_d, gl[:, :]).then_inc(gl_dma.sem, 16)
                sp.wait_ge(eg_dma.sem, eg_dma.at(b, 16))
                for e in range(2):
                    sp.dma_start(egB[64 * e:64 * e + 64, :, :],
                                 eg_d[8 * e:8 * e + 8, :].unsqueeze(0).broadcast_to([64, 8, S])
                                 ).then_inc(eg_dma.sem, 16)
                sp.wait_ge(gl_dma.sem, gl_dma.at(b, 16))
                for e in range(2):
                    sp.dma_start(glB[64 * e:64 * e + 64, :, :],
                                 gl_d[8 * e:8 * e + 8, :].unsqueeze(0).broadcast_to([64, 8, NC])
                                 ).then_inc(gl_dma.sem, 16)
                sp.wait_ge(gt_dve.sem, gt_dve.at(b, 18))
                sp.dma_start(cb_d, combT[0:E, :]).then_inc(cb_dma.sem, 16)
                sp.wait_ge(cb_dma.sem, cb_dma.at(b, 16))
                for k in range(3):
                    sp.dma_start(combB[:, 5 * k:5 * k + 5, :],
                                 cb_d[5 * k:5 * k + 5, :].unsqueeze(0).broadcast_to([128, 5, S])
                                 ).then_inc(cb_dma.sem, 16)
                sp.wait_ge(f2_mm.sem, f2_mm.at(b, NE))
                spread(b, a_dve, a_wr, a_dma, QX[0:48, :, :], KX[0:48, :, :], 8)
                sp.wait_ge(a_rs.sem, a_rs.at(b, 1))
                sp.dma_start(r_d.rearrange("g (e t) -> e g t", e=16),
                             rs[0:16, :].rearrange("a (g t) -> a g t", g=16)).then_inc(a_rd.sem, 16)
                sp.wait_ge(a_rd.sem, a_rd.at(b, 16))
                sp.dma_start(Rb, r_d.unsqueeze(1).broadcast_to([16, 8, S])).then_inc(a_rd.sem, 16)
                spread(b, b_dve, b_wr, b_dma, QH[0:96, :, :], KH[0:96, :, :], 16)
                sp.wait_ge(b_row.sem, b_row.at(b, 1))
                sp.dma_start(max_d, mrow[:, :]).then_inc(b_rdma.sem, 16)
                sp.wait_ge(b_rdma.sem, b_rdma.at(b, 16))
                sp.dma_start(QH[96:97, :, :].rearrange("a h t -> a (h t)"),
                             max_d.rearrange("q t -> (q t)").unsqueeze(0)).then_inc(b_rdma.sem, 16)
                sp.wait_ge(fin.sem, fin.at(b, 3))
                sp.dma_start(out[b, :, :], x[:, :]).then_inc(y_out.sem, 16)
                sp.wait_ge(y_out.sem, y_out.at(b, 16))
                hold(sp)

        @block.tensor
        def _(pe):
            def layer_norm(b, i):
                pe.matmul(ps[0][:, :], w("mean"), x[:, :] if i < 4 else u[:, :], start=True, stop=True).then_inc(ln_pe.sem, 1)
                pe.wait_ge(ln_act.sem, ln_act.at(b, 2 * i + 1))
                pe.matmul(ps[1][:, :], w("mean"), sq[:, :], start=True, stop=True).then_inc(ln_pe.sem, 1)

            pe.wait_ge(pack_in.sem, 32)
            pe.wait_ge(setup.sem, SETUP)
            pe.sem_inc(qs_mm.sem, 1)
            pe.sem_inc(a_r.sem, 4)
            pe.sem_inc(a_s.sem, 8)
            with pe.Fori(0, B) as b:
                pe.wait_ge(x_in_s.sem, x_in_s.at(b, 16))
                layer_norm(b, 0)
                pe.wait_ge(ln_dve.sem, ln_dve.at(b, 3))
                pe.matmul(ps[6][0:48, :], w("wab"), xn[:, :], start=True, stop=True).then_inc(ab_mm.sem, 1)
                for t in range(NT):
                    if t >= 4:
                        pe.wait_ge(taps.sem, taps.at(b, 3 * (t - 3)))
                    pe.matmul(ps[2 + t % 4][:, :], w("wqkv", 128 * t, 128 * t + 128), xn[:, :],
                              start=True, stop=True).then_inc(qkv_mm.sem, 1)
                pe.wait_ge(g_dve.sem, g_dve.at(b, 17))
                for c in range(NC):
                    for e in range(2):
                        mm = pe.matmul(ps[7][64 * e:64 * e + 64, 16 * c:16 * c + 16], RT[:, C * c:C * c + C],
                                       w("sel", 16 * e, 16 * e + 16), start=True, stop=True)
                mm.then_inc(tc_mm.sem, 1)
                with pe.Fori(0, NC) as c:
                    n = b * NC + c
                    pe.wait_ge(c_cp.sem, c_cp.at(n, 7))
                    pe.wait_ge(s0.sem, s0.at(b, 1))
                    pe.wait_ge(bd0.sem, bd0.at(b, 2))
                    for p in range(4):
                        mm = pe.matmul(ps[0][:, 128 * p:128 * p + 128], Kbd[:, p, :],
                                       KQc[:, p, :, :], start=True, stop=True)
                    mm.then_inc(kq_mm.sem, 1)
                    for p in range(4):
                        mm = pe.transpose(ps[1][:, 128 * p:128 * p + 128], Kbd[:, p, :], w("ident"))
                    mm.then_inc(kt_mm.sem, 1)
                    pe.wait_ge(o_dve.sem, o_dve.at(n - 1, 1))
                    for e in range(2):
                        mm = pe.matmul(ps[3][64 * e:64 * e + 64, :], xch[:, :], w("wz", 512 * e, 512 * e + 512),
                                       start=True, stop=True)
                    mm.then_inc(z_mm.sem, 1)
                    pe.wait_ge(s_dve.sem, s_dve.at(n - 1, 2))
                    for p in range(4):
                        mm = pe.transpose(ps[2][:, 128 * p:128 * p + 128], Vc[:, 2 * p:2 * p + 2, :], w("ident"))
                    mm.then_inc(vt_mm.sem, 1)
                    pe.wait_ge(tc_ok.sem, tc_ok.at(b, 1))
                    pe.wait_ge(z2_ok.sem, z2_ok.at(n, 1))
                    for q in range(8):
                        mm = pe.transpose(pair(6, q), Z[:, q, :], w("ident"))
                        if q % 4 == 3:
                            mm.then_inc(t2_mm.sem, 1)
                    for k, s in enumerate(LEVELS):
                        for h in range(2):
                            pe.wait_ge(t_ev.sem, t_ev.at(n, 2 * k + h + 1))
                            for q in range(4 * h, 4 * h + 4):
                                mm = pe.matmul(pair(4, q), LT[:, q, :], T[:, q, :], start=True, stop=True)
                            mm.then_inc(x_mm.sem, 1)
                        for h in range(2):
                            pe.wait_ge(w_ev.sem, w_ev.at(n, 2 * k + h + 1))
                            if k == 0:
                                pe.wait_ge(p_dve.sem, p_dve.at(n, 2))
                                pe.wait_ge(kv_ev.sem, kv_ev.at(n, 1))
                            else:
                                pe.wait_ge(z_ev.sem, z_ev.at(n, 2 * k + h - 1))
                            if s < LEVELS[-1]:
                                for q in range(4 * h, 4 * h + 4):
                                    pe.matmul(pair(6, q), Z[:, q, :], Wm[:, q, :], start=True, stop=True)
                            for q in range(4 * h, 4 * h + 4):
                                mm = pe.matmul(pair(0, q), Wm[:, q, :], Z[:, q, :], start=True, stop=True)
                            mm.then_inc(tz_mm.sem, 1)
                    pe.wait_ge(kv_ev.sem, kv_ev.at(n, 2))
                    for p in range(4):
                        mm = pe.matmul(ps[2][:, 128 * p:128 * p + 128], Kbd[:, p, :], St[:, 128 * p:128 * p + 128],
                                       start=True, stop=True)
                    mm.then_inc(ks_mm.sem, 1)
                    pe.wait_ge(sz_ok.sem, sz_ok.at(n, 1))
                    for p in range(4):
                        mm = pe.matmul(ps[3][:, 128 * p:128 * p + 128], Qbd[:, p, :], St[:, 128 * p:128 * p + 128],
                                       start=True, stop=True)
                    mm.then_inc(qs_mm.sem, 1)
                    pe.wait_ge(r_dve.sem, r_dve.at(n, 2))
                    pe.wait_ge(z_ev.sem, z_ev.at(n, 10))
                    for q in range(8):
                        mm = pe.matmul(pair(4, q), Z[:, q, :], R[:, 128 * (q // 2):128 * (q // 2) + 128],
                                       start=True, stop=True)
                        if q % 4 == 3:
                            mm.then_inc(y_mm.sem, 1)
                    pe.wait_ge(y_ev.sem, y_ev.at(n, 2))
                    for q in range(8):
                        mm = pe.matmul(pair(6, q), P[:, q, :], Y[:, 128 * (q // 2):128 * (q // 2) + 128],
                                       start=True, stop=True)
                        if q % 4 == 3:
                            mm.then_inc(o_mm.sem, 1)
                    pe.wait_ge(yd_ok.sem, yd_ok.at(n, 1))
                    for p in range(4):
                        mm = pe.matmul(ps[2][:, 128 * p:128 * p + 128], Ktok[:, p, :], Yd[:, 128 * p:128 * p + 128],
                                       start=True, stop=True)
                    mm.then_inc(s_mm.sem, 1)
                for c in range(NC):
                    pe.wait_ge(hn_ok.sem, hn_ok.at(b, c + 1))
                    if c >= 2:
                        pe.wait_ge(ot_ev.sem, ot_ev.at(b, c - 1))
                    for p in range(4):
                        mm = pe.transpose(ps[2 + c % 2][:, 128 * p:128 * p + 128], Hall[:, c, 128 * p:128 * p + 128],
                                          w("ident"))
                    mm.then_inc(ot_mm.sem, 1)
                pe.wait_ge(ot_ev.sem, ot_ev.at(b, NC))
                for k in range(8):
                    mm = pe.matmul(ps[4][:, :], w("wout", 128 * k, 128 * k + 128), oT[:, k, :],
                                   start=(k == 0), stop=(k == 7))
                mm.then_inc(op_mm.sem, 1)
                pe.wait_ge(xr.sem, xr.at(b, 1))
                layer_norm(b, 1)
                pe.wait_ge(ln_dve.sem, ln_dve.at(b, 6))
                for t in range(4):
                    mm = pe.matmul(ps[6][:, 16 * t:16 * t + E], xn[:, 128 * t:128 * t + 128], w("gate"),
                                   start=True, stop=True)
                mm.then_inc(gt_mm.sem, 1)

                def fc1(j):
                    k = j % 3
                    if j >= 3:
                        pe.wait_ge(f_act.sem, f_act.at(b, j - 2))
                        pe.wait_ge(f_dve.sem, f_dve.at(b, j - 2))
                    if j < 2:
                        wx, wg = w("sfc1", 128 * j, 128 * j + 128), w("sfc1", 256 + 128 * j, 384 + 128 * j)
                    else:
                        o = 256 * (j - 2)
                        wx, wg = w("fc1", o, o + 128), w("fc1", o + 128, o + 256)
                    pe.matmul(ps[2 * k][:, :], wx, xn[:, :], start=True, stop=True)
                    pe.matmul(ps[2 * k + 1][:, :], wg, xn[:, :], start=True, stop=True).then_inc(f1_mm.sem, 1)

                def fc2(j):
                    if j < 2:
                        pe.wait_ge(f_dve.sem, f_dve.at(b, j + 1))
                    else:
                        pe.wait_ge(f_pool.sem, f_pool.at(b, j - 1))
                    lhs = w("sfc2", 128 * j, 128 * j + 128) if j < 2 else w("fc2", 128 * (j - 2), 128 * (j - 1))
                    pe.matmul(ps[7][:, :], lhs, (hid if j < 2 else act)[j % 3], start=(j == 0), stop=(j == NE - 1)).then_inc(f2_mm.sem, 1)

                fc1(0)
                fc1(1)
                fc2(0)
                fc1(2)
                fc2(1)
                pe.wait_ge(gt_dve.sem, gt_dve.at(b, 17))
                for t in range(4):
                    mm = pe.transpose(ps[6][0:E, 128 * t:128 * t + 128], lg[:, t, 0:E], w("ident"))
                mm.then_inc(ct_mm.sem, 1)
                pe.wait_ge(gt_dve.sem, gt_dve.at(b, 18))
                pe.matmul(ps[7][:, :], w("fc2b", p1=E), combT[0:E, :], start=False, stop=False)
                for j in range(3, NE):
                    fc1(j)
                    fc2(j - 1)
                fc2(NE - 1)
                pe.wait_ge(xr.sem, xr.at(b, 2))
                layer_norm(b, 2)
                pe.wait_ge(ln_dve.sem, ln_dve.at(b, 9))
                for k, name in enumerate(("wq", "wk", "wv")):
                    pe.matmul(ps[2 + k][:, :], w(name), xn[:, :], start=True, stop=True).then_inc(a_mm.sem, 1)
                pe.wait_ge(a_dma.sem, a_dma.at(b, 12 * 16))
                pe.wait_ge(a_dve.sem, a_dve.at(b, 12))
                pe.wait_ge(a_act.sem, a_act.at(b, 1))
                pe.wait_ge(zero_ok.sem, zero_ok.at(b, 1))
                pe.matmul(ps[4][0:16, :], zero[:, 0:16], xn[:, :], start=True, stop=False, skip_group_check=True)
                with pe.Fori(0, H1 // 2) as e2:
                    n = b * (H1 // 2) + e2
                    for i in range(2):
                        pe.wait_ge(a_kx.sem, a_kx.at(n, 2 * i + 2))
                        for k in range(4):
                            pe.wait_ge(a_e.sem, a_e.at(n, 4 * i + k - 3))
                            pe.matmul(ps[k][:, :], KXe[i][0:48, 128 * k:128 * k + 128],
                                      QXe[i][0:48, :], start=True, stop=True).then_inc(a_s.sem, 1)
                        for k in range(4):
                            pe.wait_ge(a_e.sem, a_e.at(n, 4 * i + k + 1))
                            pe.wait_ge(a_zp.sem, a_zp.at(n, 4 * i + k + 1))
                            pe.matmul(ps[4][0:16, :], ZP[:, k, :], Ering[k], start=False, stop=False,
                                      skip_group_check=True).then_inc(a_r.sem, 1)
                pe.matmul(ps[4][0:16, :], zero[:, 0:16], xn[:, :], start=False, stop=True,
                          skip_group_check=True).then_inc(a_sum.sem, 1)
                pe.wait_ge(a_at.sem, a_at.at(b, 1))
                pe.matmul(ps[5][:, :], w("wo"), att, start=True, stop=True).then_inc(a_wo.sem, 1)
                pe.wait_ge(xr.sem, xr.at(b, 3))
                layer_norm(b, 3)
                pe.wait_ge(ln_dve.sem, ln_dve.at(b, 12))
                layer_norm(b, 4)
                pe.wait_ge(b_xn.sem, b_xn.at(b, 1))
                for k, name in enumerate(("qw", "kw")):
                    for e in range(NX):
                        m = D >> e
                        mm = pe.matmul(ps[2 + k][:, 128 * e:128 * e + 128], w(name, p1=m),
                                       xn[0:m, 128 * e:128 * e + 128], start=True, stop=True)
                    mm.then_inc(b_mm.sem, 1)
                for e in range(NX):
                    m = D >> e
                    mm = pe.matmul(ps[4][:, 128 * e:128 * e + 128], xn[0:m, 128 * e:128 * e + 128],
                                   w("vw", p1=m), start=True, stop=True)
                mm.then_inc(b_mm.sem, 1)
                pe.wait_ge(b_dma.sem, b_dma.at(b, 12 * 16))
                pe.wait_ge(b_dve.sem, b_dve.at(b, 12))
                pe.wait_ge(b_v.sem, b_v.at(b, 4))
                for i in range(32):
                    h, q = i // 4, i % 4
                    if i >= 4:
                        pe.wait_ge(b_m.sem, b_m.at(b, i - 3))
                    pe.matmul(ps[i % 4][:, :], QH[0:96, h, 128 * q:128 * q + 128], KH[0:96, h, :],
                              start=True, stop=True).then_inc(b_s.sem, 1)
                pe.wait_ge(b_m.sem, b_m.at(b, 32))
                pe.transpose(ps[7][0:32, 0:128], mq[:, :], w("ident")).then_inc(b_tr.sem, 1)
                pe.wait_ge(b_rdma.sem, b_rdma.at(b, 32))
                pe.wait_ge(b_pool.sem, b_pool.at(b, 3))

                def pv(i):
                    h, k = i // 4, i % 4
                    pe.wait_ge(b_e.sem, b_e.at(b, i + 1))
                    pe.matmul(ps[4 + h // 4][:, :], Vp[:, k, h, :], Ering[i % 4], start=(i % 16 == 0),
                              stop=(i % 16 == 15)).then_inc(b_pv.sem, 1)

                for i in range(32):
                    h, k = i // 4, i % 4
                    if i >= 4:
                        pe.wait_ge(b_e.sem, b_e.at(b, i - 3))
                    pe.matmul(ps[i % 4][:, :], KH[0:97, h, 128 * k:128 * k + 128], QH[0:97, h, :],
                              start=True, stop=True).then_inc(b_st.sem, 1)
                    if i >= 2:
                        pv(i - 2)
                pv(30)
                pv(31)
                pe.wait_ge(b_at.sem, b_at.at(b, 2))
                for e in range(NX):
                    m = D >> e
                    mm = pe.matmul(ps[0][:, 128 * e:128 * e + 128], owm[0:m, e, :], att[0:m, 128 * e:128 * e + 128],
                                   start=True, stop=True)
                mm.then_inc(b_wo.sem, 1)

        @block.scalar
        def _(sc):
            def layer_norm(b, i):
                sc.wait_ge(ln_dve.sem, ln_dve.at(b, 3 * i + 1))
                sc.activation(sq[:, :], xc[:, :], ACT.Square).then_inc(ln_act.sem, 1)
                sc.wait_ge(ln_pe.sem, ln_pe.at(b, 2 * i + 2))
                sc.activation(sd[:, :], ps[1][:, :], ACT.Sqrt, bias=w("lneps")).then_inc(ln_act.sem, 1)

            sc.wait_ge(pack_in.sem, 32)
            sc.wait_ge(setup.sem, SETUP - 1)
            sc.activation(expA[:, :], expA[:, :], ACT.Exp).then_inc(setup.sem, 1)
            sc.wait_ge(setup.sem, SETUP)
            sc.sem_inc(a_e.sem, 4)
            with sc.Fori(0, B) as b:
                layer_norm(b, 0)

                def first_tap(t):
                    sc.wait_ge(qkv_mm.sem, qkv_mm.at(b, t + 1))
                    if t >= 2:
                        sc.wait_ge(conv.sem, conv.at(b, t - 1))
                    sc.activation(ybuf[t % 2], ps[2 + t % 4][:, :], ACT.Identity,
                                  scale=w("convw", KSZ * t + 3, KSZ * t + 4)).then_inc(tap0.sem, 1)

                sc.wait_ge(ab_mm.sem, ab_mm.at(b, 1))
                sc.activation(td[32:48, :], ps[6][32:48, :], ACT.Exp, scale=-1.0).then_inc(g_act.sem, 1)
                sc.wait_ge(g_dve.sem, g_dve.at(b, 5))
                sc.activation(tw[0:16, :], tna[0:16, :], ACT.Exp, scale=-1.0).then_inc(g_act.sem, 1)
                sc.wait_ge(g_dve.sem, g_dve.at(b, 6))
                sc.activation(tl[0:16, :], tu[0:16, :], ACT.Ln).then_inc(g_act.sem, 1)
                sc.wait_ge(g_dve.sem, g_dve.at(b, 12))
                sc.activation(EG[0:16, :], tna[0:16, :], ACT.Exp, scale=-1.0).then_inc(g_act.sem, 1)
                first_tap(0)
                for t in range(NT):
                    if t + 1 < NT:
                        first_tap(t + 1)
                    sc.wait_ge(taps.sem, taps.at(b, 3 * t + 3))
                    dst = QT[:, t, :] if t < 4 else KT[:, t - 4, :] if t < 8 else VT[:, t - 8, :]
                    sc.activation(dst, ybuf[t % 2], ACT.Silu).then_inc(conv.sem, 1)
                with sc.Fori(0, NC) as c:
                    n = b * NC + c
                    sc.wait_ge(kt_mm.sem, kt_mm.at(n, 1))
                    sc.activation(Ktok.rearrange("a p t -> a (p t)"), ps[1][:, :], ACT.Copy).then_inc(kv_ev.sem, 1)
                    sc.wait_ge(z_mm.sem, z_mm.at(n, 1))
                    sc.wait_ge(o_dve.sem, o_dve.at(n - 1, 4))
                    sc.activation(sz, ps[3][:, :], ACT.Silu).then_inc(sz_ok.sem, 1)
                    sc.wait_ge(vt_mm.sem, vt_mm.at(n, 1))
                    sc.activation(Vtok, ps[2][:, :], ACT.Copy).then_inc(kv_ev.sem, 1)
                    for h in range(2):
                        sc.wait_ge(t2_mm.sem, t2_mm.at(n, h + 1))
                        sc.activation(T[:, 4 * h:4 * h + 4, :].rearrange("a q t -> a (q t)"), ps[6 + h][:, :],
                                      ACT.Copy).then_inc(t_ev.sem, 1)
                    for k, s in enumerate(LEVELS):
                        for h in range(2):
                            sc.wait_ge(tz_mm.sem, tz_mm.at(n, 2 * k + h + 1))
                            if s < LEVELS[-1]:
                                sc.activation(T[:, 4 * h:4 * h + 4, :].rearrange("a q t -> a (q t)"),
                                              ps[6 + h][:, :], ACT.Copy).then_inc(t_ev.sem, 1)
                            sc.activation(Z[:, 4 * h:4 * h + 4, :].rearrange("a q t -> a (q t)"),
                                          ps[h][:, :], ACT.Copy).then_inc(z_ev.sem, 1)
                    for h in range(2):
                        sc.wait_ge(y_mm.sem, y_mm.at(n, h + 1))
                        src = ps[4 + h][:, :].rearrange("a (p r q) -> a p r q", p=2, r=2)
                        for r in range(2):
                            ev = sc.activation(
                                Y[:, 256 * h:256 * h + 256].rearrange("a (p r v) -> a p r v", p=2, r=2)[:, :, r, :],
                                src[:, :, r, 64 * r:64 * r + 64], ACT.Copy)
                            if r == 1:
                                ev.then_inc(y_ev.sem, 1)
                for c in range(NC):
                    sc.wait_ge(o_dve.sem, o_dve.at(b * NC + c, 4))
                    if c >= 2:
                        sc.wait_ge(var_ok.sem, var_ok.at(b, c - 1))
                    sc.activation((hq, Ot2)[c % 2], Hall[:, c, :], ACT.Square).then_inc(hq_ok.sem, 1)
                sc.wait_ge(var_ok.sem, var_ok.at(b, NC))
                sc.activation(rstd[:, :, :], var[:, :, :], ACT.Sqrt, bias=w("rmseps"), scale=1.0 / 64).then_inc(n_sd.sem, 1)
                for c in range(NC):
                    sc.wait_ge(ot_mm.sem, ot_mm.at(b, c + 1))
                    sc.activation(oT[:, :, C * c:C * c + C],
                                  ps[2 + c % 2][:, :].rearrange("a (k t) -> a k t", k=8), ACT.Copy).then_inc(ot_ev.sem, 1)
                layer_norm(b, 1)
                sc.wait_ge(gt_dve.sem, gt_dve.at(b, 3))
                sc.activation(lg[:, :, 0:E], lg[:, :, 0:E], ACT.Exp).then_inc(gt_act.sem, 1)
                for j in range(NE):
                    sc.wait_ge(f1_mm.sem, f1_mm.at(b, j + 1))
                    if j >= 3:
                        sc.wait_ge(f_dve.sem, f_dve.at(b, j - 2))
                    bias = w("sfc1b", 2 + j, 3 + j) if j < 2 else w("fc1b", 2 * (j - 2) + 1, 2 * (j - 2) + 2)
                    sc.activation(glu[j % 3], ps[2 * (j % 3) + 1][:, :], ACT.Gelu, bias=bias).then_inc(f_act.sem, 1)
                layer_norm(b, 2)
                sc.wait_ge(a_mm.sem, a_mm.at(b, 3))
                sc.activation(vT, ps[4][:, :], ACT.Identity, bias=w("bv")).then_inc(a_act.sem, 1)
                with sc.Fori(0, H1 // 2) as e2:
                    n = b * (H1 // 2) + e2
                    for k in range(8):
                        sc.wait_ge(a_m.sem, a_m.at(n, k + 1))
                        sc.wait_ge(a_r.sem, a_r.at(n, k - 3))
                        sc.activation(Ering[k % 4], ps[k % 4][:, :], ACT.Exp, bias=mcol[:, k % 4:k % 4 + 1],
                                      scale=-1.0, accum_out=zcol[:, k % 4:k % 4 + 1]).then_inc(a_e.sem, 1)
                sc.wait_ge(a_rs.sem, a_rs.at(b, 1))
                layer_norm(b, 3)
                layer_norm(b, 4)
                sc.wait_ge(b_tr.sem, b_tr.at(b, 1))
                sc.activation(mrow[:, :], ps[7][0:32, 0:128], ACT.Copy, scale=-1.0).then_inc(b_row.sem, 1)
                for i in range(32):
                    sc.wait_ge(b_st.sem, b_st.at(b, i + 1))
                    if i >= 4:
                        sc.wait_ge(b_pv.sem, b_pv.at(b, i - 3))
                    sc.activation(Ering[i % 4], ps[i % 4][:, :], ACT.Exp, scale=-1.0).then_inc(b_e.sem, 1)

        @block.vector
        def _(ve):
            def layer_norm(b, i):
                src = x if i < 4 else u
                dst = u if i == 3 else xn
                ve.wait_ge(ln_pe.sem, ln_pe.at(b, 2 * i + 1))
                ve.tensor_tensor(xc[:, :], src[:, :], ps[0][:, :], ALU.subtract).then_inc(ln_dve.sem, 1)
                ve.wait_ge(ln_act.sem, ln_act.at(b, 2 * i + 2))
                ve.reciprocal(sd[:, :], sd[:, :]).then_inc(ln_dve.sem, 1)
                ve.wait_ge(ln_dve.sem, ln_dve.at(b, 3 * i + 2))
                ve.tensor_tensor(dst[:, :], xc[:, :], sd[:, :], ALU.mult).then_inc(ln_dve.sem, 1)

            ve.wait_ge(pack_in.sem, 32)
            o, _n = at["fc2"]
            fc2 = W[:, o:o + E * 128].rearrange("a (j d) -> a j d", j=E)
            ve.tensor_tensor(fc2, fc2, w("gm").unsqueeze(2).broadcast_to([128, E, 128]), ALU.mult).then_inc(setup.sem, 1)
            o, _n = at["sfc2"]
            sfc2 = W[:, o:o + 256].rearrange("a (j d) -> a j d", j=2)
            ve.tensor_tensor(sfc2, sfc2, w("sgm").unsqueeze(2).broadcast_to([128, 2, 128]), ALU.mult).then_inc(setup.sem, 1)
            ve.tensor_scalar(w("wout"), w("wout"), w("normw"), None, ALU.mult).then_inc(setup.sem, 1)
            ve.memset(owm[:, :, :], 0.0).then_inc(setup.sem, 1)
            ve.memset(obm[:, :], 0.0).then_inc(setup.sem, 1)
            ve.wait_ge(setup.sem, 5)
            for e in range(NX):
                m = D >> e
                ve.tensor_copy(owm[0:m, e, 0:m], w("ow", 0, m, 0, m)).then_inc(setup.sem, 1)
                ve.tensor_copy(obm[0:m, e:e + 1], w("ob", p1=m)).then_inc(setup.sem, 1)
            ve.tensor_scalar(expA[:, :], w("alog"), 88.0, None, ALU.min).then_inc(setup.sem, 1)
            ve.wait_ge(setup.sem, SETUP)
            ve.sem_inc(e_ok.sem, 1)
            ve.sem_inc(o_dve.sem, 4)
            ve.sem_inc(s_dve.sem, 2)
            with ve.Fori(0, B) as b:
                ve.wait_ge(x_in_s.sem, x_in_s.at(b, 16))
                layer_norm(b, 0)
                ve.memset(RT, 0.0).then_inc(g_dve.sem, 1)
                ve.wait_ge(g_dve.sem, g_dve.at(b, 1))
                ve.wait_ge(g_act.sem, g_act.at(b, 1))
                ve.tensor_scalar(td[32:48, :], td[32:48, :], 1.0, None, ALU.add).then_inc(g_dve.sem, 1)
                ve.wait_ge(g_dve.sem, g_dve.at(b, 2))
                ve.reciprocal(RT[32:48, :], td[32:48, :]).then_inc(g_dve.sem, 1)
                ve.wait_ge(g_dve.sem, g_dve.at(b, 3))
                ve.tensor_scalar(ta[0:16, :], ps[6][0:16, :], w("dtb", p1=16), None, ALU.add).then_inc(g_dve.sem, 1)
                ve.wait_ge(g_dve.sem, g_dve.at(b, 4))
                ve.scalar_tensor_tensor(tna[0:16, :], ta[0:16, :], -1.0, ta[0:16, :], ALU.mult, ALU.max).then_inc(g_dve.sem, 1)
                ve.wait_ge(g_dve.sem, g_dve.at(b, 5))
                ve.wait_ge(g_act.sem, g_act.at(b, 2))
                ve.tensor_scalar(tu[0:16, :], tw[0:16, :], 1.0, None, ALU.add).then_inc(g_dve.sem, 1)
                ve.wait_ge(g_dve.sem, g_dve.at(b, 6))
                ve.scalar_tensor_tensor(tw[0:16, :], tu[0:16, :], -1.0, tw[0:16, :], ALU.add, ALU.subtract).then_inc(g_dve.sem, 1)
                ve.wait_ge(g_dve.sem, g_dve.at(b, 7))
                ve.wait_ge(g_act.sem, g_act.at(b, 3))
                ve.reciprocal(tu[0:16, :], tu[0:16, :]).then_inc(g_dve.sem, 1)
                ve.wait_ge(g_dve.sem, g_dve.at(b, 8))
                ve.tensor_tensor(tw[0:16, :], tw[0:16, :], tu[0:16, :], ALU.mult).then_inc(g_dve.sem, 1)
                ve.wait_ge(g_dve.sem, g_dve.at(b, 9))
                ve.tensor_tensor(tl[0:16, :], tl[0:16, :], tw[0:16, :], ALU.subtract).then_inc(g_dve.sem, 1)
                ve.wait_ge(g_dve.sem, g_dve.at(b, 10))
                ve.scalar_tensor_tensor(tl[0:16, :], ta[0:16, :], 0.0, tl[0:16, :], ALU.max, ALU.add).then_inc(g_dve.sem, 1)
                ve.wait_ge(g_dve.sem, g_dve.at(b, 11))
                ve.tensor_scalar(tna[0:16, :], tl[0:16, :], expA[0:16, :], 1e30, ALU.mult, ALU.min).then_inc(g_dve.sem, 1)
                ve.wait_ge(g_dve.sem, g_dve.at(b, 12))
                ve.wait_ge(g_act.sem, g_act.at(b, 4))
                ve.tensor_copy(EGm[0:16, :], EG[0:16, :]).then_inc(g_dve.sem, 1)
                ve.wait_ge(g_dve.sem, g_dve.at(b, 13))
                ve.memset(D1[0:16, :], 0.0).then_inc(g_dve.sem, 1)
                ve.wait_ge(g_dve.sem, g_dve.at(b, 14))
                ve.tensor_copy(D1[0:16, 0:S:C], EG[0:16, 0:S:C]).then_inc(g_dve.sem, 1)
                ve.wait_ge(g_dve.sem, g_dve.at(b, 15))
                ve.memset(EGm[0:16, 0:S:C], 0.0).then_inc(g_dve.sem, 1)
                ve.wait_ge(g_dve.sem, g_dve.at(b, 16))
                ve.tensor_tensor_scan(RT[0:16, :], EGm[0:16, :], D1[0:16, :], 0.0, ALU.mult, ALU.add).then_inc(gamma_ok.sem, 1)
                ve.wait_ge(gamma_ok.sem, gamma_ok.at(b, 1))
                ve.tensor_copy(gl[:, :], RT[0:16, C - 1:S:C]).then_inc(g_dve.sem, 1)
                for t in range(NT):
                    ve.wait_ge(tap0.sem, tap0.at(b, t + 1))
                    for k, j in enumerate((2, 1, 0)):
                        sh = KSZ - 1 - j
                        if k:
                            ve.wait_ge(taps.sem, taps.at(b, 3 * t + k))
                        ve.scalar_tensor_tensor(ybuf[t % 2][:, sh:S], ps[2 + t % 4][:, 0:S - sh],
                                                w("convw", KSZ * t + j, KSZ * t + j + 1), ybuf[t % 2][:, sh:S],
                                                ALU.mult, ALU.add).then_inc(taps.sem, 1)
                ve.wait_ge(tc_mm.sem, tc_mm.at(b, 1))
                ve.tensor_copy(tc[:, :, :, :].rearrange("a c q n -> a (c q n)"), ps[7][:, 0:NC * 16]).then_inc(tc_ok.sem, 1)
                ve.wait_ge(eg_dma.sem, eg_dma.at(b, 48))
                ve.wait_ge(gl_dma.sem, gl_dma.at(b, 48))
                ve.memset(St, 0.0).then_inc(s0.sem, 1)
                with ve.Fori(0, NC) as c:
                    n = b * NC + c
                    v3 = lambda t: t.rearrange("a (q v) -> a q v", q=8)
                    gamma = tc[:, bass.ds(c, 1), 0, :].rearrange("a c q -> a (c q)").unsqueeze(2).broadcast_to([128, 8, 64])
                    glast = glB[:, :, bass.ds(c, 1)].broadcast_to([128, 8, 64])
                    ve.wait_ge(c_d1.sem, c_d1.at(n, 1))
                    ve.wait_ge(bd0.sem, bd0.at(b, 2))
                    ve.tensor_tensor_scan(Ec, EGc, d1, 0.0, ALU.mult, ALU.add).then_inc(e_ok.sem, 1)
                    ve.wait_ge(e_ok.sem, e_ok.at(n, 1))
                    ve.wait_ge(kq_mm.sem, kq_mm.at(n, 1))
                    for dst, qk, sig in ((LT, 0, lt_dve), (P, 1, p_dve)):
                        for e in range(2):
                            rows = slice(64 * e, 64 * e + 64)
                            src = ps[0][rows, :].rearrange("a (p q t) -> a p q t", p=4, q=2)[:, :, qk, :]
                            ve.tensor_tensor(
                                dst[rows, :, 64 * e:64 * e + 64].rearrange("a (p r) t -> a p r t", r=2),
                                src.unsqueeze(2).broadcast_to([64, 4, 2, 64]),
                                Ec[rows, :].rearrange("a (p r t) -> a p r t", p=4, r=2), ALU.mult).then_inc(sig.sem, 1)
                    ve.wait_ge(lt_ok.sem, lt_ok.at(n, 1))
                    ve.tensor_tensor(Z[:, :, :], LT[:, :, :], w("mask1").unsqueeze(1).broadcast_to([128, 8, 128]),
                                     ALU.mult).then_inc(z2_ok.sem, 1)
                    for k, s in enumerate(LEVELS):
                        mask = w("masks", 128 * k, 128 * k + 128).unsqueeze(1).broadcast_to([128, 4, 128])
                        for h in range(2):
                            ve.wait_ge(x_mm.sem, x_mm.at(n, 2 * k + h + 1))
                            ve.tensor_tensor(Wm[:, 4 * h:4 * h + 4, :],
                                             ps[4 + h][:, :].rearrange("a (q t) -> a q t", q=4), mask,
                                             ALU.mult).then_inc(w_ev.sem, 1)
                    ve.wait_ge(ks_mm.sem, ks_mm.at(n, 1))
                    ve.tensor_tensor(v3(R), v3(ps[2][:, :]), gamma, ALU.mult).then_inc(r_dve.sem, 1)
                    ve.wait_ge(r_dve.sem, r_dve.at(n, 1))
                    ve.wait_ge(kv_ev.sem, kv_ev.at(n, 2))
                    ve.tensor_tensor(R, Vtok, R, ALU.subtract).then_inc(r_dve.sem, 1)
                    ve.wait_ge(qs_mm.sem, qs_mm.at(n, 1))
                    ve.tensor_tensor(v3(Ot), v3(ps[3][:, :]), gamma, ALU.mult).then_inc(o_dve.sem, 1)
                    ve.tensor_tensor(v3(St), v3(St), glast, ALU.mult).then_inc(s_dve.sem, 1)
                    ve.wait_ge(y_ev.sem, y_ev.at(n, 2))
                    ve.tensor_tensor(v3(Yd), v3(Y), v3(Ec)[:, :, 63:64].broadcast_to([128, 8, 64]),
                                     ALU.mult).then_inc(yd_ok.sem, 1)
                    ve.wait_ge(o_dve.sem, o_dve.at(n, 1))
                    for h in range(2):
                        ve.wait_ge(o_mm.sem, o_mm.at(n, h + 1))
                        for r in range(2):
                            ov = Ot[:, 256 * h:256 * h + 256].rearrange("a (p r v) -> a p r v", p=2, r=2)[:, :, r, :]
                            src = ps[6 + h][:, :].rearrange("a (p r q) -> a p r q", p=2, r=2)[:, :, r, 64 * r:64 * r + 64]
                            ins = ve.tensor_tensor(ov, ov, src, ALU.add)
                            if r == 1:
                                ins.then_inc(o_dve.sem, 1)
                    ve.wait_ge(s_mm.sem, s_mm.at(n, 1))
                    ve.wait_ge(s_dve.sem, s_dve.at(n, 1))
                    ve.tensor_tensor(St, St, ps[2][:, :], ALU.add).then_inc(s_dve.sem, 1)
                    ve.wait_ge(o_dve.sem, o_dve.at(n, 3))
                    ve.wait_ge(sz_ok.sem, sz_ok.at(n, 1))
                    hc = Hall[:, bass.ds(c, 1), :].rearrange("a c n -> a (c n)")
                    ve.scalar_tensor_tensor(hc, Ot, 0.125, sz, ALU.mult, ALU.mult).then_inc(o_dve.sem, 1)
                for c in range(NC):
                    ve.wait_ge(hq_ok.sem, hq_ok.at(b, c + 1))
                    ve.tensor_reduce(var[:, c, :], (hq, Ot2)[c % 2].rearrange("a (q v) -> a q v", q=8), AX,
                                     ALU.add).then_inc(var_ok.sem, 1)
                ve.wait_ge(n_sd.sem, n_sd.at(b, 1))
                ve.reciprocal(rstd[:, :, :], rstd[:, :, :]).then_inc(n_rs.sem, 1)
                ve.wait_ge(n_rs.sem, n_rs.at(b, 1))
                for c in range(NC):
                    hv = Hall[:, c, :].rearrange("a (q v) -> a q v", q=8)
                    ve.tensor_tensor(hv, hv, rstd[:, c, :].unsqueeze(2).broadcast_to([128, 8, 64]),
                                     ALU.mult).then_inc(hn_ok.sem, 1)
                ve.wait_ge(op_mm.sem, op_mm.at(b, 1))
                ve.tensor_tensor(x[:, :], x[:, :], ps[4][:, :], ALU.add).then_inc(xr.sem, 1)
                layer_norm(b, 1)
                ve.wait_ge(gt_mm.sem, gt_mm.at(b, 1))
                ve.tensor_copy(lg[:, :, 0:E], ps[6][:, 0:64].rearrange("a (t e) -> a t e", t=4)[:, :, 0:E]).then_inc(gt_dve.sem, 1)
                ve.wait_ge(gt_dve.sem, gt_dve.at(b, 1))
                ve.tensor_reduce(mx4, lg[:, :, 0:E], AX, ALU.max).then_inc(gt_dve.sem, 1)
                ve.wait_ge(gt_dve.sem, gt_dve.at(b, 2))
                ve.tensor_tensor(lg[:, :, 0:E], lg[:, :, 0:E], mx4.unsqueeze(2).broadcast_to([128, 4, E]), ALU.subtract).then_inc(gt_dve.sem, 1)
                ve.wait_ge(gt_dve.sem, gt_dve.at(b, 3))
                ve.wait_ge(gt_act.sem, gt_act.at(b, 1))
                ve.tensor_reduce(sm4, lg[:, :, 0:E], AX, ALU.add).then_inc(gt_dve.sem, 1)
                ve.wait_ge(gt_dve.sem, gt_dve.at(b, 4))
                ve.reciprocal(rc4, sm4).then_inc(gt_dve.sem, 1)
                ve.wait_ge(gt_dve.sem, gt_dve.at(b, 5))
                ve.tensor_tensor(scp[:, :, 0:E], lg[:, :, 0:E], rc4.unsqueeze(2).broadcast_to([128, 4, E]), ALU.mult).then_inc(gt_dve.sem, 1)
                ve.wait_ge(gt_dve.sem, gt_dve.at(b, 6))
                ve.tensor_copy(scp[:, :, E:20], w("pads").unsqueeze(1).broadcast_to([128, 4, 5])).then_inc(gt_dve.sem, 1)
                ve.wait_ge(gt_dve.sem, gt_dve.at(b, 7))
                hold(ve)
                for t in range(4):
                    ins = ve.max(m8[:, t, :], scp[:, t, :])
                    if t == 3:
                        ins.then_inc(gt_dve.sem, 1)
                        ve.wait_ge(gt_dve.sem, gt_dve.at(b, 8))
                ve.tensor_copy(tr8[:, :, 0:3], m8[:, :, 0:3]).then_inc(gt_dve.sem, 1)
                ve.wait_ge(gt_dve.sem, gt_dve.at(b, 9))
                ve.tensor_copy(tr8[:, :, 3:8], w("pads").unsqueeze(1).broadcast_to([128, 4, 5])).then_inc(gt_dve.sem, 1)
                ve.wait_ge(gt_dve.sem, gt_dve.at(b, 10))
                hold(ve)
                for t in range(4):
                    ins = ve.match_replace(rep[:, t, :], tr8[:, t, :], scp[:, t, :], -9.0)
                    if t == 3:
                        ins.then_inc(gt_dve.sem, 1)
                        ve.wait_ge(gt_dve.sem, gt_dve.at(b, 11))
                ve.tensor_tensor(pk[:, :, 0:E], rep[:, :, 0:E], scp[:, :, 0:E], ALU.not_equal).then_inc(gt_dve.sem, 1)
                ve.wait_ge(gt_dve.sem, gt_dve.at(b, 12))
                ve.tensor_tensor(lg[:, :, 0:E], pk[:, :, 0:E], scp[:, :, 0:E], ALU.mult).then_inc(gt_dve.sem, 1)
                ve.wait_ge(gt_dve.sem, gt_dve.at(b, 13))
                ve.tensor_reduce(sm4, m8[:, :, 0:3], AX, ALU.add).then_inc(gt_dve.sem, 1)
                ve.wait_ge(gt_dve.sem, gt_dve.at(b, 14))
                ve.tensor_scalar(sm4, sm4, 1e-20, None, ALU.add).then_inc(gt_dve.sem, 1)
                ve.wait_ge(gt_dve.sem, gt_dve.at(b, 15))
                ve.reciprocal(rc4, sm4).then_inc(gt_dve.sem, 1)
                ve.wait_ge(gt_dve.sem, gt_dve.at(b, 16))
                ve.tensor_tensor(lg[:, :, 0:E], lg[:, :, 0:E], rc4.unsqueeze(2).broadcast_to([128, 4, E]), ALU.mult).then_inc(gt_dve.sem, 1)
                ve.wait_ge(gt_dve.sem, gt_dve.at(b, 17))

                def hidden(j):
                    ve.wait_ge(f_act.sem, f_act.at(b, j + 1))
                    if j >= 5:
                        ve.wait_ge(f_pool.sem, f_pool.at(b, j - 4))
                    elif j >= 3:
                        ve.wait_ge(f2_mm.sem, f2_mm.at(b, j - 2))
                    bias = w("sfc1b", j, j + 1) if j < 2 else w("fc1b", 2 * (j - 2), 2 * (j - 2) + 1)
                    ve.scalar_tensor_tensor(hid[j % 3], ps[2 * (j % 3)][:, :], bias, glu[j % 3], ALU.add,
                                            ALU.mult).then_inc(f_dve.sem, 1)
                hidden(0)
                hidden(1)
                ve.wait_ge(ct_mm.sem, ct_mm.at(b, 1))
                ve.tensor_copy(combT[0:E, :], ps[6][0:E, :]).then_inc(gt_dve.sem, 1)
                for j in range(2, NE):
                    hidden(j)
                ve.wait_ge(f2_mm.sem, f2_mm.at(b, NE))
                ve.scalar_tensor_tensor(x[:, :], ps[7][:, :], w("sfc2b"), x[:, :], ALU.add, ALU.add).then_inc(xr.sem, 1)
                ve.wait_ge(xr.sem, xr.at(b, 2))
                layer_norm(b, 2)

                def split(sig, k0, src, parts):
                    ve.tensor_copy(parts[0], src).then_inc(sig.sem, 1)
                    ve.wait_ge(sig.sem, sig.at(b, k0 + 1))
                    ve.tensor_tensor(r1, src, parts[0], ALU.subtract).then_inc(sig.sem, 1)
                    ve.wait_ge(sig.sem, sig.at(b, k0 + 2))
                    ve.tensor_copy(parts[1], r1).then_inc(sig.sem, 1)
                    ve.wait_ge(sig.sem, sig.at(b, k0 + 3))
                    ve.tensor_tensor(r1, r1, parts[1], ALU.subtract).then_inc(sig.sem, 1)
                    ve.wait_ge(sig.sem, sig.at(b, k0 + 4))
                    ve.tensor_copy(parts[2], r1).then_inc(sig.sem, 1)
                    ve.wait_ge(sig.sem, sig.at(b, k0 + 5))

                def project(sig_mm, sig, bank, bias, k0, dst, parts, scale):
                    ve.tensor_scalar(dst, ps[bank][:, :], bias, scale, ALU.add, ALU.mult).then_inc(sig.sem, 1)
                    ve.wait_ge(sig.sem, sig.at(b, k0 + 1))
                    split(sig, k0 + 1, dst, parts)

                scale = float(np.float32(1.0 / np.sqrt(128)))
                ve.wait_ge(a_mm.sem, a_mm.at(b, 2))
                project(a_mm, a_dve, 2, w("bq"), 0, qs, qsp, -scale)
                project(a_mm, a_dve, 3, w("bk"), 6, ks, ksp, scale)
                hold(ve)
                with ve.Fori(0, H1 // 2) as e2:
                    n = b * (H1 // 2) + e2
                    for i in range(2):
                        for k in range(4):
                            ve.wait_ge(a_s.sem, a_s.at(n, 4 * i + k + 1))
                            ve.wait_ge(a_e.sem, a_e.at(n, 4 * i + k - 3))
                            ve.tensor_reduce(mcol[:, k:k + 1], ps[k][:, :], AX, ALU.min).then_inc(a_m.sem, 1)
                        for k in range(4):
                            ve.wait_ge(a_e.sem, a_e.at(n, 4 * i + k + 1))
                            ve.reciprocal(zrec[:, k:k + 1], zcol[:, k:k + 1]).then_inc(a_z.sem, 1)
                            ve.wait_ge(a_z.sem, a_z.at(n, 4 * i + k + 1))
                            ve.wait_ge(a_r.sem, a_r.at(n, 4 * i + k - 3))
                            ve.tensor_scalar(ZP[:, k, :], w("onehot")[:, bass.ds(e2 * 32 + 16 * i, 16)],
                                             zrec[:, k:k + 1], None, ALU.mult).then_inc(a_zp.sem, 1)
                ve.wait_ge(a_sum.sem, a_sum.at(b, 1))
                ve.tensor_copy(rs[0:16, :], ps[4][0:16, :]).then_inc(a_rs.sem, 1)
                ve.wait_ge(a_rd.sem, a_rd.at(b, 32))
                ve.tensor_tensor(att, vT, Rb, ALU.mult).then_inc(a_at.sem, 1)
                ve.wait_ge(a_wo.sem, a_wo.at(b, 1))
                ve.scalar_tensor_tensor(x[:, :], ps[5][:, :], w("bo"), x[:, :], ALU.add, ALU.add).then_inc(xr.sem, 1)
                ve.wait_ge(xr.sem, xr.at(b, 3))
                layer_norm(b, 3)
                ve.wait_ge(ln_dve.sem, ln_dve.at(b, 12))
                layer_norm(b, 4)
                ve.wait_ge(ln_dve.sem, ln_dve.at(b, 15))
                ve.tensor_scalar(xn[:, :], xn[:, :], w("nw"), w("nb"), ALU.mult, ALU.add).then_inc(b_xn.sem, 1)
                ve.tensor_tensor(x[:, :], x[:, :], u[:, :], ALU.add).then_inc(fin.sem, 1)
                scale = float(D) ** -0.5
                ve.wait_ge(b_mm.sem, b_mm.at(b, 2))
                project(b_mm, b_dve, 2, w("qb"), 0, qs, qsp, -scale)
                project(b_mm, b_dve, 3, w("kb"), 6, ks, ksp, 1.0)
                ve.wait_ge(b_mm.sem, b_mm.at(b, 3))
                ve.wait_ge(b_pool.sem, b_pool.at(b, 2))
                for k in range(4):
                    for g2 in range(2):
                        base = 1024 * k + 512 * g2
                        ins = ve.tensor_tensor(
                            vslots(base),
                            ps[4][:, 128 * k + 64 * g2:128 * k + 64 * g2 + 64].rearrange("a (h y) -> a h y", h=4),
                            w("vb", 64 * g2, 64 * g2 + 64).rearrange("a (h y) -> a h y", h=4), ALU.add)
                    ins.then_inc(b_v.sem, 1)
                for i in range(32):
                    ve.wait_ge(b_s.sem, b_s.at(b, i + 1))
                    ve.tensor_reduce(mq[:, i:i + 1], ps[i % 4][:, :], AX, ALU.min).then_inc(b_m.sem, 1)
                for g2 in range(2):
                    ve.wait_ge(b_pv.sem, b_pv.at(b, 16 * g2 + 16))
                    ve.reciprocal((rcp, r1)[g2][0:64, :], ps[4 + g2][64:128, :]).then_inc(b_rc.sem, 1)
                    ve.wait_ge(b_rc.sem, b_rc.at(b, g2 + 1))
                    ve.tensor_tensor(att[64 * g2:64 * g2 + 64, :], ps[4 + g2][0:64, :], (rcp, r1)[g2][0:64, :],
                                     ALU.mult).then_inc(b_at.sem, 1)
                ve.wait_ge(b_wo.sem, b_wo.at(b, 1))
                ve.wait_ge(fin.sem, fin.at(b, 1))
                ve.tensor_tensor(x[:, :], x[:, :], ps[0][:, :], ALU.add).then_inc(fin.sem, 1)
                ve.wait_ge(fin.sem, fin.at(b, 2))
                xe = x[:, :].rearrange("a (e t) -> a e t", e=NX)
                ve.tensor_tensor(xe, xe, obm[:, :].unsqueeze(2).broadcast_to([128, NX, 128]), ALU.add).then_inc(fin.sem, 1)

        @block.gpsimd
        def _(po):
            po.wait_ge(pack_in.sem, 32)
            with po.Fori(0, B) as b:
                po.wait_ge(conv.sem, conv.at(b, NT))
                hold(po)
                po.memset(P, 0.0).then_inc(bd0.sem, 1)
                po.wait_ge(tc_ok.sem, tc_ok.at(b, 1))
                hold(po)
                po.memset(LT, 0.0).then_inc(bd0.sem, 1)
                with po.Fori(0, NC) as c:
                    n = b * NC + c
                    tok = bass.ds(c * C, C)
                    po.wait_ge(bd0.sem, bd0.at(b, 2))
                    po.wait_ge(eg_dma.sem, eg_dma.at(b, 48))
                    po.wait_ge(e_ok.sem, e_ok.at(n - 1, 1))
                    hold(po)
                    po.tensor_copy(EGc.rearrange("a (q t) -> a q t", q=8), egB[:, :, tok]).then_inc(eg_cp.sem, 1)
                    po.tensor_tensor(d1.rearrange("a (q t) -> a q t", q=8),
                                     w("identc").unsqueeze(1).broadcast_to([128, 8, C]),
                                     tc[:, bass.ds(c, 1), 1, :].rearrange("a c q -> a (c q)").unsqueeze(2).broadcast_to([128, 8, C]),
                                     ALU.mult).then_inc(c_d1.sem, 1)
                    po.wait_ge(qs_mm.sem, qs_mm.at(n - 1, 1))
                    half = w("half").unsqueeze(1).unsqueeze(3).broadcast_to([128, 4, 2, C])
                    for dst, src in ((Kbd, KT), (Qbd, QT)):
                        po.tensor_tensor(dst.rearrange("a p (e t) -> a p e t", e=2),
                                         src[:, :, tok].unsqueeze(2).broadcast_to([128, 4, 2, C]), half,
                                         ALU.mult).then_inc(c_cp.sem, 1)
                    po.tensor_copy(KQc[:, :, 0, :], KT[:, :, tok]).then_inc(c_cp.sem, 1)
                    po.tensor_copy(KQc[:, :, 1, :], QT[:, :, tok]).then_inc(c_cp.sem, 1)
                    for h in range(2):
                        po.tensor_copy(Vc[:, 4 * h:4 * h + 4, :], VT[:, 4 * h:4 * h + 4, tok]).then_inc(c_cp.sem, 1)
                    po.tensor_copy(xch[:, :], xn[:, tok]).then_inc(c_cp.sem, 1)
                    po.wait_ge(lt_dve.sem, lt_dve.at(n, 2))
                    hold(po)
                    po.affine_select(out=LT, in_=LT, compare_op=ALU.not_equal, fill=1.0, base=0,
                                     pattern=[[0, 8], [-1, 128]], channel_multiplier=1).then_inc(lt_ok.sem, 1)
                po.wait_ge(gt_dve.sem, gt_dve.at(b, 18))
                for j in range(2, NE):
                    po.wait_ge(f_dve.sem, f_dve.at(b, j + 1))
                    po.wait_ge(cb_dma.sem, cb_dma.at(b, 64))
                    if j >= 5:
                        po.wait_ge(f2_mm.sem, f2_mm.at(b, j - 2))
                    po.tensor_tensor(act[j % 3], hid[j % 3], combB[:, j - 2, :], ALU.mult).then_inc(f_pool.sem, 1)
                po.wait_ge(f2_mm.sem, f2_mm.at(b, NE))
                hold(po)
                po.memset(zero[:, 0:16], 0.0).then_inc(zero_ok.sem, 1)
                po.wait_ge(zero_ok.sem, zero_ok.at(b, 1))
                hold(po)
                with po.Fori(0, H1 // 2) as e2:
                    n = b * (H1 // 2) + e2
                    for i in range(2):
                        po.wait_ge(a_dma.sem, a_dma.at(b, 12 * 16))
                        po.wait_ge(a_s.sem, a_s.at(n, 4 * i - 4))
                        hold(po)
                        po.tensor_copy(QXe[i][0:48, :].rearrange("a (g t) -> a g t", g=16),
                                       QX[0:48, :, bass.ds(e2 * 64 + 32 * i, 32)]).then_inc(a_kx.sem, 1)
                        po.tensor_copy(KXe[i][0:48, :].rearrange("a (g t) -> a g t", g=16),
                                       KX[0:48, :, bass.ds(e2 * 64 + 32 * i, 32)]).then_inc(a_kx.sem, 1)
                po.wait_ge(xr.sem, xr.at(b, 3))
                hold(po)
                po.memset(Vflat, 0.0).then_inc(b_pool.sem, 1)
                po.wait_ge(b_pool.sem, b_pool.at(b, 1))
                hold(po)
                for g2 in range(8):
                    ins = po.memset(vslots(512 * g2 + 64), 1.0)
                ins.then_inc(b_pool.sem, 1)
                po.wait_ge(b_pool.sem, b_pool.at(b, 2))
                hold(po)
                po.memset(KH[96:97, :, :], 1.0).then_inc(b_pool.sem, 1)


def _head_order():
    return [(2 * p + e) * 2 + r for e in range(2) for p in range(4) for r in range(2)]


def pack_inputs(i):
    f = np.float32

    def col(v):
        v = np.asarray(v).reshape(-1)
        return np.concatenate([v, np.zeros(128 - v.size, f)])[:, None]

    def cols(m):
        return np.ascontiguousarray(np.asarray(m).T)

    order = _head_order()
    parts = {}
    parts["wqkv"] = cols(i["L0_attn_W_qkv"])
    parts["convw"] = np.asarray(i["L0_attn_conv_w"]).reshape(NT, 128, KSZ).transpose(1, 0, 2).reshape(128, NT * KSZ)
    parts["wz"] = cols(i["L0_attn_W_z"]).reshape(128, 4, 2, 128).transpose(0, 2, 1, 3).reshape(128, 1024)
    parts["wab"] = np.concatenate([cols(i["L0_attn_W_a"])[:, order], np.zeros((128, 16), f),
                                   cols(i["L0_attn_W_b"])[:, order]], 1)
    parts["dtb"], parts["alog"] = col(np.asarray(i["L0_attn_dt_bias"])[order]), col(np.asarray(i["L0_attn_A_log"])[order])
    parts["normw"] = col(np.tile(np.asarray(i["L0_attn_norm_weight"]), 2))
    parts["wout"] = cols(i["L0_attn_W_out"]).reshape(8, 128, 128).transpose(1, 0, 2).reshape(128, 1024)
    parts["gate"] = cols(i["L0_ffn_gate_w"])
    parts["fc1"] = np.asarray(i["L0_ffn_fc1_w"]).transpose(2, 0, 1).reshape(128, E * 256)
    parts["fc1b"] = np.asarray(i["L0_ffn_fc1_b"]).reshape(E * 2, 128).T
    parts["gm"] = cols(i["L0_ffn_geglu_mult"])
    parts["fc2"] = np.asarray(i["L0_ffn_fc2_w"]).transpose(2, 0, 1).reshape(128, E * 128)
    parts["fc2b"] = np.concatenate([np.asarray(i["L0_ffn_fc2_b"]), np.zeros((128 - E, 128), f)], 0)
    parts["sfc1"] = cols(i["L0_ffn_s_fc1_w"])
    parts["sfc1b"] = np.asarray(i["L0_ffn_s_fc1_b"]).reshape(4, 128).T
    parts["sgm"] = np.asarray(i["L0_ffn_s_geglu_mult"]).reshape(2, 128).T
    parts["sfc2"] = cols(i["L0_ffn_s_fc2_w"]).reshape(2, 128, 128).transpose(1, 0, 2).reshape(128, 256)
    parts["sfc2b"] = col(i["L0_ffn_s_fc2_b"])
    for k in "qkvo":
        parts["w" + k], parts["b" + k] = np.asarray(i["L1_attn_W" + k]), col(i["L1_attn_b" + k])
        parts[k + "w"] = cols(i[f"L1_ffn_{k}_w"])
    for k in "qko":
        parts[k + "b"] = col(i[f"L1_ffn_{k}_b"])
    parts["vb"] = np.broadcast_to(np.asarray(i["L1_ffn_v_b"]), (128, 128))
    parts["nw"], parts["nb"] = col(i["L1_ffn_norm_w"]), col(i["L1_ffn_norm_b"])
    eye = np.eye(128, dtype=f)
    parts["ident"], parts["mean"] = eye, np.full((128, 128), 1.0 / 128, f)
    r, c = np.arange(128)[:, None], np.arange(128)[None, :]

    def doubling(s):
        low = (r // (2 * s) == c // (2 * s)) & (r // s == c // s + 1)
        return (eye - low).astype(f)

    parts["masks"] = np.concatenate([doubling(s) for s in LEVELS], 1)
    parts["mask1"] = doubling(1).T
    parts["identc"] = np.concatenate([np.eye(C, dtype=f)] * 2, 0)
    parts["half"] = (r // 64 == np.arange(2)[None, :]).astype(f)
    sel = np.zeros((128, 32), f)
    for e in range(2):
        for q in range(8):
            sel[8 * e + q, 16 * e + q] = 1
            sel[32 + 8 * e + q, 16 * e + 8 + q] = 1
    parts["sel"] = sel
    parts["onehot"] = np.broadcast_to(np.eye(16, dtype=f).reshape(1, 256), (128, 256))
    parts["lneps"], parts["rmseps"] = np.full((128, 1), LN_EPS, f), np.full((128, 1), RMS_EPS, f)
    parts["pads"] = np.broadcast_to(np.array([-1, -2, -3, -4, -5], f), (128, 5))
    at, n = columns()
    for name, (o, width) in at.items():
        assert parts[name].shape == (128, width), (name, parts[name].shape, width)
    return np.ascontiguousarray(np.concatenate([parts[name] for name in at], 1))


def kernel(**inputs):
    import concourse.bacc as bacc
    from concourse.bass_utils import run_bass_kernel_spmd

    nc = bacc.Bacc("TRN2", target_bir_lowering=False, num_devices=1)
    arrays = {
        "x_channels": np.ascontiguousarray(np.asarray(inputs["L0_attn_hidden_states"]).transpose(0, 2, 1)),
        "weights": pack_inputs(inputs),
    }
    args = [nc.dram_tensor(k, a.shape, F32, kind="ExternalInput").ap() for k, a in arrays.items()]
    args.append(nc.dram_tensor("y_channels", (B, D, S), F32, kind="ExternalOutput").ap())
    build(nc, *args)
    r = run_bass_kernel_spmd(nc, [arrays], core_ids=[0])
    return np.ascontiguousarray(r.results[0]["y_channels"].transpose(0, 2, 1))
```

```python
from contextlib import ExitStack

import numpy as np

import concourse.bass as bass
from concourse import mybir

F32 = mybir.dt.float32
BF16 = mybir.dt.bfloat16
ALU = mybir.AluOpType
ACT = mybir.ActivationFunctionType
AX = mybir.AxisListType.X

B, S, D = 8, 512, 128
C = 64
NC = S // C
NT = 16
KSZ = 4
E, TOPK = 15, 3
NE = E + 2
H1 = 16
H2 = 8
NX = 4
LN_EPS, RMS_EPS = 1e-5, 1e-6
SETUP = 18
Q_PARTS, K_PARTS = (0, 0, 1, 0, 1, 2), (0, 1, 0, 2, 1, 0)
BASE = 8
LEVELS = [8, 16, 32]


def columns():
    widths = dict(
        wqkv=NT * 128, convw=NT * KSZ, wz=1024, wab=48, dtb=1, alog=1, normw=1, wout=8 * 128,
        gate=E, fc1=E * 256, fc1b=E * 2, gm=E, fc2=E * 128, fc2b=128, sfc1=512, sfc1b=4, sgm=2,
        sfc2=256, sfc2b=1, wq=128, wk=128, wv=128, wo=128, bq=1, bk=1, bv=1, bo=1,
        nw=1, nb=1, qw=128, kw=128, vw=128, ow=128, qb=1, kb=1, vb=128, ob=1,
        ident=128, mean=128, masks=128 * len(LEVELS), same8=128, blk8=8, blk16=16, diag8=64, delta8=8, identc=64, half=2, sel=32, onehot=256,
        lneps=1, rmseps=1, pads=5)
    at, n = {}, 0
    for name, w in widths.items():
        at[name] = (n, w)
        n += w
    return at, n


def build(nc, x_in, pack, out):
    at, npack = columns()
    with ExitStack() as ctx:
        def sb(name, shape, dt=F32):
            return ctx.enter_context(nc.sbuf_tensor(name, shape, dt))

        class Signal:

            def __init__(self, name, per, credit=0):
                self.sem, self.per, self.credit = ctx.enter_context(nc.semaphore(name)), per, credit

            def at(self, i, k):
                return i * self.per + (k + self.credit)

        W = sb("W", [128, npack])

        def w(name, lo=0, hi=None, p0=0, p1=128):
            o, n = at[name]
            return W[p0:p1, o + lo:o + (n if hi is None else hi)]

        x = sb("x", [128, S])
        xn = sb("xn", [128, S])
        xc = sb("xc", [128, S])
        sq = sb("sq", [128, S])
        sd = sb("sd", [128, S])
        u = sb("u", [128, S])
        expA = sb("expA", [128, 1])
        owm = sb("owm", [128, NX, 128])
        obm = sb("obm", [128, NX])
        gl = sb("gl", [16, NC])
        glB = sb("glB", [128, 8, NC])
        tc = sb("tc", [128, NC, 2, 8])
        var = sb("var", [128, NC, 8])
        rstd = sb("rstd", [128, NC, 8])
        mq = sb("mq", [128, 32])
        mrow = sb("mrow", [32, 128], BF16)

        A = sb("arenaA", [128, 16384])
        KT = A[:, 0:2048].rearrange("a (p t) -> a p t", p=4)
        QT = A[:, 2048:4096].rearrange("a (p t) -> a p t", p=4)
        VT = A[:, 4096:8192].rearrange("a (k t) -> a k t", k=8)
        egB = A[:, 8192:12288].rearrange("a (q t) -> a q t", q=8)
        Hall = A[:, 12288:16384].rearrange("a (c n) -> a c n", c=NC)
        oT = A[:, 0:4096].rearrange("a (k t) -> a k t", k=8)
        combB = A[:, 0:E * S].rearrange("a (j t) -> a j t", j=E)
        QX = A[:, 0:4096].bitcast(BF16).rearrange("a (g t) -> a g t", g=16)
        KX = A[:, 4096:8192].bitcast(BF16).rearrange("a (g t) -> a g t", g=16)
        Rb = A[:, 8192:8704]
        QH = A[:, 0:2048].bitcast(BF16).rearrange("a (h t) -> a h t", h=8)
        KH = A[:, 2048:4096].bitcast(BF16).rearrange("a (h t) -> a h t", h=8)
        Vflat = A[:, 4096:8192]

        def vslots(base):
            return A[:, 4096 + base:4096 + base + 576].rearrange("a (h z) -> a h z", z=144)[:, :, 0:16]

        Vp = A[:, 4096:8192].rearrange("a (k h c) -> a k h c", k=4, h=8)

        Bn = sb("arenaB", [128, 35 * 512])
        slot = [0]

        def take(n):
            slot[0] += n
            return Bn[:, 512 * (slot[0] - n):512 * slot[0]]

        Kbd, Qbd, Ktok = ([take(1).rearrange("a (p t) -> a p t", p=4) for _ in range(2)] for _ in range(3))
        Vtok, sz, Ec = ([take(1) for _ in range(2)] for _ in range(3))
        P = [take(2).rearrange("a (q t) -> a q t", q=8) for _ in range(2)]
        KQc = take(1).rearrange("a (p q t) -> a p q t", p=4, q=2)
        Vc = take(1).rearrange("a (k t) -> a k t", k=8)
        LT = take(2).rearrange("a (q t) -> a q t", q=8)
        d1, EGc, R, Y, Yd, Ot, hq, St, Lc = (take(1) for _ in range(9))
        rhs8 = hq
        M8 = Yd
        xch = sb("xch", [128, C])
        An = sb("An", [128, 8, BASE, BASE + 1])
        X8 = sb("X8", [128, 8, BASE + 1])
        Xd = sb("Xd", [128, 8, BASE])
        prod = sb("prod", [128, 8, BASE])
        tail = slot[0]
        T = take(2).rearrange("a (q t) -> a q t", q=8)
        Z = take(2).rearrange("a (q t) -> a q t", q=8)
        Wm = take(2).rearrange("a (q t) -> a q t", q=8)
        nslots = slot[0]
        slot[0] = tail
        ta, tna, tw, tu, tl, td = (take(1) for _ in range(6))
        Ot2 = Lc
        ybuf = [k.rearrange("a p t -> a (p t)") for k in Kbd]
        RT = LT[:, 0:4].rearrange("a q t -> a (q t)")
        EG = LT[:, 4:8].rearrange("a q t -> a (q t)")
        EGm, D1 = R, Y
        assert nslots <= 35, nslots
        slot[0] = 0
        glu = [take(1) for _ in range(3)]
        hid = [take(1) for _ in range(3)]
        act = [take(1) for _ in range(3)]
        combT = take(1)
        lg, scp, rep, pk = (take(1) for _ in range(4))
        lg, scp, rep, pk = (t[:, 0:80].rearrange("a (t e) -> a t e", t=4) for t in (lg, scp, rep, pk))
        small = take(1)
        m8 = small[:, 0:32].rearrange("a (t e) -> a t e", t=4)
        tr8 = small[:, 32:64].rearrange("a (t e) -> a t e", t=4)
        mx4, sm4, rc4 = small[:, 64:68], small[:, 68:72], small[:, 72:76]
        slot[0] = 0
        qs, ks, vT, r1, att = (take(1) for _ in range(5))
        qsp = [take(1)[:, 0:256].bitcast(BF16) for _ in range(3)]
        ksp = [take(1)[:, 0:256].bitcast(BF16) for _ in range(3)]
        Ering = [take(1) for _ in range(4)]
        rs = take(1)
        mcol = take(1)
        zcol, zrec = mcol[:, 16:20], mcol[:, 32:36]
        ZP = take(1)[:, 0:64].rearrange("a (k e) -> a k e", k=4)
        zero = take(1)
        rcp = take(1)
        QXe = [take(1)[:, 0:256].bitcast(BF16) for _ in range(2)]
        KXe = [take(1)[:, 0:256].bitcast(BF16) for _ in range(2)]

        ps = [ctx.enter_context(nc.psum_tensor(f"bank{i}", [128, 512], F32)) for i in range(8)]

        def pair(i, q):
            return ps[i + q // 4][:, 128 * (q % 4):128 * (q % 4) + 128]

        eg_d = nc.dram_tensor("eg_scratch", [16, S], F32, kind="Internal").ap()
        gl_d = nc.dram_tensor("gl_scratch", [16, NC], F32, kind="Internal").ap()
        cb_d = nc.dram_tensor("comb_scratch", [E, S], F32, kind="Internal").ap()
        part_d = nc.dram_tensor("parts_scratch", [6, 128, S], BF16, kind="Internal").ap()
        max_d = nc.dram_tensor("max_scratch", [32, 128], BF16, kind="Internal").ap()
        r_d = nc.dram_tensor("rowsum_scratch", [16, S], F32, kind="Internal").ap()

        pack_in = Signal("pack_in", 0)
        setup = Signal("setup", 0)
        x_in_s = Signal("x_loaded", 16)
        y_out = Signal("y_stored", 16)
        NLN = 5
        ln_pe, ln_dve, ln_act = Signal("ln_pe", 2 * NLN), Signal("ln_dve", 3 * NLN), Signal("ln_act", 2 * NLN)
        qkv_mm = Signal("qkv_mm", NT)
        tap0 = Signal("conv_tap0", NT)
        taps = Signal("conv_taps", 3 * NT)
        conv = Signal("conv_done", NT)
        ab_mm = Signal("ab_mm", 1)
        g_act, g_dve = Signal("gates_act", 4), Signal("gates_dve", 17)
        gamma_ok = Signal("gamma_ready", 1)
        gl_dma, eg_dma = Signal("gl_dma", 48), Signal("eg_dma", 48)
        tc_mm, tc_ok = Signal("tokcols_mm", 1), Signal("tokcols_ready", 1)
        s0, bd0 = Signal("state_zero", 1), Signal("blocks_zeroed", 2)
        c_cp = Signal("chunk_copied", 7)
        eg_cp = Signal("chunk_decays_copied", 1)
        c_d1 = Signal("chunk_beta_diag", 1)
        kq_mm, kt_mm, vt_mm, z_mm = (Signal(n, 1, 1) for n in ("kq_mm", "ktok_mm", "vtok_mm", "z_mm"))
        e_ok = Signal("decay_ready", 1, 1)
        lc_ok, p_dve = Signal("l_compact", 1), Signal("p_ready", 2)
        lt_ok = Signal("lt_ready", 2)
        m8_ok = Signal("l_blocks", 3)
        a8_mm, a8_ev = Signal("l_blocks_spread", 1), Signal("l_blocks_ready", 1)
        x8_ok, z8_ok = Signal("substitution", 2 * (BASE - 1)), Signal("z8_ready", 1)
        kv_ev = Signal("ktok_vtok_ready", 2)
        sz_ok = Signal("silu_z_ready", 1)
        t8_mm = Signal("t8_mm", 2)
        x_mm, w_ev = Signal("level_x_mm", 6, 6), Signal("level_w_ready", 6)
        tz_mm, t_ev, z_ev = Signal("level_tz_mm", 6), Signal("level_t_ready", 6), Signal("level_z_ready", 6, 6)
        ks_mm, qs_mm = Signal("ks_mm", 1), Signal("qs_mm", 1, 2)
        r_dve = Signal("r_dve", 2)
        y_mm, y_ev, yd_ok = Signal("y_mm", 2), Signal("y_ready", 2), Signal("yd_ready", 1)
        o_mm, o_dve = Signal("o_mm", 2), Signal("o_dve", 4, 4)
        s_mm, s_dve = Signal("state_mm", 1), Signal("state_dve", 2, 2)
        hq_ok, var_ok = Signal("h_squared", NC), Signal("var_ready", NC)
        n_sd, n_rs = Signal("rms_sqrt", 1), Signal("rms_recip", 1)
        hn_ok, ot_mm, ot_ev = Signal("h_normed", NC), Signal("o_turned", NC), Signal("o_turned_ready", NC)
        op_mm = Signal("out_proj", 1)
        xr = Signal("x_updated", 3)
        gt_mm, gt_act, gt_dve = Signal("gate_mm", 1), Signal("gate_exp", 1), Signal("gate_dve", 18)
        ct_mm = Signal("comb_turned", 1)
        cb_dma = Signal("comb_dma", 64)
        f1_mm, f_act, f_dve = (Signal(n, NE) for n in ("fc1_mm", "gelu_ready", "hidden_ready"))
        f_pool = Signal("weighted", E)
        f2_mm = Signal("fc2_mm", NE)
        a_mm, a_dve, a_act = Signal("attn_proj_mm", 3), Signal("attn_split", 12), Signal("attn_v", 1)
        a_wr, b_wr = Signal("a_parts_stored", 96), Signal("b_parts_stored", 96)
        a_dma = Signal("attn_spread", 12 * 16)
        a_kx = Signal("a_qk_copied", 4)
        a_s, a_m, a_e = Signal("a_scores", 8, 8), Signal("a_min", 8), Signal("a_exp", 8, 4)
        a_z, a_zp, a_r = Signal("a_recip", 8), Signal("a_cols", 8), Signal("a_rowsum", 8, 4)
        a_sum = Signal("a_sum_mm", 1)
        a_rs, a_rd, a_at, a_wo = Signal("a_sum_ready", 1), Signal("a_sum_dma", 32), Signal("a_out", 1), Signal("a_wo", 1)
        b_xn = Signal("nested_affine", 1)
        b_mm, b_dve, b_pool, b_v = Signal("b_proj_mm", 3), Signal("b_split", 12), Signal("b_vpad", 3), Signal("b_v_ready", 4)
        b_dma = Signal("b_spread", 12 * 16)
        b_s, b_m = Signal("b_scores", 32), Signal("b_min", 32)
        b_tr, b_row, b_rdma = Signal("b_max_turned", 1), Signal("b_max_row", 1), Signal("b_max_dma", 32)
        b_st, b_e, b_pv = Signal("b_scores_t", 32), Signal("b_exp", 32), Signal("b_pv", 32)
        b_rc, b_at = Signal("b_recip", 2), Signal("b_out", 2)
        b_wo = Signal("b_wo", 1)
        fin = Signal("final", 3)
        zero_ok = Signal("zero_ready", 1)
        passed = Signal("passed", 0)

        block = ctx.enter_context(nc.Block())

        def hold(eng):
            eng.sem_inc(passed.sem, 1)

        @block.sync
        def _(sp):
            def spread(b, split, wrote, sent, q, k, width):
                for t, (dst, parts, order) in enumerate(((q, qsp, Q_PARTS), (k, ksp, K_PARTS))):
                    for part in range(3):
                        sp.wait_ge(split.sem, split.at(b, 6 * t + 2 * part + 2))
                        sp.dma_start(part_d[3 * t + part, :, :], parts[part]).then_inc(wrote.sem, 16)
                        sp.wait_ge(wrote.sem, wrote.at(b, 16 * (3 * t + part + 1)))
                        src = part_d[3 * t + part, :, :].rearrange("(g x) t -> x g t", x=width)
                        for i in range(6):
                            if order[i] == part:
                                sp.dma_start(dst[width * i:width * i + width, :, :], src).then_inc(sent.sem, 16)

            half = npack // 2
            sp.dma_start(W[:, 0:half], pack[:, 0:half]).then_inc(pack_in.sem, 16)
            sp.dma_start(W[:, half:npack], pack[:, half:npack]).then_inc(pack_in.sem, 16)
            with sp.Fori(0, B) as b:
                sp.dma_start(x[:, :], x_in[b, :, :]).then_inc(x_in_s.sem, 16)
                sp.wait_ge(g_dve.sem, g_dve.at(b, 16))
                sp.dma_start(eg_d, EGm[0:16, :]).then_inc(eg_dma.sem, 16)
                sp.wait_ge(g_dve.sem, g_dve.at(b, 17))
                sp.dma_start(gl_d, gl[:, :]).then_inc(gl_dma.sem, 16)
                sp.wait_ge(eg_dma.sem, eg_dma.at(b, 16))
                for e in range(2):
                    sp.dma_start(egB[64 * e:64 * e + 64, :, :],
                                 eg_d[8 * e:8 * e + 8, :].unsqueeze(0).broadcast_to([64, 8, S])
                                 ).then_inc(eg_dma.sem, 16)
                sp.wait_ge(gl_dma.sem, gl_dma.at(b, 16))
                for e in range(2):
                    sp.dma_start(glB[64 * e:64 * e + 64, :, :],
                                 gl_d[8 * e:8 * e + 8, :].unsqueeze(0).broadcast_to([64, 8, NC])
                                 ).then_inc(gl_dma.sem, 16)
                sp.wait_ge(gt_dve.sem, gt_dve.at(b, 18))
                sp.dma_start(cb_d, combT[0:E, :]).then_inc(cb_dma.sem, 16)
                sp.wait_ge(cb_dma.sem, cb_dma.at(b, 16))
                for k in range(3):
                    sp.dma_start(combB[:, 5 * k:5 * k + 5, :],
                                 cb_d[5 * k:5 * k + 5, :].unsqueeze(0).broadcast_to([128, 5, S])
                                 ).then_inc(cb_dma.sem, 16)
                sp.wait_ge(f2_mm.sem, f2_mm.at(b, NE))
                spread(b, a_dve, a_wr, a_dma, QX[0:48, :, :], KX[0:48, :, :], 8)
                sp.wait_ge(a_rs.sem, a_rs.at(b, 1))
                sp.dma_start(r_d.rearrange("g (e t) -> e g t", e=16),
                             rs[0:16, :].rearrange("a (g t) -> a g t", g=16)).then_inc(a_rd.sem, 16)
                sp.wait_ge(a_rd.sem, a_rd.at(b, 16))
                sp.dma_start(Rb, r_d.unsqueeze(1).broadcast_to([16, 8, S])).then_inc(a_rd.sem, 16)
                spread(b, b_dve, b_wr, b_dma, QH[0:96, :, :], KH[0:96, :, :], 16)
                sp.wait_ge(b_row.sem, b_row.at(b, 1))
                sp.dma_start(max_d, mrow[:, :]).then_inc(b_rdma.sem, 16)
                sp.wait_ge(b_rdma.sem, b_rdma.at(b, 16))
                sp.dma_start(QH[96:97, :, :].rearrange("a h t -> a (h t)"),
                             max_d.rearrange("q t -> (q t)").unsqueeze(0)).then_inc(b_rdma.sem, 16)
                sp.wait_ge(fin.sem, fin.at(b, 3))
                sp.dma_start(out[b, :, :], x[:, :]).then_inc(y_out.sem, 16)
                sp.wait_ge(y_out.sem, y_out.at(b, 16))
                hold(sp)

        @block.tensor
        def _(pe):
            def layer_norm(b, i):
                pe.matmul(ps[0][:, :], w("mean"), x[:, :] if i < 4 else u[:, :], start=True, stop=True).then_inc(ln_pe.sem, 1)
                pe.wait_ge(ln_act.sem, ln_act.at(b, 2 * i + 1))
                pe.matmul(ps[1][:, :], w("mean"), sq[:, :], start=True, stop=True).then_inc(ln_pe.sem, 1)

            pe.wait_ge(pack_in.sem, 32)
            pe.wait_ge(setup.sem, SETUP)
            for sig in (qs_mm, kq_mm, kt_mm, vt_mm, z_mm, x_mm):
                pe.sem_inc(sig.sem, sig.credit)
            pe.sem_inc(a_r.sem, 4)
            pe.sem_inc(a_s.sem, 8)
            with pe.Fori(0, B) as b:
                pe.wait_ge(x_in_s.sem, x_in_s.at(b, 16))
                layer_norm(b, 0)
                pe.wait_ge(ln_dve.sem, ln_dve.at(b, 3))
                pe.matmul(ps[6][0:48, :], w("wab"), xn[:, :], start=True, stop=True).then_inc(ab_mm.sem, 1)
                for t in range(NT):
                    if t >= 4:
                        pe.wait_ge(taps.sem, taps.at(b, 3 * (t - 3)))
                    pe.matmul(ps[2 + t % 4][:, :], w("wqkv", 128 * t, 128 * t + 128), xn[:, :],
                              start=True, stop=True).then_inc(qkv_mm.sem, 1)
                    if t == 12:
                        pe.wait_ge(g_dve.sem, g_dve.at(b, 17))
                        for c in range(NC):
                            for e in range(2):
                                mm = pe.matmul(ps[7][64 * e:64 * e + 64, 16 * c:16 * c + 16],
                                               RT[:, C * c:C * c + C], w("sel", 16 * e, 16 * e + 16),
                                               start=True, stop=True)
                        mm.then_inc(tc_mm.sem, 1)
                def front_kq(n, par):
                    pe.wait_ge(c_cp.sem, c_cp.at(n, 7))
                    pe.wait_ge(z_ev.sem, z_ev.at(n - 1, 6))
                    for p in range(4):
                        mm = pe.matmul(ps[0][:, 128 * p:128 * p + 128], Kbd[par][:, p, :],
                                       KQc[:, p, :, :], start=True, stop=True)
                    mm.then_inc(kq_mm.sem, 1)
                    for p in range(4):
                        mm = pe.transpose(ps[1][:, 128 * p:128 * p + 128], Kbd[par][:, p, :], w("ident"))
                    mm.then_inc(kt_mm.sem, 1)

                def front_zv(n):
                    pe.wait_ge(o_dve.sem, o_dve.at(n - 1, 1))
                    for e in range(2):
                        mm = pe.matmul(ps[3][64 * e:64 * e + 64, :], xch[:, :], w("wz", 512 * e, 512 * e + 512),
                                       start=True, stop=True)
                    mm.then_inc(z_mm.sem, 1)
                    pe.wait_ge(kv_ev.sem, kv_ev.at(n, 1))
                    for p in range(4):
                        mm = pe.transpose(ps[1][:, 128 * p:128 * p + 128], Vc[:, 2 * p:2 * p + 2, :], w("ident"))
                    mm.then_inc(vt_mm.sem, 1)

                def spread_blocks(n):
                    pe.wait_ge(m8_ok.sem, m8_ok.at(n, 3))
                    pe.matmul(ps[4][:, :], w("same8"), rhs8, start=True, stop=True).then_inc(a8_mm.sem, 1)

                def inverse(n):
                    pe.wait_ge(z8_ok.sem, z8_ok.at(n, 1))
                    for q in range(8):
                        mm = pe.transpose(pair(4, q), Z[:, q, :], w("ident"))
                        if q % 4 == 3:
                            mm.then_inc(t8_mm.sem, 1)
                    pe.wait_ge(lt_ok.sem, lt_ok.at(n, 2))
                    for k, s in enumerate(LEVELS):
                        for h in range(2):
                            pe.wait_ge(t_ev.sem, t_ev.at(n, 2 * k + h + 1))
                            for q in range(4 * h, 4 * h + 4):
                                mm = pe.matmul(pair(4, q), LT[:, q, :], T[:, q, :], start=True, stop=True)
                            mm.then_inc(x_mm.sem, 1)
                        for h in range(2):
                            pe.wait_ge(w_ev.sem, w_ev.at(n, 2 * k + h + 1))
                            if k == 0:
                                pe.wait_ge(p_dve.sem, p_dve.at(n, 2))
                                pe.wait_ge(kv_ev.sem, kv_ev.at(n, 2))
                                pe.wait_ge(o_dve.sem, o_dve.at(n - 1, 3))
                            else:
                                pe.wait_ge(z_ev.sem, z_ev.at(n, 2 * k + h - 1))
                            if s < LEVELS[-1]:
                                for q in range(4 * h, 4 * h + 4):
                                    pe.matmul(pair(6, q), Z[:, q, :], Wm[:, q, :], start=True, stop=True)
                            for q in range(4 * h, 4 * h + 4):
                                mm = pe.matmul(pair(0, q), Wm[:, q, :], Z[:, q, :], start=True, stop=True)
                            mm.then_inc(tz_mm.sem, 1)

                def state_in(n, par):
                    pe.wait_ge(s_dve.sem, s_dve.at(n - 1, 2))
                    pe.wait_ge(s0.sem, s0.at(b, 1))
                    for p in range(4):
                        mm = pe.matmul(ps[2][:, 128 * p:128 * p + 128], Kbd[par][:, p, :],
                                       St[:, 128 * p:128 * p + 128], start=True, stop=True)
                    mm.then_inc(ks_mm.sem, 1)
                    pe.wait_ge(sz_ok.sem, sz_ok.at(n, 1))
                    for p in range(4):
                        mm = pe.matmul(ps[3][:, 128 * p:128 * p + 128], Qbd[par][:, p, :],
                                       St[:, 128 * p:128 * p + 128], start=True, stop=True)
                    mm.then_inc(qs_mm.sem, 1)

                def solve(n):
                    pe.wait_ge(r_dve.sem, r_dve.at(n, 2))
                    pe.wait_ge(z_ev.sem, z_ev.at(n, 6))
                    for q in range(8):
                        mm = pe.matmul(pair(4, q), Z[:, q, :], R[:, 128 * (q // 2):128 * (q // 2) + 128],
                                       start=True, stop=True)
                        if q % 4 == 3:
                            mm.then_inc(y_mm.sem, 1)

                def outputs(n, par):
                    pe.wait_ge(y_ev.sem, y_ev.at(n, 2))
                    for q in range(8):
                        mm = pe.matmul(pair(6, q), P[par][:, q, :], Y[:, 128 * (q // 2):128 * (q // 2) + 128],
                                       start=True, stop=True)
                        if q % 4 == 3:
                            mm.then_inc(o_mm.sem, 1)
                    pe.wait_ge(yd_ok.sem, yd_ok.at(n, 1))
                    for p in range(4):
                        mm = pe.matmul(ps[2][:, 128 * p:128 * p + 128], Ktok[par][:, p, :],
                                       Yd[:, 128 * p:128 * p + 128], start=True, stop=True)
                    mm.then_inc(s_mm.sem, 1)

                def step(n, par):
                    state_in(n, par)
                    front_kq(n + 1, 1 - par)
                    solve(n)
                    front_zv(n + 1)
                    pe.wait_ge(y_ev.sem, y_ev.at(n, 2))
                    spread_blocks(n + 1)
                    outputs(n, par)
                    inverse(n + 1)

                n0 = b * NC
                front_kq(n0, 0)
                front_zv(n0)
                pe.wait_ge(tc_ok.sem, tc_ok.at(b, 1))
                spread_blocks(n0)
                inverse(n0)
                with pe.Fori(0, NC // 2 - 1) as c2:
                    for par in range(2):
                        step(n0 + c2 * 2 + par, par)
                step(n0 + (NC - 2), 0)
                state_in(n0 + (NC - 1), 1)
                solve(n0 + (NC - 1))
                outputs(n0 + (NC - 1), 1)
                for c in range(NC):
                    pe.wait_ge(hn_ok.sem, hn_ok.at(b, c + 1))
                    if c >= 2:
                        pe.wait_ge(ot_ev.sem, ot_ev.at(b, c - 1))
                    for p in range(4):
                        mm = pe.transpose(ps[2 + c % 2][:, 128 * p:128 * p + 128], Hall[:, c, 128 * p:128 * p + 128],
                                          w("ident"))
                    mm.then_inc(ot_mm.sem, 1)
                pe.wait_ge(ot_ev.sem, ot_ev.at(b, NC))
                for k in range(8):
                    mm = pe.matmul(ps[4][:, :], w("wout", 128 * k, 128 * k + 128), oT[:, k, :],
                                   start=(k == 0), stop=(k == 7))
                mm.then_inc(op_mm.sem, 1)
                pe.wait_ge(xr.sem, xr.at(b, 1))
                layer_norm(b, 1)
                pe.wait_ge(ln_dve.sem, ln_dve.at(b, 6))
                for t in range(4):
                    mm = pe.matmul(ps[6][:, 16 * t:16 * t + E], xn[:, 128 * t:128 * t + 128], w("gate"),
                                   start=True, stop=True)
                mm.then_inc(gt_mm.sem, 1)

                def fc1(j):
                    k = j % 3
                    if j >= 3:
                        pe.wait_ge(f_act.sem, f_act.at(b, j - 2))
                        pe.wait_ge(f_dve.sem, f_dve.at(b, j - 2))
                    if j < 2:
                        wx, wg = w("sfc1", 128 * j, 128 * j + 128), w("sfc1", 256 + 128 * j, 384 + 128 * j)
                    else:
                        o = 256 * (j - 2)
                        wx, wg = w("fc1", o, o + 128), w("fc1", o + 128, o + 256)
                    pe.matmul(ps[2 * k][:, :], wx, xn[:, :], start=True, stop=True)
                    pe.matmul(ps[2 * k + 1][:, :], wg, xn[:, :], start=True, stop=True).then_inc(f1_mm.sem, 1)

                def fc2(j):
                    if j < 2:
                        pe.wait_ge(f_dve.sem, f_dve.at(b, j + 1))
                    else:
                        pe.wait_ge(f_pool.sem, f_pool.at(b, j - 1))
                    lhs = w("sfc2", 128 * j, 128 * j + 128) if j < 2 else w("fc2", 128 * (j - 2), 128 * (j - 1))
                    pe.matmul(ps[7][:, :], lhs, (hid if j < 2 else act)[j % 3], start=(j == 0), stop=(j == NE - 1)).then_inc(f2_mm.sem, 1)

                fc1(0)
                fc1(1)
                fc2(0)
                fc1(2)
                fc2(1)
                pe.wait_ge(gt_dve.sem, gt_dve.at(b, 17))
                for t in range(4):
                    mm = pe.transpose(ps[6][0:E, 128 * t:128 * t + 128], lg[:, t, 0:E], w("ident"))
                mm.then_inc(ct_mm.sem, 1)
                pe.wait_ge(gt_dve.sem, gt_dve.at(b, 18))
                pe.matmul(ps[7][:, :], w("fc2b", p1=E), combT[0:E, :], start=False, stop=False)
                for j in range(3, NE):
                    fc1(j)
                    fc2(j - 1)
                fc2(NE - 1)
                pe.wait_ge(xr.sem, xr.at(b, 2))
                layer_norm(b, 2)
                pe.wait_ge(ln_dve.sem, ln_dve.at(b, 9))
                for k, name in enumerate(("wq", "wk", "wv")):
                    pe.matmul(ps[2 + k][:, :], w(name), xn[:, :], start=True, stop=True).then_inc(a_mm.sem, 1)
                pe.wait_ge(a_dma.sem, a_dma.at(b, 12 * 16))
                pe.wait_ge(a_dve.sem, a_dve.at(b, 12))
                pe.wait_ge(a_act.sem, a_act.at(b, 1))
                pe.wait_ge(zero_ok.sem, zero_ok.at(b, 1))
                pe.matmul(ps[4][0:16, :], zero[:, 0:16], xn[:, :], start=True, stop=False, skip_group_check=True)
                with pe.Fori(0, H1 // 2) as e2:
                    n = b * (H1 // 2) + e2
                    for i in range(2):
                        pe.wait_ge(a_kx.sem, a_kx.at(n, 2 * i + 2))
                        for k in range(4):
                            pe.wait_ge(a_e.sem, a_e.at(n, 4 * i + k - 3))
                            pe.matmul(ps[k][:, :], KXe[i][0:48, 128 * k:128 * k + 128],
                                      QXe[i][0:48, :], start=True, stop=True).then_inc(a_s.sem, 1)
                        for k in range(4):
                            pe.wait_ge(a_e.sem, a_e.at(n, 4 * i + k + 1))
                            pe.wait_ge(a_zp.sem, a_zp.at(n, 4 * i + k + 1))
                            pe.matmul(ps[4][0:16, :], ZP[:, k, :], Ering[k], start=False, stop=False,
                                      skip_group_check=True).then_inc(a_r.sem, 1)
                pe.matmul(ps[4][0:16, :], zero[:, 0:16], xn[:, :], start=False, stop=True,
                          skip_group_check=True).then_inc(a_sum.sem, 1)
                pe.wait_ge(a_at.sem, a_at.at(b, 1))
                pe.matmul(ps[5][:, :], w("wo"), att, start=True, stop=True).then_inc(a_wo.sem, 1)
                pe.wait_ge(xr.sem, xr.at(b, 3))
                layer_norm(b, 3)
                pe.wait_ge(ln_dve.sem, ln_dve.at(b, 12))
                layer_norm(b, 4)
                pe.wait_ge(b_xn.sem, b_xn.at(b, 1))
                for k, name in enumerate(("qw", "kw")):
                    for e in range(NX):
                        m = D >> e
                        mm = pe.matmul(ps[2 + k][:, 128 * e:128 * e + 128], w(name, p1=m),
                                       xn[0:m, 128 * e:128 * e + 128], start=True, stop=True)
                    mm.then_inc(b_mm.sem, 1)
                for e in range(NX):
                    m = D >> e
                    mm = pe.matmul(ps[4][:, 128 * e:128 * e + 128], xn[0:m, 128 * e:128 * e + 128],
                                   w("vw", p1=m), start=True, stop=True)
                mm.then_inc(b_mm.sem, 1)
                pe.wait_ge(b_dma.sem, b_dma.at(b, 12 * 16))
                pe.wait_ge(b_dve.sem, b_dve.at(b, 12))
                pe.wait_ge(b_v.sem, b_v.at(b, 4))
                for i in range(32):
                    h, q = i // 4, i % 4
                    if i >= 4:
                        pe.wait_ge(b_m.sem, b_m.at(b, i - 3))
                    pe.matmul(ps[i % 4][:, :], QH[0:96, h, 128 * q:128 * q + 128], KH[0:96, h, :],
                              start=True, stop=True).then_inc(b_s.sem, 1)
                pe.wait_ge(b_m.sem, b_m.at(b, 32))
                pe.transpose(ps[7][0:32, 0:128], mq[:, :], w("ident")).then_inc(b_tr.sem, 1)
                pe.wait_ge(b_rdma.sem, b_rdma.at(b, 32))
                pe.wait_ge(b_pool.sem, b_pool.at(b, 3))

                def pv(i):
                    h, k = i // 4, i % 4
                    pe.wait_ge(b_e.sem, b_e.at(b, i + 1))
                    pe.matmul(ps[4 + h // 4][:, :], Vp[:, k, h, :], Ering[i % 4], start=(i % 16 == 0),
                              stop=(i % 16 == 15)).then_inc(b_pv.sem, 1)

                for i in range(32):
                    h, k = i // 4, i % 4
                    if i >= 4:
                        pe.wait_ge(b_e.sem, b_e.at(b, i - 3))
                    pe.matmul(ps[i % 4][:, :], KH[0:97, h, 128 * k:128 * k + 128], QH[0:97, h, :],
                              start=True, stop=True).then_inc(b_st.sem, 1)
                    if i >= 2:
                        pv(i - 2)
                pv(30)
                pv(31)
                pe.wait_ge(b_at.sem, b_at.at(b, 2))
                for e in range(NX):
                    m = D >> e
                    mm = pe.matmul(ps[0][:, 128 * e:128 * e + 128], owm[0:m, e, :], att[0:m, 128 * e:128 * e + 128],
                                   start=True, stop=True)
                mm.then_inc(b_wo.sem, 1)

        @block.scalar
        def _(sc):
            def layer_norm(b, i):
                sc.wait_ge(ln_dve.sem, ln_dve.at(b, 3 * i + 1))
                sc.activation(sq[:, :], xc[:, :], ACT.Square).then_inc(ln_act.sem, 1)
                sc.wait_ge(ln_pe.sem, ln_pe.at(b, 2 * i + 2))
                sc.activation(sd[:, :], ps[1][:, :], ACT.Sqrt, bias=w("lneps")).then_inc(ln_act.sem, 1)

            sc.wait_ge(pack_in.sem, 32)
            sc.wait_ge(setup.sem, SETUP - 1)
            sc.activation(expA[:, :], expA[:, :], ACT.Exp).then_inc(setup.sem, 1)
            sc.wait_ge(setup.sem, SETUP)
            sc.sem_inc(a_e.sem, 4)
            sc.sem_inc(z_ev.sem, 6)
            with sc.Fori(0, B) as b:
                layer_norm(b, 0)

                def first_tap(t):
                    sc.wait_ge(qkv_mm.sem, qkv_mm.at(b, t + 1))
                    if t >= 2:
                        sc.wait_ge(conv.sem, conv.at(b, t - 1))
                    sc.activation(ybuf[t % 2], ps[2 + t % 4][:, :], ACT.Identity,
                                  scale=w("convw", KSZ * t + 3, KSZ * t + 4)).then_inc(tap0.sem, 1)

                sc.wait_ge(ab_mm.sem, ab_mm.at(b, 1))
                sc.activation(td[32:48, :], ps[6][32:48, :], ACT.Exp, scale=-1.0).then_inc(g_act.sem, 1)
                first_tap(0)
                sc.wait_ge(g_dve.sem, g_dve.at(b, 5))
                sc.activation(tw[0:16, :], tna[0:16, :], ACT.Exp, scale=-1.0).then_inc(g_act.sem, 1)
                sc.wait_ge(g_dve.sem, g_dve.at(b, 6))
                sc.activation(tl[0:16, :], tu[0:16, :], ACT.Ln).then_inc(g_act.sem, 1)
                for t in range(NT):
                    if t + 1 < NT:
                        first_tap(t + 1)
                    if t == 4:
                        sc.wait_ge(g_dve.sem, g_dve.at(b, 12))
                        sc.activation(EG[0:16, :], tna[0:16, :], ACT.Exp, scale=-1.0).then_inc(g_act.sem, 1)
                    sc.wait_ge(taps.sem, taps.at(b, 3 * t + 3))
                    dst = QT[:, t, :] if t < 4 else KT[:, t - 4, :] if t < 8 else VT[:, t - 8, :]
                    sc.activation(dst, ybuf[t % 2], ACT.Silu).then_inc(conv.sem, 1)

                def k_out(n, par):
                    sc.wait_ge(kt_mm.sem, kt_mm.at(n, 1))
                    sc.activation(Ktok[par].rearrange("a p t -> a (p t)"), ps[1][:, :], ACT.Copy).then_inc(kv_ev.sem, 1)

                def zv_out(n, par):
                    sc.wait_ge(z_mm.sem, z_mm.at(n, 1))
                    sc.activation(sz[par], ps[3][:, :], ACT.Silu).then_inc(sz_ok.sem, 1)
                    sc.wait_ge(vt_mm.sem, vt_mm.at(n, 1))
                    sc.activation(Vtok[par], ps[1][:, :], ACT.Copy).then_inc(kv_ev.sem, 1)

                def blocks_out(n):
                    sc.wait_ge(a8_mm.sem, a8_mm.at(n, 1))
                    sc.activation(An[:, :, :, 1:BASE + 1].rearrange("a q i j -> a (q i) j"),
                                  ps[4][:, :].rearrange("a (q j) -> a q j", j=BASE), ACT.Copy).then_inc(a8_ev.sem, 1)

                def y_outs(n):
                    for h in range(2):
                        sc.wait_ge(y_mm.sem, y_mm.at(n, h + 1))
                        src = ps[4 + h][:, :].rearrange("a (p r q) -> a p r q", p=2, r=2)
                        for r in range(2):
                            ev = sc.activation(
                                Y[:, 256 * h:256 * h + 256].rearrange("a (p r v) -> a p r v", p=2, r=2)[:, :, r, :],
                                src[:, :, r, 64 * r:64 * r + 64], ACT.Copy)
                            if r == 1:
                                ev.then_inc(y_ev.sem, 1)

                def inverse(n):
                    for h in range(2):
                        sc.wait_ge(t8_mm.sem, t8_mm.at(n, h + 1))
                        sc.activation(T[:, 4 * h:4 * h + 4, :].rearrange("a q t -> a (q t)"), ps[4 + h][:, :],
                                      ACT.Copy).then_inc(t_ev.sem, 1)
                    for k, s in enumerate(LEVELS):
                        for h in range(2):
                            sc.wait_ge(tz_mm.sem, tz_mm.at(n, 2 * k + h + 1))
                            if s < LEVELS[-1]:
                                sc.activation(T[:, 4 * h:4 * h + 4, :].rearrange("a q t -> a (q t)"),
                                              ps[6 + h][:, :], ACT.Copy).then_inc(t_ev.sem, 1)
                            sc.activation(Z[:, 4 * h:4 * h + 4, :].rearrange("a q t -> a (q t)"),
                                          ps[h][:, :], ACT.Copy).then_inc(z_ev.sem, 1)

                def step(n, par):
                    k_out(n + 1, 1 - par)
                    y_outs(n)
                    zv_out(n + 1, 1 - par)
                    blocks_out(n + 1)
                    inverse(n + 1)

                n0 = b * NC
                k_out(n0, 0)
                zv_out(n0, 0)
                blocks_out(n0)
                inverse(n0)
                with sc.Fori(0, NC // 2 - 1) as c2:
                    for par in range(2):
                        step(n0 + c2 * 2 + par, par)
                step(n0 + (NC - 2), 0)
                y_outs(n0 + (NC - 1))
                for c in range(NC):
                    sc.wait_ge(o_dve.sem, o_dve.at(b * NC + c, 4))
                    if c >= 2:
                        sc.wait_ge(var_ok.sem, var_ok.at(b, c - 1))
                    sc.activation((hq, Ot2)[c % 2], Hall[:, c, :], ACT.Square).then_inc(hq_ok.sem, 1)
                sc.wait_ge(var_ok.sem, var_ok.at(b, NC))
                sc.activation(rstd[:, :, :], var[:, :, :], ACT.Sqrt, bias=w("rmseps"), scale=1.0 / 64).then_inc(n_sd.sem, 1)
                for c in range(NC):
                    sc.wait_ge(ot_mm.sem, ot_mm.at(b, c + 1))
                    sc.activation(oT[:, :, C * c:C * c + C],
                                  ps[2 + c % 2][:, :].rearrange("a (k t) -> a k t", k=8), ACT.Copy).then_inc(ot_ev.sem, 1)
                layer_norm(b, 1)
                sc.wait_ge(gt_dve.sem, gt_dve.at(b, 3))
                sc.activation(lg[:, :, 0:E], lg[:, :, 0:E], ACT.Exp).then_inc(gt_act.sem, 1)
                for j in range(NE):
                    sc.wait_ge(f1_mm.sem, f1_mm.at(b, j + 1))
                    if j >= 3:
                        sc.wait_ge(f_dve.sem, f_dve.at(b, j - 2))
                    bias = w("sfc1b", 2 + j, 3 + j) if j < 2 else w("fc1b", 2 * (j - 2) + 1, 2 * (j - 2) + 2)
                    sc.activation(glu[j % 3], ps[2 * (j % 3) + 1][:, :], ACT.Gelu, bias=bias).then_inc(f_act.sem, 1)
                layer_norm(b, 2)
                sc.wait_ge(a_mm.sem, a_mm.at(b, 3))
                sc.activation(vT, ps[4][:, :], ACT.Identity, bias=w("bv")).then_inc(a_act.sem, 1)
                with sc.Fori(0, H1 // 2) as e2:
                    n = b * (H1 // 2) + e2
                    for k in range(8):
                        sc.wait_ge(a_m.sem, a_m.at(n, k + 1))
                        sc.wait_ge(a_r.sem, a_r.at(n, k - 3))
                        sc.activation(Ering[k % 4], ps[k % 4][:, :], ACT.Exp, bias=mcol[:, k % 4:k % 4 + 1],
                                      scale=-1.0, accum_out=zcol[:, k % 4:k % 4 + 1]).then_inc(a_e.sem, 1)
                sc.wait_ge(a_rs.sem, a_rs.at(b, 1))
                layer_norm(b, 3)
                layer_norm(b, 4)
                sc.wait_ge(b_tr.sem, b_tr.at(b, 1))
                sc.activation(mrow[:, :], ps[7][0:32, 0:128], ACT.Copy, scale=-1.0).then_inc(b_row.sem, 1)
                for i in range(32):
                    sc.wait_ge(b_st.sem, b_st.at(b, i + 1))
                    if i >= 4:
                        sc.wait_ge(b_pv.sem, b_pv.at(b, i - 3))
                    sc.activation(Ering[i % 4], ps[i % 4][:, :], ACT.Exp, scale=-1.0).then_inc(b_e.sem, 1)

        @block.vector
        def _(ve):
            def layer_norm(b, i):
                src = x if i < 4 else u
                dst = u if i == 3 else xn
                ve.wait_ge(ln_pe.sem, ln_pe.at(b, 2 * i + 1))
                ve.tensor_tensor(xc[:, :], src[:, :], ps[0][:, :], ALU.subtract).then_inc(ln_dve.sem, 1)
                ve.wait_ge(ln_act.sem, ln_act.at(b, 2 * i + 2))
                ve.reciprocal(sd[:, :], sd[:, :]).then_inc(ln_dve.sem, 1)
                ve.wait_ge(ln_dve.sem, ln_dve.at(b, 3 * i + 2))
                ve.tensor_tensor(dst[:, :], xc[:, :], sd[:, :], ALU.mult).then_inc(ln_dve.sem, 1)

            ve.wait_ge(pack_in.sem, 32)
            o, _n = at["fc2"]
            fc2 = W[:, o:o + E * 128].rearrange("a (j d) -> a j d", j=E)
            ve.tensor_tensor(fc2, fc2, w("gm").unsqueeze(2).broadcast_to([128, E, 128]), ALU.mult).then_inc(setup.sem, 1)
            o, _n = at["sfc2"]
            sfc2 = W[:, o:o + 256].rearrange("a (j d) -> a j d", j=2)
            ve.tensor_tensor(sfc2, sfc2, w("sgm").unsqueeze(2).broadcast_to([128, 2, 128]), ALU.mult).then_inc(setup.sem, 1)
            ve.tensor_scalar(w("wout"), w("wout"), w("normw"), None, ALU.mult).then_inc(setup.sem, 1)
            ve.memset(owm[:, :, :], 0.0).then_inc(setup.sem, 1)
            ve.memset(obm[:, :], 0.0).then_inc(setup.sem, 1)
            ve.wait_ge(setup.sem, 5)
            for e in range(NX):
                m = D >> e
                ve.tensor_copy(owm[0:m, e, 0:m], w("ow", 0, m, 0, m)).then_inc(setup.sem, 1)
                ve.tensor_copy(obm[0:m, e:e + 1], w("ob", p1=m)).then_inc(setup.sem, 1)
            ve.tensor_scalar(expA[:, :], w("alog"), 88.0, None, ALU.min).then_inc(setup.sem, 1)
            ve.memset(X8[:, :, 0:1], 1.0).then_inc(setup.sem, 1)
            ve.tensor_copy(X8[:, :, 1], w("delta8", 0, 1).broadcast_to([128, 8])).then_inc(setup.sem, 1)
            ve.tensor_copy(An[:, :, :, 0], w("delta8").unsqueeze(1).broadcast_to([128, 8, BASE])).then_inc(setup.sem, 1)
            ve.wait_ge(setup.sem, SETUP)
            ve.sem_inc(e_ok.sem, 1)
            ve.sem_inc(o_dve.sem, 4)
            ve.sem_inc(s_dve.sem, 2)
            with ve.Fori(0, B) as b:
                ve.wait_ge(x_in_s.sem, x_in_s.at(b, 16))
                layer_norm(b, 0)
                def conv_tile(t):
                    ve.wait_ge(tap0.sem, tap0.at(b, t + 1))
                    for k, j in enumerate((2, 1, 0)):
                        sh = KSZ - 1 - j
                        if k:
                            ve.wait_ge(taps.sem, taps.at(b, 3 * t + k))
                        ve.scalar_tensor_tensor(ybuf[t % 2][:, sh:S], ps[2 + t % 4][:, 0:S - sh],
                                                w("convw", KSZ * t + j, KSZ * t + j + 1), ybuf[t % 2][:, sh:S],
                                                ALU.mult, ALU.add).then_inc(taps.sem, 1)

                ve.memset(RT, 0.0).then_inc(g_dve.sem, 1)
                ve.wait_ge(g_dve.sem, g_dve.at(b, 1))
                ve.wait_ge(g_act.sem, g_act.at(b, 1))
                ve.tensor_scalar(td[32:48, :], td[32:48, :], 1.0, None, ALU.add).then_inc(g_dve.sem, 1)
                ve.wait_ge(g_dve.sem, g_dve.at(b, 2))
                ve.reciprocal(RT[32:48, :], td[32:48, :]).then_inc(g_dve.sem, 1)
                ve.tensor_scalar(ta[0:16, :], ps[6][0:16, :], w("dtb", p1=16), None, ALU.add).then_inc(g_dve.sem, 1)
                ve.wait_ge(g_dve.sem, g_dve.at(b, 4))
                ve.scalar_tensor_tensor(tna[0:16, :], ta[0:16, :], -1.0, ta[0:16, :], ALU.mult,
                                        ALU.max).then_inc(g_dve.sem, 1)
                conv_tile(0)
                ve.wait_ge(g_act.sem, g_act.at(b, 2))
                ve.tensor_scalar(tu[0:16, :], tw[0:16, :], 1.0, None, ALU.add).then_inc(g_dve.sem, 1)
                ve.wait_ge(g_dve.sem, g_dve.at(b, 6))
                ve.scalar_tensor_tensor(tw[0:16, :], tu[0:16, :], -1.0, tw[0:16, :], ALU.add,
                                        ALU.subtract).then_inc(g_dve.sem, 1)
                conv_tile(1)
                ve.wait_ge(g_dve.sem, g_dve.at(b, 7))
                ve.wait_ge(g_act.sem, g_act.at(b, 3))
                ve.reciprocal(tu[0:16, :], tu[0:16, :]).then_inc(g_dve.sem, 1)
                ve.wait_ge(g_dve.sem, g_dve.at(b, 8))
                ve.tensor_tensor(tw[0:16, :], tw[0:16, :], tu[0:16, :], ALU.mult).then_inc(g_dve.sem, 1)
                conv_tile(2)
                ve.wait_ge(g_dve.sem, g_dve.at(b, 9))
                ve.tensor_tensor(tl[0:16, :], tl[0:16, :], tw[0:16, :], ALU.subtract).then_inc(g_dve.sem, 1)
                ve.wait_ge(g_dve.sem, g_dve.at(b, 10))
                ve.scalar_tensor_tensor(tl[0:16, :], ta[0:16, :], 0.0, tl[0:16, :], ALU.max,
                                        ALU.add).then_inc(g_dve.sem, 1)
                conv_tile(3)
                ve.wait_ge(g_dve.sem, g_dve.at(b, 11))
                ve.tensor_scalar(tna[0:16, :], tl[0:16, :], expA[0:16, :], 1e30, ALU.mult,
                                 ALU.min).then_inc(g_dve.sem, 1)
                for t in range(4, 7):
                    conv_tile(t)
                ve.wait_ge(g_act.sem, g_act.at(b, 4))
                ve.tensor_copy(EGm[0:16, :], EG[0:16, :]).then_inc(g_dve.sem, 1)
                ve.memset(D1[0:16, :], 0.0).then_inc(g_dve.sem, 1)
                ve.wait_ge(g_dve.sem, g_dve.at(b, 14))
                ve.tensor_copy(D1[0:16, 0:S:C], EG[0:16, 0:S:C]).then_inc(g_dve.sem, 1)
                ve.memset(EGm[0:16, 0:S:C], 0.0).then_inc(g_dve.sem, 1)
                ve.wait_ge(g_dve.sem, g_dve.at(b, 16))
                ve.tensor_tensor_scan(RT[0:16, :], EGm[0:16, :], D1[0:16, :], 0.0, ALU.mult, ALU.add).then_inc(gamma_ok.sem, 1)
                conv_tile(7)
                ve.wait_ge(gamma_ok.sem, gamma_ok.at(b, 1))
                ve.tensor_copy(gl[:, :], RT[0:16, C - 1:S:C]).then_inc(g_dve.sem, 1)
                for t in range(8, NT):
                    conv_tile(t)
                ve.wait_ge(tc_mm.sem, tc_mm.at(b, 1))
                ve.tensor_copy(tc[:, :, :, :].rearrange("a c q n -> a (c q n)"), ps[7][:, 0:NC * 16]).then_inc(tc_ok.sem, 1)
                ve.wait_ge(eg_dma.sem, eg_dma.at(b, 48))
                ve.wait_ge(gl_dma.sem, gl_dma.at(b, 48))
                ve.memset(St, 0.0).then_inc(s0.sem, 1)

                def v3(t):
                    return t.rearrange("a (q v) -> a q v", q=8)

                def gamma(c):
                    return tc[:, bass.ds(c, 1), 0, :].rearrange("a c q -> a (c q)").unsqueeze(2).broadcast_to([128, 8, 64])

                def decays(n, par):
                    ve.wait_ge(c_d1.sem, c_d1.at(n, 1))
                    ve.tensor_tensor_scan(Ec[par], EGc, d1, 0.0, ALU.mult, ALU.add).then_inc(e_ok.sem, 1)

                def triangle(n, par):
                    ve.wait_ge(e_ok.sem, e_ok.at(n, 1))
                    ve.wait_ge(kq_mm.sem, kq_mm.at(n, 1))
                    kk = ps[0][:, :].rearrange("a (p q t) -> a p q t", p=4, q=2)[:, :, 0, :]
                    ve.tensor_tensor(Lc.rearrange("a (p r t) -> a p r t", p=4, r=2),
                                     kk.unsqueeze(2).broadcast_to([128, 4, 2, 64]),
                                     Ec[par].rearrange("a (p r t) -> a p r t", p=4, r=2), ALU.mult).then_inc(lc_ok.sem, 1)

                def blocks(n):
                    ve.wait_ge(lc_ok.sem, lc_ok.at(n, 1))
                    ve.tensor_tensor(M8.rearrange("a (q i k) -> a q k i", q=8, i=BASE),
                                     Lc.rearrange("a (q k i) -> a q k i", q=8, i=BASE),
                                     w("blk8").unsqueeze(1).unsqueeze(3).broadcast_to([128, 8, 8, BASE]),
                                     ALU.mult).then_inc(m8_ok.sem, 1)
                    ve.wait_ge(m8_ok.sem, m8_ok.at(n, 1))
                    ve.tensor_reduce(Xd[:, :, :].rearrange("a q i -> a (q i)"), M8.rearrange("a (q k) -> a q k", k=8), AX,
                                     ALU.add).then_inc(m8_ok.sem, 1)
                    ve.wait_ge(m8_ok.sem, m8_ok.at(n, 2))
                    ve.tensor_tensor(rhs8.rearrange("a (q i j) -> a q i j", q=8, i=BASE),
                                     Xd[:, :, :].unsqueeze(3).broadcast_to([128, 8, BASE, BASE]),
                                     w("diag8").rearrange("a (i j) -> a i j", i=BASE).unsqueeze(1).broadcast_to(
                                         [128, 8, BASE, BASE]), ALU.mult).then_inc(m8_ok.sem, 1)

                def substitute(n):
                    ve.wait_ge(a8_ev.sem, a8_ev.at(n, 1))
                    for i in range(1, BASE):
                        if i > 1:
                            ve.wait_ge(x8_ok.sem, x8_ok.at(n, 2 * i - 2))
                        ve.tensor_tensor(prod[:, :, 0:i + 1], An[:, :, i, 0:i + 1], X8[:, :, 0:i + 1],
                                         ALU.mult).then_inc(x8_ok.sem, 1)
                        ve.wait_ge(x8_ok.sem, x8_ok.at(n, 2 * i - 1))
                        ve.tensor_reduce(X8[:, :, i + 1], prod[:, :, 0:i + 1], AX, ALU.add).then_inc(x8_ok.sem, 1)
                    ve.wait_ge(x8_ok.sem, x8_ok.at(n, 2 * (BASE - 1)))
                    ve.tensor_tensor(Z[:, :, :].rearrange("a q (k i) -> a q k i", i=BASE),
                                     X8[:, :, 1:BASE + 1].unsqueeze(2).broadcast_to([128, 8, 16, BASE]),
                                     w("blk16").unsqueeze(1).unsqueeze(3).broadcast_to([128, 8, 16, BASE]),
                                     ALU.mult).then_inc(z8_ok.sem, 1)

                def within(n, par):
                    ve.wait_ge(bd0.sem, bd0.at(b, 2))
                    for e in range(2):
                        rows = slice(64 * e, 64 * e + 64)
                        src = ps[0][rows, :].rearrange("a (p q t) -> a p q t", p=4, q=2)[:, :, 1, :]
                        ve.tensor_tensor(
                            P[par][rows, :, 64 * e:64 * e + 64].rearrange("a (p r) t -> a p r t", r=2),
                            src.unsqueeze(2).broadcast_to([64, 4, 2, 64]),
                            Ec[par][rows, :].rearrange("a (p r t) -> a p r t", p=4, r=2), ALU.mult).then_inc(p_dve.sem, 1)

                def level(n, k):
                    mask = w("masks", 128 * k, 128 * k + 128).unsqueeze(1).broadcast_to([128, 4, 128])
                    for h in range(2):
                        ve.wait_ge(x_mm.sem, x_mm.at(n, 2 * k + h + 1))
                        ve.tensor_tensor(Wm[:, 4 * h:4 * h + 4, :], ps[4 + h][:, :].rearrange("a (q t) -> a q t", q=4),
                                         mask, ALU.mult).then_inc(w_ev.sem, 1)

                def residual(n, c, par):
                    ve.wait_ge(ks_mm.sem, ks_mm.at(n, 1))
                    ve.tensor_tensor(v3(R), v3(ps[2][:, :]), gamma(c), ALU.mult).then_inc(r_dve.sem, 1)
                    ve.wait_ge(r_dve.sem, r_dve.at(n, 1))
                    ve.wait_ge(kv_ev.sem, kv_ev.at(n, 2))
                    ve.tensor_tensor(R, Vtok[par], R, ALU.subtract).then_inc(r_dve.sem, 1)

                def outer(n, c):
                    ve.wait_ge(qs_mm.sem, qs_mm.at(n, 1))
                    ve.tensor_tensor(v3(Ot), v3(ps[3][:, :]), gamma(c), ALU.mult).then_inc(o_dve.sem, 1)

                def last_decay(n, par):
                    ve.wait_ge(y_ev.sem, y_ev.at(n, 2))
                    ve.tensor_tensor(v3(Yd), v3(Y), v3(Ec[par])[:, :, 63:64].broadcast_to([128, 8, 64]),
                                     ALU.mult).then_inc(yd_ok.sem, 1)

                def new_state(n, c):
                    glast = glB[:, :, bass.ds(c, 1)].broadcast_to([128, 8, 64])
                    ve.tensor_tensor(v3(St), v3(St), glast, ALU.mult).then_inc(s_dve.sem, 1)
                    ve.wait_ge(s_mm.sem, s_mm.at(n, 1))
                    ve.wait_ge(s_dve.sem, s_dve.at(n, 1))
                    ve.tensor_tensor(St, St, ps[2][:, :], ALU.add).then_inc(s_dve.sem, 1)

                def heads(n, c, par):
                    for h in range(2):
                        ve.wait_ge(o_mm.sem, o_mm.at(n, h + 1))
                        for r in range(2):
                            ov = Ot[:, 256 * h:256 * h + 256].rearrange("a (p r v) -> a p r v", p=2, r=2)[:, :, r, :]
                            src = ps[6 + h][:, :].rearrange("a (p r q) -> a p r q", p=2, r=2)[:, :, r, 64 * r:64 * r + 64]
                            ins = ve.tensor_tensor(ov, ov, src, ALU.add)
                            if r == 1:
                                ins.then_inc(o_dve.sem, 1)
                    ve.wait_ge(o_dve.sem, o_dve.at(n, 3))
                    hc = Hall[:, bass.ds(c, 1), :].rearrange("a c n -> a (c n)")
                    ve.scalar_tensor_tensor(hc, Ot, 0.125, sz[par], ALU.mult, ALU.mult).then_inc(o_dve.sem, 1)

                def step(n, c, par):
                    residual(n, c, par)
                    decays(n + 1, 1 - par)
                    triangle(n + 1, 1 - par)
                    outer(n, c)
                    blocks(n + 1)
                    last_decay(n, par)
                    substitute(n + 1)
                    within(n + 1, 1 - par)
                    new_state(n, c)
                    level(n + 1, 0)
                    heads(n, c, par)
                    level(n + 1, 1)
                    level(n + 1, 2)

                n0 = b * NC
                decays(n0, 0)
                triangle(n0, 0)
                blocks(n0)
                substitute(n0)
                within(n0, 0)
                for k in range(len(LEVELS)):
                    level(n0, k)
                with ve.Fori(0, NC // 2 - 1) as c2:
                    for par in range(2):
                        step(n0 + c2 * 2 + par, c2 * 2 + par, par)
                step(n0 + (NC - 2), NC - 2, 0)
                residual(n0 + (NC - 1), NC - 1, 1)
                outer(n0 + (NC - 1), NC - 1)
                last_decay(n0 + (NC - 1), 1)
                new_state(n0 + (NC - 1), NC - 1)
                heads(n0 + (NC - 1), NC - 1, 1)
                for c in range(NC):
                    ve.wait_ge(hq_ok.sem, hq_ok.at(b, c + 1))
                    ve.tensor_reduce(var[:, c, :], (hq, Ot2)[c % 2].rearrange("a (q v) -> a q v", q=8), AX,
                                     ALU.add).then_inc(var_ok.sem, 1)
                ve.wait_ge(n_sd.sem, n_sd.at(b, 1))
                ve.reciprocal(rstd[:, :, :], rstd[:, :, :]).then_inc(n_rs.sem, 1)
                ve.wait_ge(n_rs.sem, n_rs.at(b, 1))
                for c in range(NC):
                    hv = Hall[:, c, :].rearrange("a (q v) -> a q v", q=8)
                    ve.tensor_tensor(hv, hv, rstd[:, c, :].unsqueeze(2).broadcast_to([128, 8, 64]),
                                     ALU.mult).then_inc(hn_ok.sem, 1)
                ve.wait_ge(op_mm.sem, op_mm.at(b, 1))
                ve.tensor_tensor(x[:, :], x[:, :], ps[4][:, :], ALU.add).then_inc(xr.sem, 1)
                layer_norm(b, 1)
                ve.wait_ge(gt_mm.sem, gt_mm.at(b, 1))
                ve.tensor_copy(lg[:, :, 0:E], ps[6][:, 0:64].rearrange("a (t e) -> a t e", t=4)[:, :, 0:E]).then_inc(gt_dve.sem, 1)
                ve.wait_ge(gt_dve.sem, gt_dve.at(b, 1))
                ve.tensor_reduce(mx4, lg[:, :, 0:E], AX, ALU.max).then_inc(gt_dve.sem, 1)
                ve.wait_ge(gt_dve.sem, gt_dve.at(b, 2))
                ve.tensor_tensor(lg[:, :, 0:E], lg[:, :, 0:E], mx4.unsqueeze(2).broadcast_to([128, 4, E]), ALU.subtract).then_inc(gt_dve.sem, 1)
                ve.wait_ge(gt_dve.sem, gt_dve.at(b, 3))
                ve.wait_ge(gt_act.sem, gt_act.at(b, 1))
                ve.tensor_reduce(sm4, lg[:, :, 0:E], AX, ALU.add).then_inc(gt_dve.sem, 1)
                ve.wait_ge(gt_dve.sem, gt_dve.at(b, 4))
                ve.reciprocal(rc4, sm4).then_inc(gt_dve.sem, 1)
                ve.wait_ge(gt_dve.sem, gt_dve.at(b, 5))
                ve.tensor_tensor(scp[:, :, 0:E], lg[:, :, 0:E], rc4.unsqueeze(2).broadcast_to([128, 4, E]), ALU.mult).then_inc(gt_dve.sem, 1)
                ve.wait_ge(gt_dve.sem, gt_dve.at(b, 6))
                ve.tensor_copy(scp[:, :, E:20], w("pads").unsqueeze(1).broadcast_to([128, 4, 5])).then_inc(gt_dve.sem, 1)
                ve.wait_ge(gt_dve.sem, gt_dve.at(b, 7))
                hold(ve)
                for t in range(4):
                    ins = ve.max(m8[:, t, :], scp[:, t, :])
                    if t == 3:
                        ins.then_inc(gt_dve.sem, 1)
                        ve.wait_ge(gt_dve.sem, gt_dve.at(b, 8))
                ve.tensor_copy(tr8[:, :, 0:3], m8[:, :, 0:3]).then_inc(gt_dve.sem, 1)
                ve.wait_ge(gt_dve.sem, gt_dve.at(b, 9))
                ve.tensor_copy(tr8[:, :, 3:8], w("pads").unsqueeze(1).broadcast_to([128, 4, 5])).then_inc(gt_dve.sem, 1)
                ve.wait_ge(gt_dve.sem, gt_dve.at(b, 10))
                hold(ve)
                for t in range(4):
                    ins = ve.match_replace(rep[:, t, :], tr8[:, t, :], scp[:, t, :], -9.0)
                    if t == 3:
                        ins.then_inc(gt_dve.sem, 1)
                        ve.wait_ge(gt_dve.sem, gt_dve.at(b, 11))
                ve.tensor_tensor(pk[:, :, 0:E], rep[:, :, 0:E], scp[:, :, 0:E], ALU.not_equal).then_inc(gt_dve.sem, 1)
                ve.wait_ge(gt_dve.sem, gt_dve.at(b, 12))
                ve.tensor_tensor(lg[:, :, 0:E], pk[:, :, 0:E], scp[:, :, 0:E], ALU.mult).then_inc(gt_dve.sem, 1)
                ve.wait_ge(gt_dve.sem, gt_dve.at(b, 13))
                ve.tensor_reduce(sm4, m8[:, :, 0:3], AX, ALU.add).then_inc(gt_dve.sem, 1)
                ve.wait_ge(gt_dve.sem, gt_dve.at(b, 14))
                ve.tensor_scalar(sm4, sm4, 1e-20, None, ALU.add).then_inc(gt_dve.sem, 1)
                ve.wait_ge(gt_dve.sem, gt_dve.at(b, 15))
                ve.reciprocal(rc4, sm4).then_inc(gt_dve.sem, 1)
                ve.wait_ge(gt_dve.sem, gt_dve.at(b, 16))
                ve.tensor_tensor(lg[:, :, 0:E], lg[:, :, 0:E], rc4.unsqueeze(2).broadcast_to([128, 4, E]), ALU.mult).then_inc(gt_dve.sem, 1)
                ve.wait_ge(gt_dve.sem, gt_dve.at(b, 17))

                def hidden(j):
                    ve.wait_ge(f_act.sem, f_act.at(b, j + 1))
                    if j >= 5:
                        ve.wait_ge(f_pool.sem, f_pool.at(b, j - 4))
                    elif j >= 3:
                        ve.wait_ge(f2_mm.sem, f2_mm.at(b, j - 2))
                    bias = w("sfc1b", j, j + 1) if j < 2 else w("fc1b", 2 * (j - 2), 2 * (j - 2) + 1)
                    ve.scalar_tensor_tensor(hid[j % 3], ps[2 * (j % 3)][:, :], bias, glu[j % 3], ALU.add,
                                            ALU.mult).then_inc(f_dve.sem, 1)
                hidden(0)
                hidden(1)
                ve.wait_ge(ct_mm.sem, ct_mm.at(b, 1))
                ve.tensor_copy(combT[0:E, :], ps[6][0:E, :]).then_inc(gt_dve.sem, 1)
                for j in range(2, NE):
                    hidden(j)
                ve.wait_ge(f2_mm.sem, f2_mm.at(b, NE))
                ve.scalar_tensor_tensor(x[:, :], ps[7][:, :], w("sfc2b"), x[:, :], ALU.add, ALU.add).then_inc(xr.sem, 1)
                ve.wait_ge(xr.sem, xr.at(b, 2))
                layer_norm(b, 2)

                def split(sig, k0, src, parts):
                    ve.tensor_copy(parts[0], src).then_inc(sig.sem, 1)
                    ve.wait_ge(sig.sem, sig.at(b, k0 + 1))
                    ve.tensor_tensor(r1, src, parts[0], ALU.subtract).then_inc(sig.sem, 1)
                    ve.wait_ge(sig.sem, sig.at(b, k0 + 2))
                    ve.tensor_copy(parts[1], r1).then_inc(sig.sem, 1)
                    ve.wait_ge(sig.sem, sig.at(b, k0 + 3))
                    ve.tensor_tensor(r1, r1, parts[1], ALU.subtract).then_inc(sig.sem, 1)
                    ve.wait_ge(sig.sem, sig.at(b, k0 + 4))
                    ve.tensor_copy(parts[2], r1).then_inc(sig.sem, 1)
                    ve.wait_ge(sig.sem, sig.at(b, k0 + 5))

                def project(sig_mm, sig, bank, bias, k0, dst, parts, scale):
                    ve.tensor_scalar(dst, ps[bank][:, :], bias, scale, ALU.add, ALU.mult).then_inc(sig.sem, 1)
                    ve.wait_ge(sig.sem, sig.at(b, k0 + 1))
                    split(sig, k0 + 1, dst, parts)

                scale = float(np.float32(1.0 / np.sqrt(128)))
                ve.wait_ge(a_mm.sem, a_mm.at(b, 2))
                project(a_mm, a_dve, 2, w("bq"), 0, qs, qsp, -scale)
                project(a_mm, a_dve, 3, w("bk"), 6, ks, ksp, scale)
                hold(ve)
                with ve.Fori(0, H1 // 2) as e2:
                    n = b * (H1 // 2) + e2
                    for i in range(2):
                        for k in range(4):
                            ve.wait_ge(a_s.sem, a_s.at(n, 4 * i + k + 1))
                            ve.wait_ge(a_e.sem, a_e.at(n, 4 * i + k - 3))
                            ve.tensor_reduce(mcol[:, k:k + 1], ps[k][:, :], AX, ALU.min).then_inc(a_m.sem, 1)
                        for k in range(4):
                            ve.wait_ge(a_e.sem, a_e.at(n, 4 * i + k + 1))
                            ve.reciprocal(zrec[:, k:k + 1], zcol[:, k:k + 1]).then_inc(a_z.sem, 1)
                            ve.wait_ge(a_z.sem, a_z.at(n, 4 * i + k + 1))
                            ve.wait_ge(a_r.sem, a_r.at(n, 4 * i + k - 3))
                            ve.tensor_scalar(ZP[:, k, :], w("onehot")[:, bass.ds(e2 * 32 + 16 * i, 16)],
                                             zrec[:, k:k + 1], None, ALU.mult).then_inc(a_zp.sem, 1)
                ve.wait_ge(a_sum.sem, a_sum.at(b, 1))
                ve.tensor_copy(rs[0:16, :], ps[4][0:16, :]).then_inc(a_rs.sem, 1)
                ve.wait_ge(a_rd.sem, a_rd.at(b, 32))
                ve.tensor_tensor(att, vT, Rb, ALU.mult).then_inc(a_at.sem, 1)
                ve.wait_ge(a_wo.sem, a_wo.at(b, 1))
                ve.scalar_tensor_tensor(x[:, :], ps[5][:, :], w("bo"), x[:, :], ALU.add, ALU.add).then_inc(xr.sem, 1)
                ve.wait_ge(xr.sem, xr.at(b, 3))
                layer_norm(b, 3)
                ve.wait_ge(ln_dve.sem, ln_dve.at(b, 12))
                layer_norm(b, 4)
                ve.wait_ge(ln_dve.sem, ln_dve.at(b, 15))
                ve.tensor_scalar(xn[:, :], xn[:, :], w("nw"), w("nb"), ALU.mult, ALU.add).then_inc(b_xn.sem, 1)
                ve.tensor_tensor(x[:, :], x[:, :], u[:, :], ALU.add).then_inc(fin.sem, 1)
                scale = float(D) ** -0.5
                ve.wait_ge(b_mm.sem, b_mm.at(b, 2))
                project(b_mm, b_dve, 2, w("qb"), 0, qs, qsp, -scale)
                project(b_mm, b_dve, 3, w("kb"), 6, ks, ksp, 1.0)
                ve.wait_ge(b_mm.sem, b_mm.at(b, 3))
                ve.wait_ge(b_pool.sem, b_pool.at(b, 2))
                for k in range(4):
                    for g2 in range(2):
                        base = 1024 * k + 512 * g2
                        ins = ve.tensor_tensor(
                            vslots(base),
                            ps[4][:, 128 * k + 64 * g2:128 * k + 64 * g2 + 64].rearrange("a (h y) -> a h y", h=4),
                            w("vb", 64 * g2, 64 * g2 + 64).rearrange("a (h y) -> a h y", h=4), ALU.add)
                    ins.then_inc(b_v.sem, 1)
                for i in range(32):
                    ve.wait_ge(b_s.sem, b_s.at(b, i + 1))
                    ve.tensor_reduce(mq[:, i:i + 1], ps[i % 4][:, :], AX, ALU.min).then_inc(b_m.sem, 1)
                for g2 in range(2):
                    ve.wait_ge(b_pv.sem, b_pv.at(b, 16 * g2 + 16))
                    ve.reciprocal((rcp, r1)[g2][0:64, :], ps[4 + g2][64:128, :]).then_inc(b_rc.sem, 1)
                    ve.wait_ge(b_rc.sem, b_rc.at(b, g2 + 1))
                    ve.tensor_tensor(att[64 * g2:64 * g2 + 64, :], ps[4 + g2][0:64, :], (rcp, r1)[g2][0:64, :],
                                     ALU.mult).then_inc(b_at.sem, 1)
                ve.wait_ge(b_wo.sem, b_wo.at(b, 1))
                ve.wait_ge(fin.sem, fin.at(b, 1))
                ve.tensor_tensor(x[:, :], x[:, :], ps[0][:, :], ALU.add).then_inc(fin.sem, 1)
                ve.wait_ge(fin.sem, fin.at(b, 2))
                xe = x[:, :].rearrange("a (e t) -> a e t", e=NX)
                ve.tensor_tensor(xe, xe, obm[:, :].unsqueeze(2).broadcast_to([128, NX, 128]), ALU.add).then_inc(fin.sem, 1)

        @block.gpsimd
        def _(po):
            po.wait_ge(pack_in.sem, 32)
            with po.Fori(0, B) as b:
                po.wait_ge(x_in_s.sem, x_in_s.at(b, 16))
                hold(po)
                po.memset(P[0], 0.0).then_inc(bd0.sem, 1)
                po.memset(P[1], 0.0).then_inc(bd0.sem, 1)
                half = w("half").unsqueeze(1).unsqueeze(3)

                def copies(n, c, par):
                    tok = bass.ds(c * C, C)
                    po.wait_ge(eg_dma.sem, eg_dma.at(b, 48))
                    po.wait_ge(tc_ok.sem, tc_ok.at(b, 1))
                    po.wait_ge(e_ok.sem, e_ok.at(n - 1, 1))
                    hold(po)
                    po.tensor_copy(EGc.rearrange("a (q t) -> a q t", q=8), egB[:, :, tok]).then_inc(eg_cp.sem, 1)
                    po.tensor_tensor(d1.rearrange("a (q t) -> a q t", q=8),
                                     w("identc").unsqueeze(1).broadcast_to([128, 8, C]),
                                     tc[:, bass.ds(c, 1), 1, :].rearrange("a c q -> a (c q)").unsqueeze(2).broadcast_to([128, 8, C]),
                                     ALU.mult).then_inc(c_d1.sem, 1)
                    po.wait_ge(conv.sem, conv.at(b, NT))
                    po.wait_ge(qs_mm.sem, qs_mm.at(n - 2, 1))
                    po.wait_ge(kq_mm.sem, kq_mm.at(n - 1, 1))
                    po.wait_ge(z_mm.sem, z_mm.at(n - 1, 1))
                    po.wait_ge(vt_mm.sem, vt_mm.at(n - 1, 1))
                    hold(po)
                    for dst, src in ((Kbd[par], KT), (Qbd[par], QT)):
                        po.tensor_tensor(dst.rearrange("a p (e t) -> a p e t", e=2),
                                         src[:, :, tok].unsqueeze(2).broadcast_to([128, 4, 2, C]),
                                         half.broadcast_to([128, 4, 2, C]), ALU.mult).then_inc(c_cp.sem, 1)
                    po.tensor_copy(KQc[:, :, 0, :], KT[:, :, tok]).then_inc(c_cp.sem, 1)
                    po.tensor_copy(KQc[:, :, 1, :], QT[:, :, tok]).then_inc(c_cp.sem, 1)
                    for h in range(2):
                        po.tensor_copy(Vc[:, 4 * h:4 * h + 4, :], VT[:, 4 * h:4 * h + 4, tok]).then_inc(c_cp.sem, 1)
                    po.tensor_copy(xch[:, :], xn[:, tok]).then_inc(c_cp.sem, 1)

                def triangle(n):
                    po.wait_ge(lc_ok.sem, lc_ok.at(n, 1))
                    po.wait_ge(x_mm.sem, x_mm.at(n - 1, 6))
                    hold(po)
                    po.tensor_tensor(LT[:, :, :].rearrange("a q (e t) -> a q e t", e=2),
                                     Lc.rearrange("a (q t) -> a q t", q=8).unsqueeze(2).broadcast_to([128, 8, 2, C]),
                                     half.broadcast_to([128, 8, 2, C]), ALU.mult).then_inc(lt_ok.sem, 1)
                    po.wait_ge(lt_ok.sem, lt_ok.at(n, 1))
                    hold(po)
                    po.affine_select(out=LT, in_=LT, compare_op=ALU.not_equal, fill=1.0, base=0,
                                     pattern=[[0, 8], [-1, 128]], channel_multiplier=1).then_inc(lt_ok.sem, 1)

                n0 = b * NC
                copies(n0, 0, 0)
                with po.Fori(0, NC // 2 - 1) as c2:
                    for par in range(2):
                        triangle(n0 + c2 * 2 + par)
                        copies(n0 + c2 * 2 + par + 1, c2 * 2 + par + 1, 1 - par)
                triangle(n0 + (NC - 2))
                copies(n0 + (NC - 1), NC - 1, 1)
                triangle(n0 + (NC - 1))
                po.wait_ge(gt_dve.sem, gt_dve.at(b, 18))
                for j in range(2, NE):
                    po.wait_ge(f_dve.sem, f_dve.at(b, j + 1))
                    po.wait_ge(cb_dma.sem, cb_dma.at(b, 64))
                    if j >= 5:
                        po.wait_ge(f2_mm.sem, f2_mm.at(b, j - 2))
                    po.tensor_tensor(act[j % 3], hid[j % 3], combB[:, j - 2, :], ALU.mult).then_inc(f_pool.sem, 1)
                po.wait_ge(f2_mm.sem, f2_mm.at(b, NE))
                hold(po)
                po.memset(zero[:, 0:16], 0.0).then_inc(zero_ok.sem, 1)
                po.wait_ge(zero_ok.sem, zero_ok.at(b, 1))
                hold(po)
                with po.Fori(0, H1 // 2) as e2:
                    n = b * (H1 // 2) + e2
                    for i in range(2):
                        po.wait_ge(a_dma.sem, a_dma.at(b, 12 * 16))
                        po.wait_ge(a_s.sem, a_s.at(n, 4 * i - 4))
                        hold(po)
                        po.tensor_copy(QXe[i][0:48, :].rearrange("a (g t) -> a g t", g=16),
                                       QX[0:48, :, bass.ds(e2 * 64 + 32 * i, 32)]).then_inc(a_kx.sem, 1)
                        po.tensor_copy(KXe[i][0:48, :].rearrange("a (g t) -> a g t", g=16),
                                       KX[0:48, :, bass.ds(e2 * 64 + 32 * i, 32)]).then_inc(a_kx.sem, 1)
                po.wait_ge(xr.sem, xr.at(b, 3))
                hold(po)
                po.memset(Vflat, 0.0).then_inc(b_pool.sem, 1)
                po.wait_ge(b_pool.sem, b_pool.at(b, 1))
                hold(po)
                for g2 in range(8):
                    ins = po.memset(vslots(512 * g2 + 64), 1.0)
                ins.then_inc(b_pool.sem, 1)
                po.wait_ge(b_pool.sem, b_pool.at(b, 2))
                hold(po)
                po.memset(KH[96:97, :, :], 1.0).then_inc(b_pool.sem, 1)


def _head_order():
    return [(2 * p + e) * 2 + r for e in range(2) for p in range(4) for r in range(2)]


def pack_inputs(i):
    f = np.float32

    def col(v):
        v = np.asarray(v).reshape(-1)
        return np.concatenate([v, np.zeros(128 - v.size, f)])[:, None]

    def cols(m):
        return np.ascontiguousarray(np.asarray(m).T)

    order = _head_order()
    parts = {}
    parts["wqkv"] = cols(i["L0_attn_W_qkv"])
    parts["convw"] = np.asarray(i["L0_attn_conv_w"]).reshape(NT, 128, KSZ).transpose(1, 0, 2).reshape(128, NT * KSZ)
    parts["wz"] = cols(i["L0_attn_W_z"]).reshape(128, 4, 2, 128).transpose(0, 2, 1, 3).reshape(128, 1024)
    parts["wab"] = np.concatenate([cols(i["L0_attn_W_a"])[:, order], np.zeros((128, 16), f),
                                   cols(i["L0_attn_W_b"])[:, order]], 1)
    parts["dtb"], parts["alog"] = col(np.asarray(i["L0_attn_dt_bias"])[order]), col(np.asarray(i["L0_attn_A_log"])[order])
    parts["normw"] = col(np.tile(np.asarray(i["L0_attn_norm_weight"]), 2))
    parts["wout"] = cols(i["L0_attn_W_out"]).reshape(8, 128, 128).transpose(1, 0, 2).reshape(128, 1024)
    parts["gate"] = cols(i["L0_ffn_gate_w"])
    parts["fc1"] = np.asarray(i["L0_ffn_fc1_w"]).transpose(2, 0, 1).reshape(128, E * 256)
    parts["fc1b"] = np.asarray(i["L0_ffn_fc1_b"]).reshape(E * 2, 128).T
    parts["gm"] = cols(i["L0_ffn_geglu_mult"])
    parts["fc2"] = np.asarray(i["L0_ffn_fc2_w"]).transpose(2, 0, 1).reshape(128, E * 128)
    parts["fc2b"] = np.concatenate([np.asarray(i["L0_ffn_fc2_b"]), np.zeros((128 - E, 128), f)], 0)
    parts["sfc1"] = cols(i["L0_ffn_s_fc1_w"])
    parts["sfc1b"] = np.asarray(i["L0_ffn_s_fc1_b"]).reshape(4, 128).T
    parts["sgm"] = np.asarray(i["L0_ffn_s_geglu_mult"]).reshape(2, 128).T
    parts["sfc2"] = cols(i["L0_ffn_s_fc2_w"]).reshape(2, 128, 128).transpose(1, 0, 2).reshape(128, 256)
    parts["sfc2b"] = col(i["L0_ffn_s_fc2_b"])
    for k in "qkvo":
        parts["w" + k], parts["b" + k] = np.asarray(i["L1_attn_W" + k]), col(i["L1_attn_b" + k])
        parts[k + "w"] = cols(i[f"L1_ffn_{k}_w"])
    for k in "qko":
        parts[k + "b"] = col(i[f"L1_ffn_{k}_b"])
    parts["vb"] = np.broadcast_to(np.asarray(i["L1_ffn_v_b"]), (128, 128))
    parts["nw"], parts["nb"] = col(i["L1_ffn_norm_w"]), col(i["L1_ffn_norm_b"])
    eye = np.eye(128, dtype=f)
    parts["ident"], parts["mean"] = eye, np.full((128, 128), 1.0 / 128, f)
    r, c = np.arange(128)[:, None], np.arange(128)[None, :]

    def doubling(s):
        low = (r // (2 * s) == c // (2 * s)) & (r // s == c // s + 1)
        return (eye - low).astype(f)

    parts["masks"] = np.concatenate([doubling(s) for s in LEVELS], 1)
    parts["same8"] = (r // BASE == c // BASE).astype(f)
    parts["blk8"] = (r % C // BASE == np.arange(8)[None, :]).astype(f)
    parts["blk16"] = (r // BASE == np.arange(16)[None, :]).astype(f)
    parts["diag8"] = -(r % BASE == np.tile(np.arange(BASE), BASE)[None, :]).astype(f)
    parts["delta8"] = (r % BASE == np.arange(BASE)[None, :]).astype(f)
    parts["identc"] = np.concatenate([np.eye(C, dtype=f)] * 2, 0)
    parts["half"] = (r // 64 == np.arange(2)[None, :]).astype(f)
    sel = np.zeros((128, 32), f)
    for e in range(2):
        for q in range(8):
            sel[8 * e + q, 16 * e + q] = 1
            sel[32 + 8 * e + q, 16 * e + 8 + q] = 1
    parts["sel"] = sel
    parts["onehot"] = np.broadcast_to(np.eye(16, dtype=f).reshape(1, 256), (128, 256))
    parts["lneps"], parts["rmseps"] = np.full((128, 1), LN_EPS, f), np.full((128, 1), RMS_EPS, f)
    parts["pads"] = np.broadcast_to(np.array([-1, -2, -3, -4, -5], f), (128, 5))
    at, n = columns()
    for name, (o, width) in at.items():
        assert parts[name].shape == (128, width), (name, parts[name].shape, width)
    return np.ascontiguousarray(np.concatenate([parts[name] for name in at], 1))


def kernel(**inputs):
    import concourse.bacc as bacc
    from concourse.bass_utils import run_bass_kernel_spmd

    nc = bacc.Bacc("TRN2", target_bir_lowering=False, num_devices=1)
    arrays = {
        "x_channels": np.ascontiguousarray(np.asarray(inputs["L0_attn_hidden_states"]).transpose(0, 2, 1)),
        "weights": pack_inputs(inputs),
    }
    args = [nc.dram_tensor(k, a.shape, F32, kind="ExternalInput").ap() for k, a in arrays.items()]
    args.append(nc.dram_tensor("y_channels", (B, D, S), F32, kind="ExternalOutput").ap())
    build(nc, *args)
    r = run_bass_kernel_spmd(nc, [arrays], core_ids=[0])
    return np.ascontiguousarray(r.results[0]["y_channels"].transpose(0, 2, 1))
```

```python
from contextlib import ExitStack

import numpy as np

import concourse.bass as bass
from concourse import mybir

F32 = mybir.dt.float32
BF16 = mybir.dt.bfloat16
ALU = mybir.AluOpType
ACT = mybir.ActivationFunctionType
AX = mybir.AxisListType.X

B, S, D = 8, 512, 128
C = 64
NC = S // C
NT = 16
KSZ = 4
E, TOPK = 15, 3
NE = E + 2
H1 = 16
NX = 4
NLN = 4
LN_BANK = (6, 0, 0, 0)
LN_EPS, RMS_EPS = 1e-5, 1e-6
SETUP = 18
Q_PARTS, K_PARTS = (0, 0, 1, 0, 1, 2), (0, 1, 0, 2, 1, 0)
BASE = 8
LEVELS = [8, 16, 32]


def columns():
    widths = dict(
        wqkv=NT * 128, convw=NT * KSZ, wz=1024, wab=48, dtb=1, alog=1, normw=1, wout=8 * 128,
        gate=E, fc1=E * 256, fc1b=E * 2, gm=E, fc2=E * 128, fc2b=128, sfc1=512, sfc1b=4, sgm=2,
        sfc2=256, sfc2b=1, wq=128, wk=128, wv=128, wo=128, bq=1, bk=1, bv=1, bo=1,
        nw=1, nb=1, qw=128, kw=128, vw=128, ow=128, qb=1, kb=1, vb=128, ob=1,
        ident=128, mean=128, masks=128 * len(LEVELS), same8=128, blk8=8, blk16=16, diag8=64, delta8=8,
        identc=64, half=2, sel=32, onehot=256,
        lneps=1, lneps2=1, rmseps=1, pads=5)
    at, n = {}, 0
    for name, w in widths.items():
        at[name] = (n, w)
        n += w
    return at, n


def build(nc, x_in, pack, out):
    at, npack = columns()
    with ExitStack() as ctx:
        def sb(name, shape, dt=F32):
            return ctx.enter_context(nc.sbuf_tensor(name, shape, dt))

        class Signal:

            def __init__(self, name, per, credit=0):
                self.sem, self.per, self.credit = ctx.enter_context(nc.semaphore(name)), per, credit

            def at(self, i, k):
                return i * self.per + (k + self.credit)

        W = sb("W", [128, npack])

        def w(name, lo=0, hi=None, p0=0, p1=128):
            o, n = at[name]
            return W[p0:p1, o + lo:o + (n if hi is None else hi)]

        x = sb("x", [128, S])
        x0 = sb("x0", [128, S])
        xn = sb("xn", [128, S])
        xc = sb("xc", [128, S])
        sq = sb("sq", [128, S])
        sd = sb("sd", [128, 2, 4])
        u = sb("u", [128, S])
        expA = sb("expA", [128, 1])
        owm = sb("owm", [128, NX, 128])
        obm = sb("obm", [128, NX])
        gl = sb("gl", [16, NC])
        glB = sb("glB", [128, 8, NC])
        tc = sb("tc", [128, NC, 2, 8])
        var = sb("var", [128, NC, 8])
        rstd = sb("rstd", [128, NC, 8])
        mq = sb("mq", [128, 32])
        mrow = [sb(f"mrow{g}", [16, 128], BF16) for g in range(2)]

        A = sb("arenaA", [128, 16384])
        KT = A[:, 0:2048].rearrange("a (p t) -> a p t", p=4)
        QT = A[:, 2048:4096].rearrange("a (p t) -> a p t", p=4)
        VT = A[:, 4096:8192].rearrange("a (k t) -> a k t", k=8)
        egB = A[:, 8192:12288].rearrange("a (q t) -> a q t", q=8)
        Hall = A[:, 12288:16384].rearrange("a (c n) -> a c n", c=NC)
        oT = A[:, 0:4096].rearrange("a (k t) -> a k t", k=8)
        combB = A[:, 0:E * S].rearrange("a (j t) -> a j t", j=E)
        QX = A[:, 0:4096].bitcast(BF16).rearrange("a (g t) -> a g t", g=16)
        KX = A[:, 4096:8192].bitcast(BF16).rearrange("a (g t) -> a g t", g=16)
        Rb = A[:, 8192:8704]
        QH = A[:, 12288:14336].bitcast(BF16).rearrange("a (h t) -> a h t", h=8)
        KH = A[:, 14336:16384].bitcast(BF16).rearrange("a (h t) -> a h t", h=8)
        Vflat = A[:, 4096:8192]

        def vslots(base):
            return A[:, 4096 + base:4096 + base + 576].rearrange("a (h z) -> a h z", z=144)[:, :, 0:16]

        Vp = A[:, 4096:8192].rearrange("a (k h c) -> a k h c", k=4, h=8)

        Bn = sb("arenaB", [128, 35 * 512])
        slot = [0]

        def take(n):
            slot[0] += n
            return Bn[:, 512 * (slot[0] - n):512 * slot[0]]

        Kbd, Qbd, Ktok = ([take(1).rearrange("a (p t) -> a p t", p=4) for _ in range(2)] for _ in range(3))
        Vtok, sz, Ec = ([take(1) for _ in range(2)] for _ in range(3))
        P = [take(2).rearrange("a (q t) -> a q t", q=8) for _ in range(2)]
        KQc = take(1).rearrange("a (p q t) -> a p q t", p=4, q=2)
        Vc = take(1).rearrange("a (k t) -> a k t", k=8)
        LT = take(2).rearrange("a (q t) -> a q t", q=8)
        d1, EGc, R, Y, Yd, Ot, rhs8, St, Lc = (take(1) for _ in range(9))
        hsq = sb("hsq", [128, S])
        M8 = Yd
        xch = sb("xch", [128, C])
        An = sb("An", [128, 8, BASE, BASE + 1])
        X8 = sb("X8", [128, 8, BASE + 1])
        Xd = sb("Xd", [128, 8, BASE])
        prod = sb("prod", [128, 8, BASE])
        tail = slot[0]
        T = take(2).rearrange("a (q t) -> a q t", q=8)
        Z = take(2).rearrange("a (q t) -> a q t", q=8)
        Wm = take(2).rearrange("a (q t) -> a q t", q=8)
        nslots = slot[0]
        slot[0] = tail
        ta, tna, tw, tu, tl, td = (take(1) for _ in range(6))
        ybuf = Vtok + sz
        RT = LT[:, 0:4].rearrange("a q t -> a (q t)")
        EG = LT[:, 4:8].rearrange("a q t -> a (q t)")
        EGm, D1 = R, Y
        assert nslots <= 35, nslots
        slot[0] = 0
        glu = [take(1) for _ in range(3)]
        hid = [take(1) for _ in range(3)]
        act = [take(1) for _ in range(3)]
        combT = take(1)
        lg, scp, rep, pk = (take(1) for _ in range(4))
        lg, scp, rep, pk = (t[:, 0:80].rearrange("a (t e) -> a t e", t=4) for t in (lg, scp, rep, pk))
        small = take(1)
        m8 = small[:, 0:32].rearrange("a (t e) -> a t e", t=4)
        tr8 = small[:, 32:64].rearrange("a (t e) -> a t e", t=4)
        mx4, sm4, rc4 = small[:, 64:68], small[:, 68:72], small[:, 72:76]
        slot[0] = 0
        qs, ks, vT, r1, att = (take(1) for _ in range(5))
        qsp = [take(1)[:, 0:256].bitcast(BF16) for _ in range(3)]
        ksp = [take(1)[:, 0:256].bitcast(BF16) for _ in range(3)]
        Ering = [take(1) for _ in range(4)]
        rs = take(1)
        mcol = take(1)
        zcol, zrec = mcol[:, 16:20], mcol[:, 32:36]
        ZP = take(1)[:, 0:64].rearrange("a (k e) -> a k e", k=4)
        zero = take(1)
        slot[0] += 1
        recips = rs, mcol
        QXe = [take(1)[:, 0:256].bitcast(BF16) for _ in range(2)]
        KXe = [take(1)[:, 0:256].bitcast(BF16) for _ in range(2)]

        ps = [ctx.enter_context(nc.psum_tensor(f"bank{i}", [128, 512], F32)) for i in range(8)]

        def pair(i, q):
            return ps[i + q // 4][:, 128 * (q % 4):128 * (q % 4) + 128]

        eg_d = nc.dram_tensor("eg_scratch", [16, S], F32, kind="Internal").ap()
        gl_d = nc.dram_tensor("gl_scratch", [16, NC], F32, kind="Internal").ap()
        cb_d = nc.dram_tensor("comb_scratch", [E, S], F32, kind="Internal").ap()
        part_d = nc.dram_tensor("parts_scratch", [6, 128, S], BF16, kind="Internal").ap()
        max_d = nc.dram_tensor("max_scratch", [32, 128], BF16, kind="Internal").ap()
        r_d = nc.dram_tensor("rowsum_scratch", [16, S], F32, kind="Internal").ap()

        pack_in = Signal("pack_in", 0)
        setup = Signal("setup", 0)
        x_in_s = Signal("x_loaded", 16)
        y_out = Signal("y_stored", 16, 16)
        ln_pe, ln_dve, ln_act = Signal("ln_pe", 3 * NLN), Signal("ln_dve", 3 * NLN), Signal("ln_act", 2 * NLN)
        qkv_mm = Signal("qkv_mm", NT)
        tap0 = Signal("conv_tap0", NT)
        taps = Signal("conv_taps", 3 * NT)
        conv = Signal("conv_done", NT)
        ab_mm = Signal("ab_mm", 1)
        g_act, g_dve = Signal("gates_act", 4), Signal("gates_dve", 17)
        gamma_ok = Signal("gamma_ready", 1)
        gl_dma, eg_dma = Signal("gl_dma", 48), Signal("eg_dma", 48)
        tc_mm, tc_ok = Signal("tokcols_mm", 1), Signal("tokcols_ready", 1)
        s0, bd0 = Signal("state_zero", 1), Signal("blocks_zeroed", 2)
        c_cp = Signal("chunk_copied", 7)
        eg_cp = Signal("chunk_decays_copied", 1)
        c_d1 = Signal("chunk_beta_diag", 1)
        kq_mm, kt_mm, vt_mm, z_mm = (Signal(n, 1, 1) for n in ("kq_mm", "ktok_mm", "vtok_mm", "z_mm"))
        e_ok = Signal("decay_ready", 1, 1)
        lc_ok, p_dve = Signal("l_compact", 1), Signal("p_ready", 2)
        lt_ok = Signal("lt_ready", 2)
        m8_ok = Signal("l_blocks", 3)
        a8_mm, a8_ev = Signal("l_blocks_spread", 1), Signal("l_blocks_ready", 1)
        x8_ok, z8_ok = Signal("substitution", 2 * (BASE - 1)), Signal("z8_ready", 1)
        kv_ev = Signal("ktok_vtok_ready", 2)
        sz_ok = Signal("silu_z_ready", 1)
        t8_mm = Signal("t8_mm", 2)
        x_mm, w_ev = Signal("level_x_mm", 6, 6), Signal("level_w_ready", 6)
        tz_mm, t_ev, z_ev = Signal("level_tz_mm", 6), Signal("level_t_ready", 6, 6), Signal("level_z_ready", 6, 6)
        ks_mm, qs_mm = Signal("ks_mm", 1), Signal("qs_mm", 1, 2)
        r_dve = Signal("r_dve", 2)
        y_mm, y_ev, yd_ok = Signal("y_mm", 2, 2), Signal("y_ready", 2), Signal("yd_ready", 1)
        o_mm, o_dve = Signal("o_mm", 2), Signal("o_dve", 4, 4)
        s_mm, s_dve = Signal("state_mm", 1), Signal("state_dve", 2, 2)
        hq_ok, var_ok = Signal("h_squared", 1), Signal("var_ready", 1, 1)
        n_sd, n_rs = Signal("rms_sqrt", 1), Signal("rms_recip", 1)
        hn_ok, ot_mm, ot_ev = Signal("h_normed", NC), Signal("o_turned", NC), Signal("o_turned_ready", NC)
        op_mm = Signal("out_proj", 1)
        xr = Signal("x_updated", 3)
        gt_mm, gt_act, gt_dve = Signal("gate_mm", 1), Signal("gate_exp", 1), Signal("gate_dve", 18)
        ct_mm = Signal("comb_turned", 1)
        cb_dma, cb_in = Signal("comb_stored", 16), [Signal(f"comb_in{k}", 16) for k in range(3)]
        f1_mm, f_act, f_dve = (Signal(n, NE) for n in ("fc1_mm", "gelu_ready", "hidden_ready"))
        f_pool = Signal("weighted", E)
        f2_mm = Signal("fc2_mm", NE)
        a_mm, a_dve, a_act = Signal("attn_proj_mm", 3), Signal("attn_split", 12), Signal("attn_v", 1)
        a_wr, b_wr = ([Signal(f"{l}_part{i}_stored", 16) for i in range(6)] for l in "ab")
        a_dma = Signal("attn_spread", 12 * 16)
        a_kx = Signal("a_qk_copied", 4)
        a_s, a_m, a_e = Signal("a_scores", 8, 8), Signal("a_min", 8), Signal("a_exp", 8, 4)
        a_z, a_zp, a_r = Signal("a_recip", 8), Signal("a_cols", 8), Signal("a_rowsum", 8, 4)
        a_sum = Signal("a_sum_mm", 1)
        a_rs, a_rd, a_at, a_wo = Signal("a_sum_ready", 1), Signal("a_sum_dma", 32), Signal("a_out", 1), Signal("a_wo", 1)
        b_xn = Signal("nested_affine", 2)
        b_mm, b_dve, b_pool, b_v = Signal("b_proj_mm", 3), Signal("b_split", 12), Signal("b_vpad", 3), Signal("b_v_ready", 4)
        b_dma = Signal("b_spread", 12 * 16)
        b_s, b_m = Signal("b_scores", 32), Signal("b_min", 32)
        b_tr, b_row, b_rdma = Signal("b_max_turned", 2), Signal("b_max_row", 2), Signal("b_max_dma", 64)
        b_st, b_e, b_pv = Signal("b_scores_t", 32), Signal("b_exp", 32), Signal("b_pv", 32)
        b_rc, b_at = Signal("b_recip", 2), Signal("b_out", 2)
        b_wo = Signal("b_wo", 1)
        fin = Signal("final", 3, 3)
        zero_ok = Signal("zero_ready", 1)
        passed = Signal("passed", 0)

        block = ctx.enter_context(nc.Block())

        def hold(eng):
            eng.sem_inc(passed.sem, 1)

        def spread(eng, b, t, split, wrote, sent, dst, width):
            parts, order = ((qsp, Q_PARTS), (ksp, K_PARTS))[t]
            for part in range(3):
                eng.wait_ge(split.sem, split.at(b, 6 * t + 2 * part + 2))
                eng.dma_start(part_d[3 * t + part, :, :], parts[part]).then_inc(wrote[3 * t + part].sem, 16)
            for part in range(3):
                eng.wait_ge(wrote[3 * t + part].sem, wrote[3 * t + part].at(b, 16))
                src = part_d[3 * t + part, :, :].rearrange("(g x) t -> x g t", x=width)
                for i in range(6):
                    if order[i] == part:
                        eng.dma_start(dst[width * i:width * i + width, :, :], src).then_inc(sent.sem, 16)

        @block.sync
        def _(sp):
            half = npack // 2
            sp.dma_start(W[:, 0:half], pack[:, 0:half]).then_inc(pack_in.sem, 16)
            sp.dma_start(W[:, half:npack], pack[:, half:npack]).then_inc(pack_in.sem, 16)
            def gate_rows(b):
                sp.wait_ge(g_dve.sem, g_dve.at(b, 16))
                sp.dma_start(eg_d, EGm[0:16, :]).then_inc(eg_dma.sem, 16)
                sp.wait_ge(g_dve.sem, g_dve.at(b, 17))
                sp.dma_start(gl_d, gl[:, :]).then_inc(gl_dma.sem, 16)
                sp.wait_ge(eg_dma.sem, eg_dma.at(b, 16))
                for e in range(2):
                    sp.dma_start(egB[64 * e:64 * e + 64, :, :],
                                 eg_d[8 * e:8 * e + 8, :].unsqueeze(0).broadcast_to([64, 8, S])
                                 ).then_inc(eg_dma.sem, 16)
                sp.wait_ge(gl_dma.sem, gl_dma.at(b, 16))
                for e in range(2):
                    sp.dma_start(glB[64 * e:64 * e + 64, :, :],
                                 gl_d[8 * e:8 * e + 8, :].unsqueeze(0).broadcast_to([64, 8, NC])
                                 ).then_inc(gl_dma.sem, 16)

            def sequence(b, follow):
                if follow:
                    sp.wait_ge(xr.sem, xr.at(b, 1))
                    sp.dma_start(x0[:, :], x_in[bass.ds(b + 1, 1), :, :].rearrange("b a t -> (b a) t")).then_inc(x_in_s.sem, 16)
                else:
                    sp.wait_ge(xr.sem, xr.at(b, 1))
                    sp.sem_inc(x_in_s.sem, 16)
                sp.wait_ge(gt_dve.sem, gt_dve.at(b, 18))
                sp.dma_start(cb_d, combT[0:E, :]).then_inc(cb_dma.sem, 16)
                sp.wait_ge(cb_dma.sem, cb_dma.at(b, 16))
                for k in range(3):
                    sp.dma_start(combB[:, 5 * k:5 * k + 5, :],
                                 cb_d[5 * k:5 * k + 5, :].unsqueeze(0).broadcast_to([128, 5, S])
                                 ).then_inc(cb_in[k].sem, 16)
                sp.wait_ge(f2_mm.sem, f2_mm.at(b, NE))
                spread(sp, b, 0, a_dve, a_wr, a_dma, QX[0:48, :, :], 8)
                sp.wait_ge(a_rs.sem, a_rs.at(b, 1))
                sp.dma_start(r_d.rearrange("g (e t) -> e g t", e=16),
                             rs[0:16, :].rearrange("a (g t) -> a g t", g=16)).then_inc(a_rd.sem, 16)
                sp.wait_ge(a_rd.sem, a_rd.at(b, 16))
                sp.dma_start(Rb, r_d.unsqueeze(1).broadcast_to([16, 8, S])).then_inc(a_rd.sem, 16)
                spread(sp, b, 0, b_dve, b_wr, b_dma, QH[0:96, :, :], 16)
                for g in range(2):
                    sp.wait_ge(b_row.sem, b_row.at(b, g + 1))
                    sp.dma_start(max_d[16 * g:16 * g + 16, :], mrow[g][:, :]).then_inc(b_rdma.sem, 16)
                    sp.wait_ge(b_rdma.sem, b_rdma.at(b, 32 * g + 16))
                    sp.dma_start(QH[96:97, 4 * g:4 * g + 4, :].rearrange("a h t -> a (h t)"),
                                 max_d[16 * g:16 * g + 16, :].rearrange("q t -> (q t)").unsqueeze(0)).then_inc(b_rdma.sem, 16)
                sp.wait_ge(fin.sem, fin.at(b, 3))
                sp.dma_start(out[b, :, :], x[:, :]).then_inc(y_out.sem, 16)
                if follow:
                    gate_rows(b + 1)

            sp.sem_inc(y_out.sem, y_out.credit)
            sp.dma_start(x0[:, :], x_in[0, :, :]).then_inc(x_in_s.sem, 16)
            gate_rows(0)
            with sp.Fori(0, B - 1) as b:
                sequence(b, True)
            sequence(B - 1, False)
            sp.wait_ge(y_out.sem, y_out.at(B - 1, 16))

        @block.tensor
        def _(pe):
            def keep_warm(n):
                for _ in range(n):
                    pe.matmul(ps[5][:, :], w("ident"), w("wqkv", 0, 512), start=True, stop=True)

            def mean(b, i):
                pe.matmul(ps[LN_BANK[i]][:, :], w("mean"), (x0, x, x, x)[i][:, :], start=True, stop=True).then_inc(ln_pe.sem, 1)

            def variance(b, i):
                pe.wait_ge(ln_act.sem, ln_act.at(b, 2 * i + 1))
                for t in range(4):
                    mm = pe.matmul(ps[LN_BANK[i] + 1][:, t:t + 1], sq[:, 128 * t:128 * t + 128], w("mean", 0, 1),
                                   start=True, stop=True)
                mm.then_inc(ln_pe.sem, 1)

            def spread_scale(b, i):
                pe.wait_ge(ln_dve.sem, ln_dve.at(b, 3 * i + 2))
                for k in range(2 if i == NLN - 1 else 1):
                    for t in range(4):
                        mm = pe.matmul(ps[LN_BANK[i] + 1 - k][:, 128 * t:128 * t + 128],
                                       sd[:, k, t:t + 1].broadcast_to([128, 128]), w("ident"), start=True, stop=True)
                mm.then_inc(ln_pe.sem, 1)

            def layer_norm(b, i):
                mean(b, i)
                keep_warm(1)
                variance(b, i)
                keep_warm(1)
                spread_scale(b, i)
                keep_warm(0)

            def gates_in(b):
                pe.wait_ge(ln_dve.sem, ln_dve.at(b, 3))
                pe.matmul(ps[6][0:48, :], w("wab"), xn[:, :], start=True, stop=True).then_inc(ab_mm.sem, 1)

            def qkv(b, t):
                if t >= 4:
                    pe.wait_ge(taps.sem, taps.at(b, 6 * ((t - 4) // 2) + 5 + t % 2))
                pe.matmul(ps[t % 4][:, :], w("wqkv", 128 * t, 128 * t + 128), xn[:, :],
                          start=True, stop=True).then_inc(qkv_mm.sem, 1)

            pe.wait_ge(pack_in.sem, 32)
            pe.wait_ge(setup.sem, SETUP)
            for sig in (y_mm, qs_mm, kq_mm, kt_mm, vt_mm, z_mm, x_mm):
                pe.sem_inc(sig.sem, sig.credit)
            pe.sem_inc(a_r.sem, 4)
            pe.sem_inc(a_s.sem, 8)
            pe.wait_ge(x_in_s.sem, x_in_s.at(0, 16))
            layer_norm(0, 0)
            gates_in(0)
            for t in range(4):
                qkv(0, t)
            with pe.Fori(0, B) as b:
                def front_kq(n, par):
                    pe.wait_ge(c_cp.sem, c_cp.at(n, 4))
                    pe.wait_ge(t_ev.sem, t_ev.at(n - 1, 6))
                    for p in range(4):
                        mm = pe.matmul(ps[6][:, 128 * p:128 * p + 128], Kbd[par][:, p, :],
                                       KQc[:, p, :, :], start=True, stop=True)
                    mm.then_inc(kq_mm.sem, 1)
                    for p in range(4):
                        mm = pe.transpose(ps[7][:, 128 * p:128 * p + 128], Kbd[par][:, p, :], w("ident"))
                    mm.then_inc(kt_mm.sem, 1)

                def front_zv(n):
                    pe.wait_ge(c_cp.sem, c_cp.at(n, 7))
                    pe.wait_ge(o_dve.sem, o_dve.at(n - 1, 1))
                    for e in range(2):
                        mm = pe.matmul(ps[3][64 * e:64 * e + 64, :], xch[:, :], w("wz", 512 * e, 512 * e + 512),
                                       start=True, stop=True)
                    mm.then_inc(z_mm.sem, 1)
                    pe.wait_ge(z_ev.sem, z_ev.at(n - 1, 6))
                    for p in range(4):
                        mm = pe.transpose(ps[1][:, 128 * p:128 * p + 128], Vc[:, 2 * p:2 * p + 2, :], w("ident"))
                    mm.then_inc(vt_mm.sem, 1)

                def spread_blocks(n):
                    pe.wait_ge(m8_ok.sem, m8_ok.at(n, 3))
                    pe.wait_ge(z_ev.sem, z_ev.at(n - 1, 5))
                    pe.matmul(ps[0][:, :], w("same8"), rhs8, start=True, stop=True).then_inc(a8_mm.sem, 1)

                def inverse(n, par=None):
                    pe.wait_ge(z8_ok.sem, z8_ok.at(n, 1))
                    for q in range(8):
                        mm = pe.transpose(pair(4, q), Z[:, q, :], w("ident"))
                        if q % 4 == 3:
                            mm.then_inc(t8_mm.sem, 1)
                    pe.wait_ge(lt_ok.sem, lt_ok.at(n, 2))
                    for k, s in enumerate(LEVELS):
                        for h in range(2):
                            pe.wait_ge(t_ev.sem, t_ev.at(n, 2 * k + h + 1))
                            for q in range(4 * h, 4 * h + 4):
                                mm = pe.matmul(pair(4, q), LT[:, q, :], T[:, q, :], start=True, stop=True)
                            mm.then_inc(x_mm.sem, 1)
                        if s == LEVELS[-1] and par is not None:
                            front_kq(n + 1, par)
                        for h in range(2):
                            pe.wait_ge(w_ev.sem, w_ev.at(n, 2 * k + h + 1))
                            if k == 0:
                                pe.wait_ge(kv_ev.sem, kv_ev.at(n, 2))
                                pe.wait_ge(o_dve.sem, o_dve.at(n - 1, 3))
                            else:
                                pe.wait_ge(z_ev.sem, z_ev.at(n, 2 * k + h - 1))
                            if s < LEVELS[-1]:
                                for q in range(4 * h, 4 * h + 4):
                                    pe.matmul(pair(6, q), Z[:, q, :], Wm[:, q, :], start=True, stop=True)
                            for q in range(4 * h, 4 * h + 4):
                                mm = pe.matmul(pair(0, q), Wm[:, q, :], Z[:, q, :], start=True, stop=True)
                            mm.then_inc(tz_mm.sem, 1)

                def state_in(n, par):
                    pe.wait_ge(s_dve.sem, s_dve.at(n - 1, 2))
                    pe.wait_ge(s0.sem, s0.at(b, 1))
                    for p in range(4):
                        mm = pe.matmul(ps[2][:, 128 * p:128 * p + 128], Kbd[par][:, p, :],
                                       St[:, 128 * p:128 * p + 128], start=True, stop=True)
                    mm.then_inc(ks_mm.sem, 1)
                    pe.wait_ge(sz_ok.sem, sz_ok.at(n, 1))
                    for p in range(4):
                        mm = pe.matmul(ps[3][:, 128 * p:128 * p + 128], Qbd[par][:, p, :],
                                       St[:, 128 * p:128 * p + 128], start=True, stop=True)
                    mm.then_inc(qs_mm.sem, 1)

                def solve(n):
                    pe.wait_ge(r_dve.sem, r_dve.at(n, 2))
                    pe.wait_ge(z_ev.sem, z_ev.at(n, 6))
                    for q in range(8):
                        mm = pe.matmul(pair(4, q), Z[:, q, :], R[:, 128 * (q // 2):128 * (q // 2) + 128],
                                       start=True, stop=True)
                        if q % 4 == 3:
                            mm.then_inc(y_mm.sem, 1)

                def outputs(n, par, more=True):
                    if more:
                        pe.wait_ge(p_dve.sem, p_dve.at(n + 1, 2))
                        pe.wait_ge(kv_ev.sem, kv_ev.at(n + 1, 1))
                    pe.wait_ge(y_ev.sem, y_ev.at(n, 2))
                    for q in range(8):
                        mm = pe.matmul(pair(6, q), P[par][:, q, :], Y[:, 128 * (q // 2):128 * (q // 2) + 128],
                                       start=True, stop=True)
                        if q % 4 == 3:
                            mm.then_inc(o_mm.sem, 1)
                    pe.wait_ge(yd_ok.sem, yd_ok.at(n, 1))
                    for p in range(4):
                        mm = pe.matmul(ps[2][:, 128 * p:128 * p + 128], Ktok[par][:, p, :],
                                       Yd[:, 128 * p:128 * p + 128], start=True, stop=True)
                    mm.then_inc(s_mm.sem, 1)

                def step(n, par, more=True):
                    state_in(n, par)
                    spread_blocks(n + 1)
                    solve(n)
                    front_zv(n + 1)
                    outputs(n, par)
                    inverse(n + 1, par if more else None)

                n0 = b * NC
                for t in range(4, NT):
                    qkv(b, t)
                    if t == 5:
                        pe.wait_ge(g_dve.sem, g_dve.at(b, 17))
                        for c in range(NC):
                            for e in range(2):
                                mm = pe.matmul(ps[7][64 * e:64 * e + 64, 16 * c:16 * c + 16],
                                               RT[:, C * c:C * c + C], w("sel", 16 * e, 16 * e + 16),
                                               start=True, stop=True)
                        mm.then_inc(tc_mm.sem, 1)
                    if t == 13:
                        pe.wait_ge(tc_ok.sem, tc_ok.at(b, 1))
                        front_kq(n0, 0)
                spread_blocks(n0)
                front_zv(n0)
                inverse(n0, 1)
                with pe.Fori(0, NC // 2 - 1) as c2:
                    for par in range(2):
                        step(n0 + c2 * 2 + par, par)
                step(n0 + (NC - 2), 0, more=False)
                state_in(n0 + (NC - 1), 1)
                solve(n0 + (NC - 1))
                outputs(n0 + (NC - 1), 1, more=False)
                for c in range(NC):
                    pe.wait_ge(hn_ok.sem, hn_ok.at(b, c + 1))
                    if c >= 2:
                        pe.wait_ge(ot_ev.sem, ot_ev.at(b, c - 1))
                    for p in range(4):
                        mm = pe.transpose(ps[2 + c % 2][:, 128 * p:128 * p + 128], Hall[:, c, 128 * p:128 * p + 128],
                                          w("ident"))
                    mm.then_inc(ot_mm.sem, 1)
                pe.wait_ge(ot_ev.sem, ot_ev.at(b, NC))
                for k in range(8):
                    mm = pe.matmul(ps[4][:, :], w("wout", 128 * k, 128 * k + 128), oT[:, k, :],
                                   start=(k == 0), stop=(k == 7))
                mm.then_inc(op_mm.sem, 1)
                keep_warm(1)
                pe.wait_ge(xr.sem, xr.at(b, 1))
                layer_norm(b, 1)
                pe.wait_ge(ln_dve.sem, ln_dve.at(b, 6))
                for t in range(4):
                    mm = pe.matmul(ps[6][:, 16 * t:16 * t + E], xn[:, 128 * t:128 * t + 128], w("gate"),
                                   start=True, stop=True)
                mm.then_inc(gt_mm.sem, 1)

                def fc1(j):
                    k = j % 3
                    if j >= 3:
                        pe.wait_ge(f_act.sem, f_act.at(b, j - 2))
                        pe.wait_ge(f_dve.sem, f_dve.at(b, j - 2))
                    if j < 2:
                        wx, wg = w("sfc1", 128 * j, 128 * j + 128), w("sfc1", 256 + 128 * j, 384 + 128 * j)
                    else:
                        o = 256 * (j - 2)
                        wx, wg = w("fc1", o, o + 128), w("fc1", o + 128, o + 256)
                    pe.matmul(ps[2 * k][:, :], wx, xn[:, :], start=True, stop=True)
                    pe.matmul(ps[2 * k + 1][:, :], wg, xn[:, :], start=True, stop=True).then_inc(f1_mm.sem, 1)

                def fc2(j):
                    if j < 2:
                        pe.wait_ge(f_dve.sem, f_dve.at(b, j + 1))
                    else:
                        pe.wait_ge(f_pool.sem, f_pool.at(b, j - 1))
                    lhs = w("sfc2", 128 * j, 128 * j + 128) if j < 2 else w("fc2", 128 * (j - 2), 128 * (j - 1))
                    pe.matmul(ps[7][:, :], lhs, (hid if j < 2 else act)[j % 3], start=(j == 0), stop=(j == NE - 1)).then_inc(f2_mm.sem, 1)

                fc1(0)
                fc1(1)
                fc1(2)
                fc2(0)
                fc2(1)
                pe.wait_ge(gt_dve.sem, gt_dve.at(b, 17))
                for t in range(4):
                    mm = pe.transpose(ps[6][0:E, 128 * t:128 * t + 128], lg[:, t, 0:E], w("ident"))
                mm.then_inc(ct_mm.sem, 1)
                pe.wait_ge(gt_dve.sem, gt_dve.at(b, 18))
                pe.matmul(ps[7][:, :], w("fc2b", p1=E), combT[0:E, :], start=False, stop=False)
                for j in range(3, NE):
                    fc1(j)
                    if j >= 4:
                        fc2(j - 2)
                fc2(NE - 2)
                fc2(NE - 1)
                keep_warm(1)
                pe.wait_ge(xr.sem, xr.at(b, 2))
                layer_norm(b, 2)
                pe.wait_ge(ln_dve.sem, ln_dve.at(b, 9))
                for k, name in enumerate(("wq", "wk", "wv")):
                    pe.matmul(ps[2 + k][:, :], w(name), xn[:, :], start=True, stop=True).then_inc(a_mm.sem, 1)
                keep_warm(12)
                pe.wait_ge(a_dma.sem, a_dma.at(b, 12 * 16))
                pe.wait_ge(a_dve.sem, a_dve.at(b, 12))
                pe.wait_ge(a_act.sem, a_act.at(b, 1))
                pe.wait_ge(zero_ok.sem, zero_ok.at(b, 1))
                pe.matmul(ps[4][0:16, :], zero[:, 0:16], xn[:, :], start=True, stop=False, skip_group_check=True)

                def score(n, k):
                    if k % 4 == 0:
                        pe.wait_ge(a_kx.sem, a_kx.at(n, k // 2 + 2))
                    pe.wait_ge(a_e.sem, a_e.at(n, k - 3))
                    h = k // 4 % 2
                    pe.matmul(ps[k % 4][:, :], KXe[h][0:48, 128 * (k % 4):128 * (k % 4) + 128],
                              QXe[h][0:48, :], start=True, stop=True).then_inc(a_s.sem, 1)

                def row_sum(n, k):
                    pe.wait_ge(a_e.sem, a_e.at(n, k + 1))
                    pe.wait_ge(a_zp.sem, a_zp.at(n, k + 1))
                    pe.matmul(ps[4][0:16, :], ZP[:, k % 4, :], Ering[k % 4], start=False, stop=False,
                              skip_group_check=True).then_inc(a_r.sem, 1)

                n1 = b * (H1 // 2)
                for k in range(3):
                    score(n1, k)
                with pe.Fori(0, H1 // 2 - 1) as e2:
                    for k in range(8):
                        score(n1 + e2, k + 3)
                        row_sum(n1 + e2, k)
                for k in range(8):
                    if k < 5:
                        score(n1 + (H1 // 2 - 1), k + 3)
                    row_sum(n1 + (H1 // 2 - 1), k)
                pe.matmul(ps[4][0:16, :], zero[:, 0:16], xn[:, :], start=False, stop=True,
                          skip_group_check=True).then_inc(a_sum.sem, 1)
                keep_warm(6)
                pe.wait_ge(a_at.sem, a_at.at(b, 1))
                pe.matmul(ps[5][:, :], w("wo"), att, start=True, stop=True).then_inc(a_wo.sem, 1)
                pe.wait_ge(xr.sem, xr.at(b, 3))
                layer_norm(b, 3)
                pe.wait_ge(b_xn.sem, b_xn.at(b, 1))
                for k, name in enumerate(("qw", "kw")):
                    for e in range(NX):
                        m = D >> e
                        mm = pe.matmul(ps[2 + k][:, 128 * e:128 * e + 128], w(name, p1=m),
                                       xn[0:m, 128 * e:128 * e + 128], start=True, stop=True)
                    mm.then_inc(b_mm.sem, 1)
                for e in range(NX):
                    m = D >> e
                    mm = pe.matmul(ps[4][:, 128 * e:128 * e + 128], xn[0:m, 128 * e:128 * e + 128],
                                   w("vw", p1=m), start=True, stop=True)
                mm.then_inc(b_mm.sem, 1)
                keep_warm(10)
                pe.wait_ge(b_dma.sem, b_dma.at(b, 12 * 16))
                pe.wait_ge(b_dve.sem, b_dve.at(b, 12))
                pe.wait_ge(b_v.sem, b_v.at(b, 4))
                def negated(i):
                    h, q = i // 4, i % 4
                    if i >= 2:
                        pe.wait_ge(b_m.sem, b_m.at(b, i - 1))
                    pe.matmul(ps[2 + i % 2][:, :], QH[0:96, h, 128 * q:128 * q + 128], KH[0:96, h, :],
                              start=True, stop=True).then_inc(b_s.sem, 1)

                def turn(g):
                    pe.wait_ge(b_m.sem, b_m.at(b, 16 * g + 16))
                    pe.transpose(ps[7][0:16, 128 * g:128 * g + 128], mq[:, 16 * g:16 * g + 16],
                                 w("ident")).then_inc(b_tr.sem, 1)

                for i in range(16):
                    negated(i)
                negated(16)
                turn(0)
                negated(17)
                pe.wait_ge(b_rdma.sem, b_rdma.at(b, 32))
                pe.wait_ge(b_pool.sem, b_pool.at(b, 3))

                def pv(i):
                    h, k = i // 4, i % 4
                    pe.wait_ge(b_e.sem, b_e.at(b, i + 1))
                    pe.matmul(ps[4 + h // 4][:, :], Vp[:, k, h, :], Ering[i % 4], start=(i % 16 == 0),
                              stop=(i % 16 == 15)).then_inc(b_pv.sem, 1)

                for i in range(32):
                    h, k = i // 4, i % 4
                    if i == 16:
                        pe.wait_ge(b_rdma.sem, b_rdma.at(b, 64))
                    if i >= 2:
                        pe.wait_ge(b_e.sem, b_e.at(b, i - 1))
                    pe.matmul(ps[i % 2][:, :], KH[0:97, h, 128 * k:128 * k + 128], QH[0:97, h, :],
                              start=True, stop=True).then_inc(b_st.sem, 1)
                    if i < 7:
                        negated(18 + 2 * i)
                    if i >= 2:
                        pv(i - 2)
                    if i < 7:
                        negated(19 + 2 * i)
                    if i == 8:
                        turn(1)
                    if i == 11:
                        pe.wait_ge(x_in_s.sem, x_in_s.at(b + 1, 16))
                        mean(b + 1, 0)
                    if i == 15:
                        pe.wait_ge(b_row.sem, b_row.at(b, 2))
                        variance(b + 1, 0)
                    if i == 17:
                        spread_scale(b + 1, 0)
                    if i == 20:
                        gates_in(b + 1)
                pv(30)
                pv(31)
                for t in range(4):
                    qkv(b + 1, t)
                pe.wait_ge(b_at.sem, b_at.at(b, 2))
                for e in range(NX):
                    m = D >> e
                    mm = pe.matmul(ps[4][:, 128 * e:128 * e + 128], owm[0:m, e, :], att[0:m, 128 * e:128 * e + 128],
                                   start=True, stop=True)
                mm.then_inc(b_wo.sem, 1)

        @block.scalar
        def _(sc):
            def squares(b, i):
                sc.wait_ge(ln_dve.sem, ln_dve.at(b, 3 * i + 1))
                sc.activation(sq[:, :], xc[:, :], ACT.Square).then_inc(ln_act.sem, 1)

            def deviation(b, i):
                sc.wait_ge(ln_pe.sem, ln_pe.at(b, 3 * i + 2))
                v = ps[LN_BANK[i] + 1][:, 0:4]
                if i == NLN - 1:
                    sc.activation(sd[:, 0, :], v, ACT.Sqrt, bias=w("lneps2"), scale=1.0 + LN_EPS)
                sc.activation(sd[:, i // (NLN - 1), :], v, ACT.Sqrt, bias=w("lneps")).then_inc(ln_act.sem, 1)

            def layer_norm(b, i):
                squares(b, i)
                deviation(b, i)

            def gate_beta(b):
                sc.wait_ge(ab_mm.sem, ab_mm.at(b, 1))
                sc.activation(td[32:48, :], ps[6][32:48, :], ACT.Exp, scale=-1.0).then_inc(g_act.sem, 1)

            def gate_exp(b):
                sc.wait_ge(g_dve.sem, g_dve.at(b, 5))
                sc.activation(tw[0:16, :], tna[0:16, :], ACT.Exp, scale=-1.0).then_inc(g_act.sem, 1)

            def gate_log(b):
                sc.wait_ge(g_dve.sem, g_dve.at(b, 6))
                sc.activation(tl[0:16, :], tu[0:16, :], ACT.Ln).then_inc(g_act.sem, 1)

            def gate_decay(b):
                sc.wait_ge(g_dve.sem, g_dve.at(b, 12))
                sc.activation(EG[0:16, :], tna[0:16, :], ACT.Exp, scale=-1.0).then_inc(g_act.sem, 1)

            def first_tap(b, t):
                sc.wait_ge(qkv_mm.sem, qkv_mm.at(b, t + 1))
                if t >= 4:
                    sc.wait_ge(conv.sem, conv.at(b, t - 3))
                sc.activation(ybuf[t % 4], ps[t % 4][:, :], ACT.Identity,
                              scale=w("convw", KSZ * t + 3, KSZ * t + 4)).then_inc(tap0.sem, 1)


            sc.wait_ge(pack_in.sem, 32)
            sc.wait_ge(setup.sem, SETUP - 1)
            sc.activation(expA[:, :], expA[:, :], ACT.Exp).then_inc(setup.sem, 1)
            sc.wait_ge(setup.sem, SETUP)
            sc.sem_inc(a_e.sem, 4)
            sc.sem_inc(z_ev.sem, 6)
            sc.sem_inc(t_ev.sem, 6)
            layer_norm(0, 0)
            gate_beta(0)
            gate_exp(0)
            gate_log(0)
            gate_decay(0)
            first_tap(0, 0)
            first_tap(0, 1)
            with sc.Fori(0, B) as b:
                def k_out(n, par):
                    sc.wait_ge(kt_mm.sem, kt_mm.at(n, 1))
                    sc.activation(Ktok[par].rearrange("a p t -> a (p t)"), ps[7][:, :], ACT.Copy).then_inc(kv_ev.sem, 1)

                def zv_out(n, par):
                    sc.wait_ge(z_mm.sem, z_mm.at(n, 1))
                    sc.activation(sz[par], ps[3][:, :], ACT.Silu).then_inc(sz_ok.sem, 1)
                    sc.wait_ge(vt_mm.sem, vt_mm.at(n, 1))
                    sc.activation(Vtok[par], ps[1][:, :], ACT.Copy).then_inc(kv_ev.sem, 1)

                def blocks_out(n):
                    sc.wait_ge(a8_mm.sem, a8_mm.at(n, 1))
                    sc.activation(An[:, :, :, 1:BASE + 1].rearrange("a q i j -> a (q i) j"),
                                  ps[0][:, :].rearrange("a (q j) -> a q j", j=BASE), ACT.Copy).then_inc(a8_ev.sem, 1)

                def y_outs(n):
                    for h in range(2):
                        sc.wait_ge(y_mm.sem, y_mm.at(n, h + 1))
                        src = ps[4 + h][:, :].rearrange("a (p r q) -> a p r q", p=2, r=2)
                        for r in range(2):
                            ev = sc.activation(
                                Y[:, 256 * h:256 * h + 256].rearrange("a (p r v) -> a p r v", p=2, r=2)[:, :, r, :],
                                src[:, :, r, 64 * r:64 * r + 64], ACT.Copy)
                            if r == 1:
                                ev.then_inc(y_ev.sem, 1)

                def squares_out(n, c):
                    sc.wait_ge(o_dve.sem, o_dve.at(n, 4))
                    sc.wait_ge(var_ok.sem, var_ok.at(n - 1, 1))
                    sc.activation(hsq[:, :], Hall[:, bass.ds(c, 1), :].rearrange("a c n -> a (c n)"),
                                  ACT.Square).then_inc(hq_ok.sem, 1)

                def inverse(n, par=None, c=None):
                    for h in range(2):
                        sc.wait_ge(t8_mm.sem, t8_mm.at(n, h + 1))
                        sc.activation(T[:, 4 * h:4 * h + 4, :].rearrange("a q t -> a (q t)"), ps[4 + h][:, :],
                                      ACT.Copy).then_inc(t_ev.sem, 1)
                    for k, s in enumerate(LEVELS):
                        if s == LEVELS[-1] and par is not None:
                            k_out(n + 1, par)
                        for h in range(2):
                            sc.wait_ge(tz_mm.sem, tz_mm.at(n, 2 * k + h + 1))
                            if s < LEVELS[-1]:
                                sc.activation(T[:, 4 * h:4 * h + 4, :].rearrange("a q t -> a (q t)"),
                                              ps[6 + h][:, :], ACT.Copy).then_inc(t_ev.sem, 1)
                            sc.activation(Z[:, 4 * h:4 * h + 4, :].rearrange("a q t -> a (q t)"),
                                          ps[h][:, :], ACT.Copy).then_inc(z_ev.sem, 1)
                        if k == 0 and c is not None:
                            squares_out(n - 1, c)

                def step(n, c, par, more=True):
                    blocks_out(n + 1)
                    y_outs(n)
                    zv_out(n + 1, 1 - par)
                    inverse(n + 1, par if more else None, c)

                n0 = b * NC
                for t in range(0, NT, 2):
                    for t1 in (t, t + 1):
                        if t + 2 < NT:
                            first_tap(b, t1 + 2)
                    for t1 in (t, t + 1):
                        sc.wait_ge(taps.sem, taps.at(b, 3 * t + 5 + t1 % 2))
                        dst = QT[:, t1, :] if t < 4 else KT[:, t1 - 4, :] if t < 8 else VT[:, t1 - 8, :]
                        sc.activation(dst, ybuf[t1 % 4], ACT.Silu).then_inc(conv.sem, 1)
                    if t == 12:
                        k_out(n0, 0)
                        blocks_out(n0)
                zv_out(n0, 0)
                inverse(n0, 1)
                with sc.Fori(0, NC // 2 - 1) as c2:
                    for par in range(2):
                        step(n0 + c2 * 2 + par, c2 * 2 + par, par)
                step(n0 + (NC - 2), NC - 2, 0, more=False)
                y_outs(n0 + (NC - 1))
                squares_out(n0 + (NC - 1), NC - 1)
                sc.wait_ge(var_ok.sem, var_ok.at(n0 + (NC - 1), 1))
                sc.activation(rstd[:, :, :], var[:, :, :], ACT.Sqrt, bias=w("rmseps"), scale=1.0 / 64).then_inc(n_sd.sem, 1)
                for c in range(NC):
                    sc.wait_ge(ot_mm.sem, ot_mm.at(b, c + 1))
                    sc.activation(oT[:, :, C * c:C * c + C],
                                  ps[2 + c % 2][:, :].rearrange("a (k t) -> a k t", k=8), ACT.Copy).then_inc(ot_ev.sem, 1)
                layer_norm(b, 1)
                sc.wait_ge(gt_dve.sem, gt_dve.at(b, 3))
                sc.activation(lg[:, :, 0:E], lg[:, :, 0:E], ACT.Exp).then_inc(gt_act.sem, 1)
                for j in range(NE):
                    sc.wait_ge(f1_mm.sem, f1_mm.at(b, j + 1))
                    if j >= 3:
                        sc.wait_ge(f_dve.sem, f_dve.at(b, j - 2))
                    bias = w("sfc1b", 2 + j, 3 + j) if j < 2 else w("fc1b", 2 * (j - 2) + 1, 2 * (j - 2) + 2)
                    sc.activation(glu[j % 3], ps[2 * (j % 3) + 1][:, :], ACT.Gelu, bias=bias).then_inc(f_act.sem, 1)
                layer_norm(b, 2)
                sc.wait_ge(a_mm.sem, a_mm.at(b, 3))
                sc.activation(vT, ps[4][:, :], ACT.Identity, bias=w("bv")).then_inc(a_act.sem, 1)
                sc.wait_ge(f2_mm.sem, f2_mm.at(b, NE))
                spread(sc, b, 1, a_dve, a_wr, a_dma, KX[0:48, :, :], 8)
                with sc.Fori(0, H1 // 2) as e2:
                    n = b * (H1 // 2) + e2
                    for k in range(8):
                        sc.wait_ge(a_m.sem, a_m.at(n, k + 1))
                        sc.wait_ge(a_r.sem, a_r.at(n, k - 3))
                        sc.activation(Ering[k % 4], ps[k % 4][:, :], ACT.Exp, bias=mcol[:, k % 4:k % 4 + 1],
                                      scale=-1.0, accum_out=zcol[:, k % 4:k % 4 + 1]).then_inc(a_e.sem, 1)
                sc.wait_ge(a_rs.sem, a_rs.at(b, 1))
                layer_norm(b, 3)
                spread(sc, b, 1, b_dve, b_wr, b_dma, KH[0:96, :, :], 16)

                def max_row(g):
                    sc.wait_ge(b_tr.sem, b_tr.at(b, g + 1))
                    sc.activation(mrow[g][:, :], ps[7][0:16, 128 * g:128 * g + 128], ACT.Copy,
                                  scale=-1.0).then_inc(b_row.sem, 1)

                max_row(0)
                for i in range(32):
                    sc.wait_ge(b_st.sem, b_st.at(b, i + 1))
                    if i >= 4:
                        sc.wait_ge(b_pv.sem, b_pv.at(b, i - 3))
                    sc.activation(Ering[i % 4], ps[i % 2][:, :], ACT.Exp, scale=-1.0).then_inc(b_e.sem, 1)
                    if i == 7:
                        max_row(1)
                    if i == 12:
                        squares(b + 1, 0)
                    if i == 16:
                        deviation(b + 1, 0)
                    if i == 22:
                        gate_beta(b + 1)
                    if i == 26:
                        gate_exp(b + 1)
                    if i == 29:
                        gate_log(b + 1)
                gate_decay(b + 1)
                first_tap(b + 1, 0)
                first_tap(b + 1, 1)

        @block.vector
        def _(ve):
            def layer_norm(b, i):
                ve.wait_ge(ln_pe.sem, ln_pe.at(b, 3 * i + 1))
                ve.tensor_tensor(xc[:, :], (x0, x, x, x)[i][:, :], ps[LN_BANK[i]][:, :], ALU.subtract).then_inc(ln_dve.sem, 1)
                ve.wait_ge(ln_act.sem, ln_act.at(b, 2 * i + 2))
                n = 2 if i == NLN - 1 else 1
                ve.reciprocal(sd[:, 0:n, :], sd[:, 0:n, :]).then_inc(ln_dve.sem, 1)
                ve.wait_ge(ln_pe.sem, ln_pe.at(b, 3 * i + 3))
                ve.tensor_tensor(xn[:, :], xc[:, :], ps[LN_BANK[i] + 1][:, :], ALU.mult).then_inc(ln_dve.sem, 1)

            ve.wait_ge(pack_in.sem, 32)
            o, _n = at["fc2"]
            fc2 = W[:, o:o + E * 128].rearrange("a (j d) -> a j d", j=E)
            ve.tensor_tensor(fc2, fc2, w("gm").unsqueeze(2).broadcast_to([128, E, 128]), ALU.mult).then_inc(setup.sem, 1)
            o, _n = at["sfc2"]
            sfc2 = W[:, o:o + 256].rearrange("a (j d) -> a j d", j=2)
            ve.tensor_tensor(sfc2, sfc2, w("sgm").unsqueeze(2).broadcast_to([128, 2, 128]), ALU.mult).then_inc(setup.sem, 1)
            ve.tensor_scalar(w("wout"), w("wout"), w("normw"), None, ALU.mult).then_inc(setup.sem, 1)
            ve.memset(owm[:, :, :], 0.0).then_inc(setup.sem, 1)
            ve.memset(obm[:, :], 0.0).then_inc(setup.sem, 1)
            ve.wait_ge(setup.sem, 5)
            for e in range(NX):
                m = D >> e
                ve.tensor_copy(owm[0:m, e, 0:m], w("ow", 0, m, 0, m)).then_inc(setup.sem, 1)
                ve.tensor_copy(obm[0:m, e:e + 1], w("ob", p1=m)).then_inc(setup.sem, 1)
            ve.tensor_scalar(expA[:, :], w("alog"), 88.0, None, ALU.min).then_inc(setup.sem, 1)
            ve.memset(X8[:, :, 0:1], 1.0).then_inc(setup.sem, 1)
            ve.tensor_copy(X8[:, :, 1], w("delta8", 0, 1).broadcast_to([128, 8])).then_inc(setup.sem, 1)
            ve.tensor_copy(An[:, :, :, 0], w("delta8").unsqueeze(1).broadcast_to([128, 8, BASE])).then_inc(setup.sem, 1)
            ve.wait_ge(setup.sem, SETUP)
            ve.sem_inc(e_ok.sem, 1)
            ve.sem_inc(o_dve.sem, 4)
            ve.sem_inc(s_dve.sem, 2)
            ve.sem_inc(fin.sem, 3)
            ve.sem_inc(var_ok.sem, 1)
            def gates_split(b):
                ve.memset(RT, 0.0).then_inc(g_dve.sem, 1)
                ve.wait_ge(g_dve.sem, g_dve.at(b, 1))
                ve.wait_ge(g_act.sem, g_act.at(b, 1))
                ve.tensor_scalar(td[32:48, :], td[32:48, :], 1.0, None, ALU.add).then_inc(g_dve.sem, 1)
                ve.wait_ge(g_dve.sem, g_dve.at(b, 2))
                ve.reciprocal(RT[32:48, :], td[32:48, :]).then_inc(g_dve.sem, 1)
                ve.tensor_scalar(ta[0:16, :], ps[6][0:16, :], w("dtb", p1=16), None, ALU.add).then_inc(g_dve.sem, 1)
                ve.wait_ge(g_dve.sem, g_dve.at(b, 4))
                ve.scalar_tensor_tensor(tna[0:16, :], ta[0:16, :], -1.0, ta[0:16, :], ALU.mult,
                                        ALU.max).then_inc(g_dve.sem, 1)

            def gates_softplus(b):
                ve.wait_ge(g_act.sem, g_act.at(b, 2))
                ve.tensor_scalar(tu[0:16, :], tw[0:16, :], 1.0, None, ALU.add).then_inc(g_dve.sem, 1)
                ve.wait_ge(g_dve.sem, g_dve.at(b, 6))
                ve.scalar_tensor_tensor(tw[0:16, :], tu[0:16, :], -1.0, tw[0:16, :], ALU.add,
                                        ALU.subtract).then_inc(g_dve.sem, 1)
                ve.wait_ge(g_dve.sem, g_dve.at(b, 7))
                ve.wait_ge(g_act.sem, g_act.at(b, 3))
                ve.reciprocal(tu[0:16, :], tu[0:16, :]).then_inc(g_dve.sem, 1)
                ve.wait_ge(g_dve.sem, g_dve.at(b, 8))
                ve.tensor_tensor(tw[0:16, :], tw[0:16, :], tu[0:16, :], ALU.mult).then_inc(g_dve.sem, 1)
                ve.wait_ge(g_dve.sem, g_dve.at(b, 9))
                ve.tensor_tensor(tl[0:16, :], tl[0:16, :], tw[0:16, :], ALU.subtract).then_inc(g_dve.sem, 1)
                ve.wait_ge(g_dve.sem, g_dve.at(b, 10))
                ve.scalar_tensor_tensor(tl[0:16, :], ta[0:16, :], 0.0, tl[0:16, :], ALU.max,
                                        ALU.add).then_inc(g_dve.sem, 1)
                ve.wait_ge(g_dve.sem, g_dve.at(b, 11))
                ve.tensor_scalar(tna[0:16, :], tl[0:16, :], expA[0:16, :], 1e30, ALU.mult,
                                 ALU.min).then_inc(g_dve.sem, 1)

            def gates_decay(b):
                ve.wait_ge(g_act.sem, g_act.at(b, 4))
                ve.tensor_copy(EGm[0:16, :], EG[0:16, :]).then_inc(g_dve.sem, 1)
                ve.memset(D1[0:16, :], 0.0).then_inc(g_dve.sem, 1)
                ve.wait_ge(g_dve.sem, g_dve.at(b, 14))
                ve.tensor_copy(D1[0:16, 0:S:C], EG[0:16, 0:S:C]).then_inc(g_dve.sem, 1)
                ve.memset(EGm[0:16, 0:S:C], 0.0).then_inc(g_dve.sem, 1)
                ve.wait_ge(g_dve.sem, g_dve.at(b, 16))
                ve.tensor_tensor_scan(RT[0:16, :], EGm[0:16, :], D1[0:16, :], 0.0, ALU.mult, ALU.add).then_inc(gamma_ok.sem, 1)
                ve.wait_ge(gamma_ok.sem, gamma_ok.at(b, 1))
                ve.tensor_copy(gl[:, :], RT[0:16, C - 1:S:C]).then_inc(g_dve.sem, 1)

            def conv_pair(b, t):
                for k, j in enumerate((2, 1, 0)):
                    sh = KSZ - 1 - j
                    for t1 in (t, t + 1):
                        if k:
                            ve.wait_ge(taps.sem, taps.at(b, 3 * t + 2 * k + t1 % 2 - 1))
                        else:
                            ve.wait_ge(tap0.sem, tap0.at(b, t1 + 1))
                        ve.scalar_tensor_tensor(ybuf[t1 % 4][:, sh:S], ps[t1 % 4][:, 0:S - sh],
                                                w("convw", KSZ * t1 + j, KSZ * t1 + j + 1), ybuf[t1 % 4][:, sh:S],
                                                ALU.mult, ALU.add).then_inc(taps.sem, 1)

            layer_norm(0, 0)
            gates_split(0)
            gates_softplus(0)
            conv_pair(0, 0)
            gates_decay(0)
            with ve.Fori(0, B) as b:
                def v3(t):
                    return t.rearrange("a (q v) -> a q v", q=8)

                def gamma(c):
                    return tc[:, bass.ds(c, 1), 0, :].rearrange("a c q -> a (c q)").unsqueeze(2).broadcast_to([128, 8, 64])

                def decays(n, par):
                    ve.wait_ge(c_d1.sem, c_d1.at(n, 1))
                    ve.tensor_tensor_scan(Ec[par], EGc, d1, 0.0, ALU.mult, ALU.add).then_inc(e_ok.sem, 1)

                def triangle(n, par):
                    ve.wait_ge(e_ok.sem, e_ok.at(n, 1))
                    ve.wait_ge(kq_mm.sem, kq_mm.at(n, 1))
                    kk = ps[6][:, :].rearrange("a (p q t) -> a p q t", p=4, q=2)[:, :, 0, :]
                    ve.tensor_tensor(Lc.rearrange("a (p r t) -> a p r t", p=4, r=2),
                                     kk.unsqueeze(2).broadcast_to([128, 4, 2, 64]),
                                     Ec[par].rearrange("a (p r t) -> a p r t", p=4, r=2), ALU.mult).then_inc(lc_ok.sem, 1)

                def blocks(n):
                    ve.wait_ge(lc_ok.sem, lc_ok.at(n, 1))
                    ve.tensor_tensor(M8.rearrange("a (q i k) -> a q k i", q=8, i=BASE),
                                     Lc.rearrange("a (q k i) -> a q k i", q=8, i=BASE),
                                     w("blk8").unsqueeze(1).unsqueeze(3).broadcast_to([128, 8, 8, BASE]),
                                     ALU.mult).then_inc(m8_ok.sem, 1)
                    ve.wait_ge(m8_ok.sem, m8_ok.at(n, 1))
                    ve.tensor_reduce(Xd[:, :, :].rearrange("a q i -> a (q i)"), M8.rearrange("a (q k) -> a q k", k=8), AX,
                                     ALU.add).then_inc(m8_ok.sem, 1)
                    ve.wait_ge(m8_ok.sem, m8_ok.at(n, 2))
                    ve.tensor_tensor(rhs8.rearrange("a (q i j) -> a q i j", q=8, i=BASE),
                                     Xd[:, :, :].unsqueeze(3).broadcast_to([128, 8, BASE, BASE]),
                                     w("diag8").rearrange("a (i j) -> a i j", i=BASE).unsqueeze(1).broadcast_to(
                                         [128, 8, BASE, BASE]), ALU.mult).then_inc(m8_ok.sem, 1)

                def substitute(n):
                    ve.wait_ge(a8_ev.sem, a8_ev.at(n, 1))
                    for i in range(1, BASE):
                        if i > 1:
                            ve.wait_ge(x8_ok.sem, x8_ok.at(n, 2 * i - 2))
                        ve.tensor_tensor(prod[:, :, 0:i + 1], An[:, :, i, 0:i + 1], X8[:, :, 0:i + 1],
                                         ALU.mult).then_inc(x8_ok.sem, 1)
                        ve.wait_ge(x8_ok.sem, x8_ok.at(n, 2 * i - 1))
                        ve.tensor_reduce(X8[:, :, i + 1], prod[:, :, 0:i + 1], AX, ALU.add).then_inc(x8_ok.sem, 1)

                def block_inverses(n):
                    ve.wait_ge(x8_ok.sem, x8_ok.at(n, 2 * (BASE - 1)))
                    ve.wait_ge(y_mm.sem, y_mm.at(n - 1, 2))
                    ve.tensor_tensor(Z[:, :, :].rearrange("a q (k i) -> a q k i", i=BASE),
                                     X8[:, :, 1:BASE + 1].unsqueeze(2).broadcast_to([128, 8, 16, BASE]),
                                     w("blk16").unsqueeze(1).unsqueeze(3).broadcast_to([128, 8, 16, BASE]),
                                     ALU.mult).then_inc(z8_ok.sem, 1)

                def within(n, par):
                    ve.wait_ge(bd0.sem, bd0.at(b, 2))
                    for e in range(2):
                        rows = slice(64 * e, 64 * e + 64)
                        src = ps[6][rows, :].rearrange("a (p q t) -> a p q t", p=4, q=2)[:, :, 1, :]
                        ve.tensor_tensor(
                            P[par][rows, :, 64 * e:64 * e + 64].rearrange("a (p r) t -> a p r t", r=2),
                            src.unsqueeze(2).broadcast_to([64, 4, 2, 64]),
                            Ec[par][rows, :].rearrange("a (p r t) -> a p r t", p=4, r=2), ALU.mult).then_inc(p_dve.sem, 1)

                def level(n, k):
                    mask = w("masks", 128 * k, 128 * k + 128).unsqueeze(1).broadcast_to([128, 4, 128])
                    for h in range(2):
                        ve.wait_ge(x_mm.sem, x_mm.at(n, 2 * k + h + 1))
                        ve.tensor_tensor(Wm[:, 4 * h:4 * h + 4, :], ps[4 + h][:, :].rearrange("a (q t) -> a q t", q=4),
                                         mask, ALU.mult).then_inc(w_ev.sem, 1)

                def residual(n, c, par):
                    ve.wait_ge(ks_mm.sem, ks_mm.at(n, 1))
                    ve.tensor_tensor(v3(R), v3(ps[2][:, :]), gamma(c), ALU.mult).then_inc(r_dve.sem, 1)
                    ve.wait_ge(r_dve.sem, r_dve.at(n, 1))
                    ve.wait_ge(kv_ev.sem, kv_ev.at(n, 2))
                    ve.tensor_tensor(R, Vtok[par], R, ALU.subtract).then_inc(r_dve.sem, 1)

                def outer(n, c):
                    ve.wait_ge(qs_mm.sem, qs_mm.at(n, 1))
                    ve.tensor_tensor(v3(Ot), v3(ps[3][:, :]), gamma(c), ALU.mult).then_inc(o_dve.sem, 1)

                def last_decay(n, par):
                    ve.wait_ge(y_ev.sem, y_ev.at(n, 2))
                    ve.tensor_tensor(v3(Yd), v3(Y), v3(Ec[par])[:, :, 63:64].broadcast_to([128, 8, 64]),
                                     ALU.mult).then_inc(yd_ok.sem, 1)

                def new_state(n, c):
                    glast = glB[:, :, bass.ds(c, 1)].broadcast_to([128, 8, 64])
                    ve.tensor_tensor(v3(St), v3(St), glast, ALU.mult).then_inc(s_dve.sem, 1)
                    ve.wait_ge(s_mm.sem, s_mm.at(n, 1))
                    ve.wait_ge(s_dve.sem, s_dve.at(n, 1))
                    ve.tensor_tensor(St, St, ps[2][:, :], ALU.add).then_inc(s_dve.sem, 1)

                def heads(n):
                    ve.wait_ge(o_dve.sem, o_dve.at(n, 1))
                    for h in range(2):
                        ve.wait_ge(o_mm.sem, o_mm.at(n, h + 1))
                        for r in range(2):
                            ov = Ot[:, 256 * h:256 * h + 256].rearrange("a (p r v) -> a p r v", p=2, r=2)[:, :, r, :]
                            src = ps[6 + h][:, :].rearrange("a (p r q) -> a p r q", p=2, r=2)[:, :, r, 64 * r:64 * r + 64]
                            ins = ve.tensor_tensor(ov, ov, src, ALU.add)
                            if r == 1:
                                ins.then_inc(o_dve.sem, 1)

                def gated(n, c, par):
                    ve.wait_ge(o_dve.sem, o_dve.at(n, 3))
                    hc = Hall[:, bass.ds(c, 1), :].rearrange("a c n -> a (c n)")
                    ve.scalar_tensor_tensor(hc, Ot, 0.125, sz[par], ALU.mult, ALU.mult).then_inc(o_dve.sem, 1)

                def variances(n, c):
                    ve.wait_ge(hq_ok.sem, hq_ok.at(n, 1))
                    ve.tensor_reduce(var[:, bass.ds(c, 1), :].rearrange("a c q -> a (c q)"),
                                     hsq[:, :].rearrange("a (q v) -> a q v", q=8), AX, ALU.add).then_inc(var_ok.sem, 1)

                def step(n, c, par, more=True):
                    residual(n, c, par)
                    outer(n, c)
                    within(n + 1, 1 - par)
                    substitute(n + 1)
                    last_decay(n, par)
                    block_inverses(n + 1)
                    heads(n)
                    new_state(n, c)
                    level(n + 1, 0)
                    gated(n, c, par)
                    level(n + 1, 1)
                    if more:
                        decays(n + 2, par)
                    variances(n, c)
                    level(n + 1, 2)
                    if more:
                        triangle(n + 2, par)
                        blocks(n + 2)

                n0 = b * NC
                for t in range(2, NT, 2):
                    conv_pair(b, t)
                    if t == 6:
                        ve.wait_ge(tc_mm.sem, tc_mm.at(b, 1))
                        ve.tensor_copy(tc[:, :, :, :].rearrange("a c q n -> a (c q n)"), ps[7][:, 0:NC * 16]).then_inc(tc_ok.sem, 1)
                        ve.wait_ge(eg_dma.sem, eg_dma.at(b, 48))
                        ve.wait_ge(gl_dma.sem, gl_dma.at(b, 48))
                        ve.memset(St, 0.0).then_inc(s0.sem, 1)
                    if t == 12:
                        decays(n0, 0)
                        triangle(n0, 0)
                        blocks(n0)
                within(n0, 0)
                substitute(n0)
                block_inverses(n0)
                level(n0, 0)
                level(n0, 1)
                decays(n0 + 1, 1)
                level(n0, 2)
                triangle(n0 + 1, 1)
                blocks(n0 + 1)
                with ve.Fori(0, NC // 2 - 1) as c2:
                    for par in range(2):
                        step(n0 + c2 * 2 + par, c2 * 2 + par, par)
                step(n0 + (NC - 2), NC - 2, 0, more=False)
                residual(n0 + (NC - 1), NC - 1, 1)
                outer(n0 + (NC - 1), NC - 1)
                last_decay(n0 + (NC - 1), 1)
                heads(n0 + (NC - 1))
                new_state(n0 + (NC - 1), NC - 1)
                gated(n0 + (NC - 1), NC - 1, 1)
                variances(n0 + (NC - 1), NC - 1)
                ve.wait_ge(n_sd.sem, n_sd.at(b, 1))
                ve.reciprocal(rstd[:, :, :], rstd[:, :, :]).then_inc(n_rs.sem, 1)
                ve.wait_ge(n_rs.sem, n_rs.at(b, 1))
                for c in range(NC):
                    hv = Hall[:, c, :].rearrange("a (q v) -> a q v", q=8)
                    ve.tensor_tensor(hv, hv, rstd[:, c, :].unsqueeze(2).broadcast_to([128, 8, 64]),
                                     ALU.mult).then_inc(hn_ok.sem, 1)
                ve.wait_ge(op_mm.sem, op_mm.at(b, 1))
                ve.wait_ge(y_out.sem, y_out.at(b - 1, 16))
                ve.tensor_tensor(x[:, :], x0[:, :], ps[4][:, :], ALU.add).then_inc(xr.sem, 1)
                layer_norm(b, 1)
                ve.wait_ge(gt_mm.sem, gt_mm.at(b, 1))
                ve.tensor_copy(lg[:, :, 0:E], ps[6][:, 0:64].rearrange("a (t e) -> a t e", t=4)[:, :, 0:E]).then_inc(gt_dve.sem, 1)
                ve.wait_ge(gt_dve.sem, gt_dve.at(b, 1))
                ve.tensor_reduce(mx4, lg[:, :, 0:E], AX, ALU.max).then_inc(gt_dve.sem, 1)
                ve.wait_ge(gt_dve.sem, gt_dve.at(b, 2))
                ve.tensor_tensor(lg[:, :, 0:E], lg[:, :, 0:E], mx4.unsqueeze(2).broadcast_to([128, 4, E]), ALU.subtract).then_inc(gt_dve.sem, 1)
                ve.wait_ge(gt_dve.sem, gt_dve.at(b, 3))
                ve.wait_ge(gt_act.sem, gt_act.at(b, 1))
                ve.tensor_reduce(sm4, lg[:, :, 0:E], AX, ALU.add).then_inc(gt_dve.sem, 1)
                ve.wait_ge(gt_dve.sem, gt_dve.at(b, 4))
                ve.reciprocal(rc4, sm4).then_inc(gt_dve.sem, 1)
                ve.wait_ge(gt_dve.sem, gt_dve.at(b, 5))
                ve.tensor_tensor(scp[:, :, 0:E], lg[:, :, 0:E], rc4.unsqueeze(2).broadcast_to([128, 4, E]), ALU.mult).then_inc(gt_dve.sem, 1)
                ve.wait_ge(gt_dve.sem, gt_dve.at(b, 6))
                ve.tensor_copy(scp[:, :, E:20], w("pads").unsqueeze(1).broadcast_to([128, 4, 5])).then_inc(gt_dve.sem, 1)
                ve.wait_ge(gt_dve.sem, gt_dve.at(b, 7))
                hold(ve)
                for t in range(4):
                    ins = ve.max(m8[:, t, :], scp[:, t, :])
                    if t == 3:
                        ins.then_inc(gt_dve.sem, 1)
                        ve.wait_ge(gt_dve.sem, gt_dve.at(b, 8))
                ve.tensor_copy(tr8[:, :, 0:TOPK], m8[:, :, 0:TOPK]).then_inc(gt_dve.sem, 1)
                ve.wait_ge(gt_dve.sem, gt_dve.at(b, 9))
                ve.tensor_copy(tr8[:, :, TOPK:8], w("pads").unsqueeze(1).broadcast_to([128, 4, 5])).then_inc(gt_dve.sem, 1)
                ve.wait_ge(gt_dve.sem, gt_dve.at(b, 10))
                hold(ve)
                for t in range(4):
                    ins = ve.match_replace(rep[:, t, :], tr8[:, t, :], scp[:, t, :], -9.0)
                    if t == 3:
                        ins.then_inc(gt_dve.sem, 1)
                        ve.wait_ge(gt_dve.sem, gt_dve.at(b, 11))
                ve.tensor_tensor(pk[:, :, 0:E], rep[:, :, 0:E], scp[:, :, 0:E], ALU.not_equal).then_inc(gt_dve.sem, 1)
                ve.wait_ge(gt_dve.sem, gt_dve.at(b, 12))
                ve.tensor_tensor(lg[:, :, 0:E], pk[:, :, 0:E], scp[:, :, 0:E], ALU.mult).then_inc(gt_dve.sem, 1)
                ve.wait_ge(gt_dve.sem, gt_dve.at(b, 13))
                ve.tensor_reduce(sm4, m8[:, :, 0:TOPK], AX, ALU.add).then_inc(gt_dve.sem, 1)
                ve.wait_ge(gt_dve.sem, gt_dve.at(b, 14))
                ve.tensor_scalar(sm4, sm4, 1e-20, None, ALU.add).then_inc(gt_dve.sem, 1)
                ve.wait_ge(gt_dve.sem, gt_dve.at(b, 15))
                ve.reciprocal(rc4, sm4).then_inc(gt_dve.sem, 1)
                ve.wait_ge(gt_dve.sem, gt_dve.at(b, 16))
                ve.tensor_tensor(lg[:, :, 0:E], lg[:, :, 0:E], rc4.unsqueeze(2).broadcast_to([128, 4, E]), ALU.mult).then_inc(gt_dve.sem, 1)
                ve.wait_ge(gt_dve.sem, gt_dve.at(b, 17))

                def hidden(j):
                    ve.wait_ge(f_act.sem, f_act.at(b, j + 1))
                    if j >= 5:
                        ve.wait_ge(f_pool.sem, f_pool.at(b, j - 4))
                    elif j >= 3:
                        ve.wait_ge(f2_mm.sem, f2_mm.at(b, j - 2))
                    bias = w("sfc1b", j, j + 1) if j < 2 else w("fc1b", 2 * (j - 2), 2 * (j - 2) + 1)
                    ve.scalar_tensor_tensor(hid[j % 3], ps[2 * (j % 3)][:, :], bias, glu[j % 3], ALU.add,
                                            ALU.mult).then_inc(f_dve.sem, 1)
                hidden(0)
                hidden(1)
                ve.wait_ge(ct_mm.sem, ct_mm.at(b, 1))
                ve.tensor_copy(combT[0:E, :], ps[6][0:E, :]).then_inc(gt_dve.sem, 1)
                for j in range(2, NE):
                    hidden(j)
                ve.wait_ge(f2_mm.sem, f2_mm.at(b, NE))
                ve.scalar_tensor_tensor(x[:, :], ps[7][:, :], w("sfc2b"), x[:, :], ALU.add, ALU.add).then_inc(xr.sem, 1)
                ve.wait_ge(xr.sem, xr.at(b, 2))
                layer_norm(b, 2)

                def split(sig, k0, src, parts):
                    ve.tensor_copy(parts[0], src).then_inc(sig.sem, 1)
                    ve.wait_ge(sig.sem, sig.at(b, k0 + 1))
                    ve.tensor_tensor(r1, src, parts[0], ALU.subtract).then_inc(sig.sem, 1)
                    ve.wait_ge(sig.sem, sig.at(b, k0 + 2))
                    ve.tensor_copy(parts[1], r1).then_inc(sig.sem, 1)
                    ve.wait_ge(sig.sem, sig.at(b, k0 + 3))
                    ve.tensor_tensor(r1, r1, parts[1], ALU.subtract).then_inc(sig.sem, 1)
                    ve.wait_ge(sig.sem, sig.at(b, k0 + 4))
                    ve.tensor_copy(parts[2], r1).then_inc(sig.sem, 1)
                    ve.wait_ge(sig.sem, sig.at(b, k0 + 5))

                def project(sig_mm, sig, bank, bias, k0, dst, parts, scale):
                    ve.tensor_scalar(dst, ps[bank][:, :], bias, scale, ALU.add, ALU.mult).then_inc(sig.sem, 1)
                    ve.wait_ge(sig.sem, sig.at(b, k0 + 1))
                    split(sig, k0 + 1, dst, parts)

                scale = float(np.float32(1.0 / np.sqrt(128)))
                ve.wait_ge(a_mm.sem, a_mm.at(b, 2))
                project(a_mm, a_dve, 2, w("bq"), 0, qs, qsp, -scale)
                project(a_mm, a_dve, 3, w("bk"), 6, ks, ksp, scale)
                hold(ve)

                def least(n, k):
                    ve.wait_ge(a_s.sem, a_s.at(n, k + 1))
                    ve.wait_ge(a_e.sem, a_e.at(n, k - 3))
                    ve.tensor_reduce(mcol[:, k % 4:k % 4 + 1], ps[k % 4][:, :], AX, ALU.min).then_inc(a_m.sem, 1)

                def weights(n, e2, k):
                    j = k % 4
                    ve.wait_ge(a_e.sem, a_e.at(n, k + 1))
                    ve.reciprocal(zrec[:, j:j + 1], zcol[:, j:j + 1]).then_inc(a_z.sem, 1)
                    ve.wait_ge(a_z.sem, a_z.at(n, k + 1))
                    ve.wait_ge(a_r.sem, a_r.at(n, k - 3))
                    ve.tensor_scalar(ZP[:, j, :], w("onehot")[:, bass.ds(e2 * 32 + 16 * (k // 4), 16)],
                                     zrec[:, j:j + 1], None, ALU.mult).then_inc(a_zp.sem, 1)

                n1 = b * (H1 // 2)
                least(n1, 0)
                least(n1, 1)
                with ve.Fori(0, H1 // 2 - 1) as e2:
                    for k in range(8):
                        least(n1 + e2, k + 2)
                        weights(n1 + e2, e2, k)
                for k in range(8):
                    if k < 6:
                        least(n1 + (H1 // 2 - 1), k + 2)
                    weights(n1 + (H1 // 2 - 1), H1 // 2 - 1, k)
                ve.wait_ge(a_sum.sem, a_sum.at(b, 1))
                ve.tensor_copy(rs[0:16, :], ps[4][0:16, :]).then_inc(a_rs.sem, 1)
                ve.wait_ge(a_rd.sem, a_rd.at(b, 32))
                ve.tensor_tensor(att, vT, Rb, ALU.mult).then_inc(a_at.sem, 1)
                ve.wait_ge(a_wo.sem, a_wo.at(b, 1))
                ve.scalar_tensor_tensor(x[:, :], ps[5][:, :], w("bo"), x[:, :], ALU.add, ALU.add).then_inc(xr.sem, 1)
                ve.wait_ge(xr.sem, xr.at(b, 3))
                layer_norm(b, 3)
                ve.wait_ge(ln_dve.sem, ln_dve.at(b, 12))
                ve.tensor_scalar(xn[:, :], xn[:, :], w("nw"), w("nb"), ALU.mult, ALU.add).then_inc(b_xn.sem, 1)
                ve.tensor_tensor(u[:, :], xc[:, :], ps[0][:, :], ALU.mult).then_inc(b_xn.sem, 1)
                ve.wait_ge(b_xn.sem, b_xn.at(b, 2))
                ve.tensor_tensor(x[:, :], x[:, :], u[:, :], ALU.add).then_inc(fin.sem, 1)
                scale = float(D) ** -0.5
                ve.wait_ge(b_mm.sem, b_mm.at(b, 2))
                project(b_mm, b_dve, 2, w("qb"), 0, qs, qsp, -scale)
                project(b_mm, b_dve, 3, w("kb"), 6, ks, ksp, 1.0)
                ve.wait_ge(b_mm.sem, b_mm.at(b, 3))
                ve.wait_ge(b_pool.sem, b_pool.at(b, 2))
                for k in range(4):
                    for g2 in range(2):
                        base = 1024 * k + 512 * g2
                        ins = ve.tensor_tensor(
                            vslots(base),
                            ps[4][:, 128 * k + 64 * g2:128 * k + 64 * g2 + 64].rearrange("a (h y) -> a h y", h=4),
                            w("vb", 64 * g2, 64 * g2 + 64).rearrange("a (h y) -> a h y", h=4), ALU.add)
                    ins.then_inc(b_v.sem, 1)
                for i in range(32):
                    ve.wait_ge(b_s.sem, b_s.at(b, i + 1))
                    ve.tensor_reduce(mq[:, i:i + 1], ps[2 + i % 2][:, :], AX, ALU.min).then_inc(b_m.sem, 1)

                def heads_out(g2):
                    ve.wait_ge(b_pv.sem, b_pv.at(b, 16 * g2 + 16))
                    ve.reciprocal(recips[g2][0:64, :], ps[4 + g2][64:128, :]).then_inc(b_rc.sem, 1)
                    ve.wait_ge(b_rc.sem, b_rc.at(b, g2 + 1))
                    ve.tensor_tensor(att[64 * g2:64 * g2 + 64, :], ps[4 + g2][0:64, :], recips[g2][0:64, :],
                                     ALU.mult).then_inc(b_at.sem, 1)

                layer_norm(b + 1, 0)
                heads_out(0)
                gates_split(b + 1)
                gates_softplus(b + 1)
                heads_out(1)
                conv_pair(b + 1, 0)
                ve.wait_ge(b_wo.sem, b_wo.at(b, 1))
                ve.wait_ge(fin.sem, fin.at(b, 1))
                ve.tensor_tensor(x[:, :], x[:, :], ps[4][:, :], ALU.add).then_inc(fin.sem, 1)
                ve.wait_ge(fin.sem, fin.at(b, 2))
                xe = x[:, :].rearrange("a (e t) -> a e t", e=NX)
                ve.tensor_tensor(xe, xe, obm[:, :].unsqueeze(2).broadcast_to([128, NX, 128]), ALU.add).then_inc(fin.sem, 1)
                gates_decay(b + 1)

        @block.gpsimd
        def _(po):
            po.wait_ge(pack_in.sem, 32)
            with po.Fori(0, B) as b:
                po.wait_ge(fin.sem, fin.at(b - 1, 3))
                hold(po)
                po.memset(P[0], 0.0).then_inc(bd0.sem, 1)
                po.memset(P[1], 0.0).then_inc(bd0.sem, 1)
                half = w("half").unsqueeze(1).unsqueeze(3)

                def copies(n, c, par):
                    tok = bass.ds(c * C, C)
                    po.wait_ge(eg_dma.sem, eg_dma.at(b, 48))
                    po.wait_ge(tc_ok.sem, tc_ok.at(b, 1))
                    po.wait_ge(e_ok.sem, e_ok.at(n - 1, 1))
                    hold(po)
                    po.tensor_copy(EGc.rearrange("a (q t) -> a q t", q=8), egB[:, :, tok]).then_inc(eg_cp.sem, 1)
                    po.tensor_tensor(d1.rearrange("a (q t) -> a q t", q=8),
                                     w("identc").unsqueeze(1).broadcast_to([128, 8, C]),
                                     tc[:, bass.ds(c, 1), 1, :].rearrange("a c q -> a (c q)").unsqueeze(2).broadcast_to([128, 8, C]),
                                     ALU.mult).then_inc(c_d1.sem, 1)
                    po.wait_ge(conv.sem, conv.at(b, 8))
                    po.wait_ge(qs_mm.sem, qs_mm.at(n - 2, 1))
                    po.wait_ge(kq_mm.sem, kq_mm.at(n - 1, 1))
                    hold(po)
                    for dst, src in ((Kbd[par], KT), (Qbd[par], QT)):
                        po.tensor_tensor(dst.rearrange("a p (e t) -> a p e t", e=2),
                                         src[:, :, tok].unsqueeze(2).broadcast_to([128, 4, 2, C]),
                                         half.broadcast_to([128, 4, 2, C]), ALU.mult).then_inc(c_cp.sem, 1)
                    po.tensor_copy(KQc[:, :, 0, :], KT[:, :, tok]).then_inc(c_cp.sem, 1)
                    po.tensor_copy(KQc[:, :, 1, :], QT[:, :, tok]).then_inc(c_cp.sem, 1)
                    po.wait_ge(conv.sem, conv.at(b, NT))
                    po.wait_ge(z_mm.sem, z_mm.at(n - 1, 1))
                    po.wait_ge(vt_mm.sem, vt_mm.at(n - 1, 1))
                    hold(po)
                    for h in range(2):
                        po.tensor_copy(Vc[:, 4 * h:4 * h + 4, :], VT[:, 4 * h:4 * h + 4, tok]).then_inc(c_cp.sem, 1)
                    po.tensor_copy(xch[:, :], xn[:, tok]).then_inc(c_cp.sem, 1)

                def triangle(n):
                    po.wait_ge(lc_ok.sem, lc_ok.at(n, 1))
                    po.wait_ge(x_mm.sem, x_mm.at(n - 1, 6))
                    hold(po)
                    po.tensor_tensor(LT[:, :, :].rearrange("a q (e t) -> a q e t", e=2),
                                     Lc.rearrange("a (q t) -> a q t", q=8).unsqueeze(2).broadcast_to([128, 8, 2, C]),
                                     half.broadcast_to([128, 8, 2, C]), ALU.mult).then_inc(lt_ok.sem, 1)
                    po.wait_ge(lt_ok.sem, lt_ok.at(n, 1))
                    hold(po)
                    po.affine_select(out=LT, in_=LT, compare_op=ALU.not_equal, fill=1.0, base=0,
                                     pattern=[[0, 8], [-1, 128]], channel_multiplier=1).then_inc(lt_ok.sem, 1)

                n0 = b * NC
                copies(n0, 0, 0)
                triangle(n0)
                copies(n0 + 1, 1, 1)
                with po.Fori(0, NC // 2 - 1) as c2:
                    for par in range(2):
                        triangle(n0 + c2 * 2 + (par + 1))
                        copies(n0 + c2 * 2 + (par + 2), c2 * 2 + (par + 2), par)
                triangle(n0 + (NC - 1))
                po.wait_ge(gt_dve.sem, gt_dve.at(b, 18))
                for j in range(2, NE):
                    po.wait_ge(f_dve.sem, f_dve.at(b, j + 1))
                    third = cb_in[(j - 2) // 5]
                    po.wait_ge(third.sem, third.at(b, 16))
                    if j >= 5:
                        po.wait_ge(f2_mm.sem, f2_mm.at(b, j - 2))
                    po.tensor_tensor(act[j % 3], hid[j % 3], combB[:, j - 2, :], ALU.mult).then_inc(f_pool.sem, 1)
                po.wait_ge(f2_mm.sem, f2_mm.at(b, NE))
                hold(po)
                po.memset(zero[:, 0:16], 0.0).then_inc(zero_ok.sem, 1)
                po.wait_ge(zero_ok.sem, zero_ok.at(b, 1))
                hold(po)
                with po.Fori(0, H1 // 2) as e2:
                    n = b * (H1 // 2) + e2
                    for i in range(2):
                        po.wait_ge(a_dma.sem, a_dma.at(b, 12 * 16))
                        po.wait_ge(a_s.sem, a_s.at(n, 4 * i - 4))
                        hold(po)
                        po.tensor_copy(QXe[i][0:48, :].rearrange("a (g t) -> a g t", g=16),
                                       QX[0:48, :, bass.ds(e2 * 64 + 32 * i, 32)]).then_inc(a_kx.sem, 1)
                        po.tensor_copy(KXe[i][0:48, :].rearrange("a (g t) -> a g t", g=16),
                                       KX[0:48, :, bass.ds(e2 * 64 + 32 * i, 32)]).then_inc(a_kx.sem, 1)
                po.wait_ge(xr.sem, xr.at(b, 3))
                hold(po)
                po.memset(Vflat, 0.0).then_inc(b_pool.sem, 1)
                po.wait_ge(b_pool.sem, b_pool.at(b, 1))
                hold(po)
                for g2 in range(8):
                    ins = po.memset(vslots(512 * g2 + 64), 1.0)
                ins.then_inc(b_pool.sem, 1)
                po.wait_ge(b_pool.sem, b_pool.at(b, 2))
                hold(po)
                po.memset(KH[96:97, :, :], 1.0).then_inc(b_pool.sem, 1)
                po.wait_ge(b_pool.sem, b_pool.at(b, 3))
                hold(po)


def _head_order():
    return [(2 * p + e) * 2 + r for e in range(2) for p in range(4) for r in range(2)]


def pack_inputs(i):
    f = np.float32

    def col(v):
        v = np.asarray(v).reshape(-1)
        return np.concatenate([v, np.zeros(128 - v.size, f)])[:, None]

    def cols(m):
        return np.ascontiguousarray(np.asarray(m).T)

    order = _head_order()
    parts = {}
    parts["wqkv"] = cols(i["L0_attn_W_qkv"])
    parts["convw"] = np.asarray(i["L0_attn_conv_w"]).reshape(NT, 128, KSZ).transpose(1, 0, 2).reshape(128, NT * KSZ)
    parts["wz"] = cols(i["L0_attn_W_z"]).reshape(128, 4, 2, 128).transpose(0, 2, 1, 3).reshape(128, 1024)
    parts["wab"] = np.concatenate([cols(i["L0_attn_W_a"])[:, order], np.zeros((128, 16), f),
                                   cols(i["L0_attn_W_b"])[:, order]], 1)
    parts["dtb"], parts["alog"] = col(np.asarray(i["L0_attn_dt_bias"])[order]), col(np.asarray(i["L0_attn_A_log"])[order])
    parts["normw"] = col(np.tile(np.asarray(i["L0_attn_norm_weight"]), 2))
    parts["wout"] = cols(i["L0_attn_W_out"]).reshape(8, 128, 128).transpose(1, 0, 2).reshape(128, 1024)
    parts["gate"] = cols(i["L0_ffn_gate_w"])
    parts["fc1"] = np.asarray(i["L0_ffn_fc1_w"]).transpose(2, 0, 1).reshape(128, E * 256)
    parts["fc1b"] = np.asarray(i["L0_ffn_fc1_b"]).reshape(E * 2, 128).T
    parts["gm"] = cols(i["L0_ffn_geglu_mult"])
    parts["fc2"] = np.asarray(i["L0_ffn_fc2_w"]).transpose(2, 0, 1).reshape(128, E * 128)
    parts["fc2b"] = np.concatenate([np.asarray(i["L0_ffn_fc2_b"]), np.zeros((128 - E, 128), f)], 0)
    parts["sfc1"] = cols(i["L0_ffn_s_fc1_w"])
    parts["sfc1b"] = np.asarray(i["L0_ffn_s_fc1_b"]).reshape(4, 128).T
    parts["sgm"] = np.asarray(i["L0_ffn_s_geglu_mult"]).reshape(2, 128).T
    parts["sfc2"] = cols(i["L0_ffn_s_fc2_w"]).reshape(2, 128, 128).transpose(1, 0, 2).reshape(128, 256)
    parts["sfc2b"] = col(i["L0_ffn_s_fc2_b"])
    for k in "qkvo":
        parts["w" + k], parts["b" + k] = np.asarray(i["L1_attn_W" + k]), col(i["L1_attn_b" + k])
        parts[k + "w"] = cols(i[f"L1_ffn_{k}_w"])
    for k in "qko":
        parts[k + "b"] = col(i[f"L1_ffn_{k}_b"])
    parts["vb"] = np.broadcast_to(np.asarray(i["L1_ffn_v_b"]), (128, 128))
    parts["nw"], parts["nb"] = col(i["L1_ffn_norm_w"]), col(i["L1_ffn_norm_b"])
    eye = np.eye(128, dtype=f)
    parts["ident"], parts["mean"] = eye, np.full((128, 128), 1.0 / 128, f)
    r, c = np.arange(128)[:, None], np.arange(128)[None, :]

    def doubling(s):
        low = (r // (2 * s) == c // (2 * s)) & (r // s == c // s + 1)
        return (eye - low).astype(f)

    parts["masks"] = np.concatenate([doubling(s) for s in LEVELS], 1)
    parts["same8"] = (r // BASE == c // BASE).astype(f)
    parts["blk8"] = (r % C // BASE == np.arange(8)[None, :]).astype(f)
    parts["blk16"] = (r // BASE == np.arange(16)[None, :]).astype(f)
    parts["diag8"] = -(r % BASE == np.tile(np.arange(BASE), BASE)[None, :]).astype(f)
    parts["delta8"] = (r % BASE == np.arange(BASE)[None, :]).astype(f)
    parts["identc"] = np.concatenate([np.eye(C, dtype=f)] * 2, 0)
    parts["half"] = (r // 64 == np.arange(2)[None, :]).astype(f)
    sel = np.zeros((128, 32), f)
    for e in range(2):
        for q in range(8):
            sel[8 * e + q, 16 * e + q] = 1
            sel[32 + 8 * e + q, 16 * e + 8 + q] = 1
    parts["sel"] = sel
    parts["onehot"] = np.broadcast_to(np.eye(16, dtype=f).reshape(1, 256), (128, 256))
    parts["lneps2"] = np.full((128, 1), LN_EPS ** 2, f)
    parts["lneps"], parts["rmseps"] = np.full((128, 1), LN_EPS, f), np.full((128, 1), RMS_EPS, f)
    parts["pads"] = np.broadcast_to(np.array([-1, -2, -3, -4, -5], f), (128, 5))
    at, n = columns()
    for name, (o, width) in at.items():
        assert parts[name].shape == (128, width), (name, parts[name].shape, width)
    return np.ascontiguousarray(np.concatenate([parts[name] for name in at], 1))


def kernel(**inputs):
    import concourse.bacc as bacc
    from concourse.bass_utils import run_bass_kernel_spmd

    nc = bacc.Bacc("TRN2", target_bir_lowering=False, num_devices=1)
    arrays = {
        "x_channels": np.ascontiguousarray(np.asarray(inputs["L0_attn_hidden_states"]).transpose(0, 2, 1)),
        "weights": pack_inputs(inputs),
    }
    args = [nc.dram_tensor(k, a.shape, F32, kind="ExternalInput").ap() for k, a in arrays.items()]
    args.append(nc.dram_tensor("y_channels", (B, D, S), F32, kind="ExternalOutput").ap())
    build(nc, *args)
    r = run_bass_kernel_spmd(nc, [arrays], core_ids=[0])
    return np.ascontiguousarray(r.results[0]["y_channels"].transpose(0, 2, 1))
```
